# Optimizing a Trainium2 kernel written in Bass

```python
import numpy as np
import jax
import jax.numpy as jnp

def _softmax(x, axis=-1):
    return jax.nn.softmax(x, axis=axis)

def _gelu(x):
    return jax.nn.gelu(x, approximate=True)

def _silu(x):
    return jax.nn.silu(x)

def _sigmoid(x):
    return jax.nn.sigmoid(x)

def _layernorm(x, axis=-1, eps=1e-05):
    m = jnp.mean(x, axis=axis, keepdims=True)
    v = jnp.var(x, axis=axis, keepdims=True)
    return (x - m) / jnp.sqrt(v + eps)

def _scatter_add(tgt, idx, src, axis=0):
    return tgt.at[idx].add(src)

def _segment_sum(src, seg, n):
    return jax.ops.segment_sum(src, seg, n)
kernel_name = 'mk_decoder_postln_d2_seqx_r4_0cd960'

def setup_inputs(seed: int=0):
    np.random.seed(seed)
    _w = jnp.asarray

    def _rec_inputs():
        import jax
        import jax.numpy as jnp
        _rk = jax.random.key(seed)
        x = -0.0002928 + 1 * jax.random.normal(jax.random.fold_in(_rk, 1), (8, 256, 512), jnp.float32)
        _lenS = 256 - jax.random.randint(jax.random.fold_in(_rk, 7), (8,), 0, max(1, 256 // 4) + 1, jnp.int32)
        _lenS2 = 256 - jax.random.randint(jax.random.fold_in(_rk, 8), (8,), 0, max(1, 256 // 4) + 1, jnp.int32)
        _ctx_2048P = jax.random.normal(jax.random.fold_in(_rk, 11), (8, 16, 512), jnp.float32)
        _ctx_2048c = jax.random.dirichlet(jax.random.fold_in(_rk, 511), 0.3 * jnp.ones((16,), jnp.float32), (8, 256))
        _ctx_2048t = jnp.einsum('bsk,bkd->bsd', _ctx_2048c, _ctx_2048P)
        _ctx_2048t = _ctx_2048t * jax.lax.rsqrt(jnp.mean(jnp.square(_ctx_2048t)) + 1e-12) * 0.953939
        ctx_2048 = -1.39393e-06 + 0.999914 * (_ctx_2048t + 0.3 * jax.random.normal(jax.random.fold_in(_rk, 611), (8, 256, 512), jnp.float32))
        _validS = jnp.arange(256)[None, :] < _lenS[:, None]
        _validS2 = jnp.arange(256)[None, :] < _lenS2[:, None]
        _causal = jnp.tril(jnp.ones((256, 256), dtype=bool))
        mask_Bx1x2048_fk1 = jnp.where(jnp.ones((8, 1, 512), dtype=bool), 1.0, 0.0).astype(jnp.float32)
        return (x, ctx_2048, mask_Bx1x2048_fk1)
    x, ctx_2048, mask_Bx1x2048_fk1 = _rec_inputs()

    def _L0_attn_setup():
        import jax, jax.numpy as jnp
        import numpy as np
        import math
        D_MODEL = 512
        NUM_HEADS = 16
        MAX_SEQ_LEN = 512
        BATCH = 2
        key = jax.random.key(seed)
        k1, k2, k3, k4, k5 = jax.random.split(key, 5)
        s = 1.0 / math.sqrt(D_MODEL)
        return {'x': jax.random.normal(k1, (BATCH, MAX_SEQ_LEN, D_MODEL), dtype=jnp.float32), 'q_out': jax.random.normal(k2, (D_MODEL, D_MODEL), dtype=jnp.float32) * s, 'k_out': jax.random.normal(k3, (D_MODEL, D_MODEL), dtype=jnp.float32) * s, 'v_out': jax.random.normal(k4, (D_MODEL, D_MODEL), dtype=jnp.float32) * s, 'w_out': jax.random.normal(k5, (MAX_SEQ_LEN, MAX_SEQ_LEN), dtype=jnp.float32) * s}
    _L0_attn_all = _L0_attn_setup()
    _L0_attn_in = {k: v for k, v in _L0_attn_all.items() if k in ('q_out', 'k_out', 'v_out', 'w_out')}
    del _L0_attn_all

    def _L0_xattn_setup():
        import math
        import jax, jax.numpy as jnp
        import numpy as np
        SIZE = 256
        HEADS = 16
        HEAD_DIM = SIZE // HEADS
        B, T, S = (2, 512, 512)
        NEG = 1000000.0
        key = jax.random.key(seed)
        ks = jax.random.split(key, 10)
        target = jax.random.normal(ks[0], (B, SIZE, T), dtype=jnp.float32)
        source = jax.random.normal(ks[1], (B, SIZE, S), dtype=jnp.float32)
        target_mask = (jax.random.uniform(ks[2], (B, 1, T)) > 0.1).astype(jnp.float32)
        source_mask = (jax.random.uniform(ks[3], (B, 1, S)) > 0.1).astype(jnp.float32)
        scale = 1.0 / math.sqrt(SIZE)
        Wq = jax.random.normal(ks[4], (SIZE, SIZE), dtype=jnp.float32) * scale
        Wk = jax.random.normal(ks[5], (SIZE, SIZE), dtype=jnp.float32) * scale
        Wv = jax.random.normal(ks[6], (SIZE, SIZE), dtype=jnp.float32) * scale
        bq = jax.random.normal(ks[7], (SIZE,), dtype=jnp.float32) * 0.01
        bk = jax.random.normal(ks[8], (SIZE,), dtype=jnp.float32) * 0.01
        bv = jax.random.normal(ks[9], (SIZE,), dtype=jnp.float32) * 0.01
        return {'target': target, 'source': source, 'target_mask': target_mask, 'source_mask': source_mask, 'Wq': Wq, 'bq': bq, 'Wk': Wk, 'bk': bk, 'Wv': Wv, 'bv': bv}
    _L0_xattn_all = _L0_xattn_setup()
    _L0_xattn_in = {k: v for k, v in _L0_xattn_all.items() if k in ('Wq', 'bq', 'Wk', 'bk', 'Wv', 'bv')}
    del _L0_xattn_all

    def _L0_ffn_setup():
        import jax, jax.numpy as jnp
        import numpy as np
        B, L, D = (2, 256, 512)
        E, TOP_K, RANK, DFF = (8, 2, 8, 1376)

        def _lora(x, A, Bm, scale):
            return x @ A @ Bm * scale

        def _expert_lora(x, A, Bm, w, scale):
            xA = jnp.einsum('bld,edr->bler', x, A)
            xAB = jnp.einsum('bler,erd->bled', xA, Bm) * scale
            return (xAB * w).sum(axis=2)
        key = jax.random.key(seed)
        ks = jax.random.split(key, 18)
        r = lambda k, s, sc: jax.random.normal(k, s, dtype=jnp.float32) * sc
        inv_d = 1.0 / np.sqrt(D)
        inv_f = 1.0 / np.sqrt(DFF)
        return {'x': r(ks[0], (B, L, D), 1.0), 'W_router': r(ks[1], (D, E), inv_d), 'W_gate': r(ks[2], (D, DFF), inv_d), 'W_up': r(ks[3], (D, DFF), inv_d), 'W_down': r(ks[4], (DFF, D), inv_f), 'sA_gate': r(ks[5], (D, RANK), inv_d), 'sB_gate': r(ks[6], (RANK, DFF), 0.02), 'sA_up': r(ks[7], (D, RANK), inv_d), 'sB_up': r(ks[8], (RANK, DFF), 0.02), 'sA_down': r(ks[9], (DFF, RANK), inv_f), 'sB_down': r(ks[10], (RANK, D), 0.02), 'A_gate': r(ks[11], (E, D, RANK), inv_d), 'B_gate': r(ks[12], (E, RANK, DFF), 0.02), 'A_up': r(ks[13], (E, D, RANK), inv_d), 'B_up': r(ks[14], (E, RANK, DFF), 0.02), 'A_down': r(ks[15], (E, DFF, RANK), inv_f), 'B_down': r(ks[16], (E, RANK, D), 0.02), 'expert_bias': jnp.zeros((E,), dtype=jnp.float32)}
    _L0_ffn_all = _L0_ffn_setup()
    _L0_ffn_in = {k: v for k, v in _L0_ffn_all.items() if k in ('W_router', 'W_gate', 'W_up', 'W_down', 'sA_gate', 'sB_gate', 'sA_up', 'sB_up', 'sA_down', 'sB_down', 'A_gate', 'B_gate', 'A_up', 'B_up', 'A_down', 'B_down', 'expert_bias')}
    del _L0_ffn_all

    def _L1_attn_setup():
        import jax, jax.numpy as jnp
        import numpy as np
        import math
        D_MODEL = 512
        N_HEADS = 16
        Q_PROJ = D_MODEL // 4
        KV_PROJ = D_MODEL // 4
        DH = D_MODEL // N_HEADS
        LN_EPS = 1e-05

        def _layernorm(x, gamma, beta):
            mu = jnp.mean(x, axis=-1, keepdims=True)
            var = jnp.var(x, axis=-1, keepdims=True)
            return (x - mu) * jax.lax.rsqrt(var + LN_EPS) * gamma + beta
        key = jax.random.key(seed)
        ks = jax.random.split(key, 7)
        B, S = (2, 512)
        x = jax.random.normal(ks[0], (B, S, D_MODEL), dtype=jnp.float32)
        W_dq = 0.01 * jax.random.normal(ks[1], (D_MODEL, Q_PROJ), dtype=jnp.float32)
        W_uq = 0.01 * jax.random.normal(ks[2], (Q_PROJ, D_MODEL), dtype=jnp.float32)
        W_dkv = 0.01 * jax.random.normal(ks[3], (D_MODEL, KV_PROJ), dtype=jnp.float32)
        W_ukv = 0.01 * jax.random.normal(ks[4], (KV_PROJ, 2 * D_MODEL), dtype=jnp.float32)
        W_o = 0.01 * jax.random.normal(ks[5], (D_MODEL, D_MODEL), dtype=jnp.float32)
        q_ln_g = jnp.ones((Q_PROJ,), jnp.float32)
        q_ln_b = jnp.zeros((Q_PROJ,), jnp.float32)
        kv_ln_g = jnp.ones((KV_PROJ,), jnp.float32)
        kv_ln_b = jnp.zeros((KV_PROJ,), jnp.float32)
        return {'x': x, 'W_dq': W_dq, 'W_uq': W_uq, 'q_ln_g': q_ln_g, 'q_ln_b': q_ln_b, 'W_dkv': W_dkv, 'W_ukv': W_ukv, 'kv_ln_g': kv_ln_g, 'kv_ln_b': kv_ln_b, 'W_o': W_o}
    _L1_attn_all = _L1_attn_setup()
    _L1_attn_in = {k: v for k, v in _L1_attn_all.items() if k in ('W_dq', 'W_uq', 'q_ln_g', 'q_ln_b', 'W_dkv', 'W_ukv', 'kv_ln_g', 'kv_ln_b', 'W_o')}
    del _L1_attn_all

    def _L1_xattn_setup():
        import jax, jax.numpy as jnp
        import numpy as np
        HIDDEN = 512
        N_HEADS = 16
        N_KV_HEADS = 4
        HEAD_DIM = 128
        EPS = 1e-06

        def rms_norm(x, w, eps=EPS):
            xf = x.astype(jnp.float32)
            var = jnp.mean(xf * xf, axis=-1, keepdims=True)
            return w * (xf * jax.lax.rsqrt(var + eps)).astype(x.dtype)
        key = jax.random.key(seed)
        ks = jax.random.split(key, 8)
        B, S, S_ENC = (4, 512, 256)
        inner = N_HEADS * HEAD_DIM
        kv_dim = N_KV_HEADS * HEAD_DIM
        s = 0.02
        return {'hidden_states': jax.random.normal(ks[0], (B, S, HIDDEN), jnp.float32), 'encoder_hidden_states': jax.random.normal(ks[1], (B, S_ENC, HIDDEN), jnp.float32), 'Wq': jax.random.normal(ks[2], (HIDDEN, inner), jnp.float32) * s, 'Wk': jax.random.normal(ks[3], (HIDDEN, kv_dim), jnp.float32) * s, 'Wv': jax.random.normal(ks[4], (HIDDEN, kv_dim), jnp.float32) * s, 'Wo': jax.random.normal(ks[5], (inner, HIDDEN), jnp.float32) * s, 'q_norm_w': jnp.ones((HEAD_DIM,), jnp.float32), 'k_norm_w': jnp.ones((HEAD_DIM,), jnp.float32)}
    _L1_xattn_all = _L1_xattn_setup()
    _L1_xattn_in = {k: v for k, v in _L1_xattn_all.items() if k in ('Wq', 'Wk', 'Wv', 'Wo', 'q_norm_w', 'k_norm_w')}
    del _L1_xattn_all

    def _L1_ffn_setup():
        import jax, jax.numpy as jnp
        import numpy as np
        SEQ, BS, D, F, E = (256, 2, 512, 512, 8)
        key = jax.random.key(seed)
        ks = jax.random.split(key, 8)
        s = 0.02
        return {'hidden_states': jax.random.normal(ks[0], (SEQ, BS, D), jnp.float32), 'router_w': jax.random.normal(ks[1], (D, E), jnp.float32) * s, 'gate_w': jax.random.normal(ks[2], (E, D, F), jnp.float32) * s, 'up_w': jax.random.normal(ks[3], (E, D, F), jnp.float32) * s, 'down_w': jax.random.normal(ks[4], (E, F, D), jnp.float32) * s, 'shared_gate_w': jax.random.normal(ks[5], (D, F), jnp.float32) * s, 'shared_up_w': jax.random.normal(ks[6], (D, F), jnp.float32) * s, 'shared_down_w': jax.random.normal(ks[7], (F, D), jnp.float32) * s}
    _L1_ffn_all = _L1_ffn_setup()
    _L1_ffn_in = {k: v for k, v in _L1_ffn_all.items() if k in ('router_w', 'gate_w', 'up_w', 'down_w', 'shared_gate_w', 'shared_up_w', 'shared_down_w')}
    del _L1_ffn_all
    return {'x': x, 'ctx_2048': ctx_2048, 'mask_Bx1x2048_fk1': mask_Bx1x2048_fk1, 'L0_attn_q_out': _L0_attn_in['q_out'], 'L0_attn_k_out': _L0_attn_in['k_out'], 'L0_attn_v_out': _L0_attn_in['v_out'], 'L0_attn_w_out': _L0_attn_in['w_out'], 'L0_xattn_Wq': _L0_xattn_in['Wq'], 'L0_xattn_bq': _L0_xattn_in['bq'], 'L0_xattn_Wk': _L0_xattn_in['Wk'], 'L0_xattn_bk': _L0_xattn_in['bk'], 'L0_xattn_Wv': _L0_xattn_in['Wv'], 'L0_xattn_bv': _L0_xattn_in['bv'], 'L0_ffn_W_router': _L0_ffn_in['W_router'], 'L0_ffn_W_gate': _L0_ffn_in['W_gate'], 'L0_ffn_W_up': _L0_ffn_in['W_up'], 'L0_ffn_W_down': _L0_ffn_in['W_down'], 'L0_ffn_sA_gate': _L0_ffn_in['sA_gate'], 'L0_ffn_sB_gate': _L0_ffn_in['sB_gate'], 'L0_ffn_sA_up': _L0_ffn_in['sA_up'], 'L0_ffn_sB_up': _L0_ffn_in['sB_up'], 'L0_ffn_sA_down': _L0_ffn_in['sA_down'], 'L0_ffn_sB_down': _L0_ffn_in['sB_down'], 'L0_ffn_A_gate': _L0_ffn_in['A_gate'], 'L0_ffn_B_gate': _L0_ffn_in['B_gate'], 'L0_ffn_A_up': _L0_ffn_in['A_up'], 'L0_ffn_B_up': _L0_ffn_in['B_up'], 'L0_ffn_A_down': _L0_ffn_in['A_down'], 'L0_ffn_B_down': _L0_ffn_in['B_down'], 'L0_ffn_expert_bias': _L0_ffn_in['expert_bias'], 'L1_attn_W_dq': _L1_attn_in['W_dq'], 'L1_attn_W_uq': _L1_attn_in['W_uq'], 'L1_attn_q_ln_g': _L1_attn_in['q_ln_g'], 'L1_attn_q_ln_b': _L1_attn_in['q_ln_b'], 'L1_attn_W_dkv': _L1_attn_in['W_dkv'], 'L1_attn_W_ukv': _L1_attn_in['W_ukv'], 'L1_attn_kv_ln_g': _L1_attn_in['kv_ln_g'], 'L1_attn_kv_ln_b': _L1_attn_in['kv_ln_b'], 'L1_attn_W_o': _L1_attn_in['W_o'], 'L1_xattn_Wq': _L1_xattn_in['Wq'], 'L1_xattn_Wk': _L1_xattn_in['Wk'], 'L1_xattn_Wv': _L1_xattn_in['Wv'], 'L1_xattn_Wo': _L1_xattn_in['Wo'], 'L1_xattn_q_norm_w': _L1_xattn_in['q_norm_w'], 'L1_xattn_k_norm_w': _L1_xattn_in['k_norm_w'], 'L1_ffn_router_w': _L1_ffn_in['router_w'], 'L1_ffn_gate_w': _L1_ffn_in['gate_w'], 'L1_ffn_up_w': _L1_ffn_in['up_w'], 'L1_ffn_down_w': _L1_ffn_in['down_w'], 'L1_ffn_shared_gate_w': _L1_ffn_in['shared_gate_w'], 'L1_ffn_shared_up_w': _L1_ffn_in['shared_up_w'], 'L1_ffn_shared_down_w': _L1_ffn_in['shared_down_w']}

def reference(x, ctx_2048, mask_Bx1x2048_fk1, L0_attn_q_out, L0_attn_k_out, L0_attn_v_out, L0_attn_w_out, L0_xattn_Wq, L0_xattn_bq, L0_xattn_Wk, L0_xattn_bk, L0_xattn_Wv, L0_xattn_bv, L0_ffn_W_router, L0_ffn_W_gate, L0_ffn_W_up, L0_ffn_W_down, L0_ffn_sA_gate, L0_ffn_sB_gate, L0_ffn_sA_up, L0_ffn_sB_up, L0_ffn_sA_down, L0_ffn_sB_down, L0_ffn_A_gate, L0_ffn_B_gate, L0_ffn_A_up, L0_ffn_B_up, L0_ffn_A_down, L0_ffn_B_down, L0_ffn_expert_bias, L1_attn_W_dq, L1_attn_W_uq, L1_attn_q_ln_g, L1_attn_q_ln_b, L1_attn_W_dkv, L1_attn_W_ukv, L1_attn_kv_ln_g, L1_attn_kv_ln_b, L1_attn_W_o, L1_xattn_Wq, L1_xattn_Wk, L1_xattn_Wv, L1_xattn_Wo, L1_xattn_q_norm_w, L1_xattn_k_norm_w, L1_ffn_router_w, L1_ffn_gate_w, L1_ffn_up_w, L1_ffn_down_w, L1_ffn_shared_gate_w, L1_ffn_shared_up_w, L1_ffn_shared_down_w):
    import jax
    import jax.numpy as jnp

    def _L0_attn_ref(x, q_out, k_out, v_out, w_out):
        import jax, jax.numpy as jnp
        import numpy as np
        import math
        D_MODEL = 512
        NUM_HEADS = 16
        MAX_SEQ_LEN = 512
        BATCH = 2
        b, t, d = x.shape
        h = NUM_HEADS
        d_head = d // h

        def split_heads(y):
            return y.reshape(b, t, h, d_head).transpose(0, 2, 1, 3)
        q = split_heads(x @ q_out)
        k = split_heads(x @ k_out)
        v = split_heads(x @ v_out)
        score = jnp.einsum('bhqd,bhkd->bhqk', q, k) / math.sqrt(d_head)
        causal_mask = jnp.triu(jnp.ones((t, t), dtype=bool), k=1)
        score = jnp.where(causal_mask, -jnp.inf, score)
        weights = jax.nn.softmax(score, axis=-1)
        ctx = jnp.einsum('bhqk,bhkd->bhqd', weights, v)
        ctx = ctx.transpose(0, 2, 1, 3).reshape(b, t, d)
        return ctx @ w_out

    def _L0_xattn_ref(target, source, target_mask, source_mask, Wq, bq, Wk, bk, Wv, bv):
        import math
        import jax, jax.numpy as jnp
        import numpy as np
        SIZE = 256
        HEADS = 16
        HEAD_DIM = SIZE // HEADS
        B, T, S = (2, 512, 512)
        NEG = 1000000.0
        b, _, t = target.shape
        s = source.shape[-1]
        q = jnp.einsum('oc,bct->bot', Wq, target) + bq[None, :, None]
        k = jnp.einsum('oc,bcs->bos', Wk, source) + bk[None, :, None]
        v = jnp.einsum('oc,bcs->bos', Wv, source) + bv[None, :, None]
        q = q.reshape(b, HEADS, HEAD_DIM, t)
        k = k.reshape(b, HEADS, HEAD_DIM, s)
        v = v.reshape(b, HEADS, HEAD_DIM, s)
        dot = jnp.einsum('bhdt,bhds->bhts', q, k) / math.sqrt(HEAD_DIM)
        mask = target_mask[:, :, :, None] * source_mask[:, :, None, :]
        dot = mask * dot - (1.0 - mask) * NEG
        amap = jax.nn.softmax(dot, axis=-1) * mask
        out = jnp.einsum('bhts,bhds->bhdt', amap, v)
        return out.reshape(b, HEADS * HEAD_DIM, t)

    def _L0_ffn_ref(x, W_router, W_gate, W_up, W_down, sA_gate, sB_gate, sA_up, sB_up, sA_down, sB_down, A_gate, B_gate, A_up, B_up, A_down, B_down, expert_bias):
        import jax, jax.numpy as jnp
        import numpy as np
        B, L, D = (2, 256, 512)
        E, TOP_K, RANK, DFF = (8, 2, 8, 1376)

        def _lora(x, A, Bm, scale):
            return x @ A @ Bm * scale

        def _expert_lora(x, A, Bm, w, scale):
            xA = jnp.einsum('bld,edr->bler', x, A)
            xAB = jnp.einsum('bler,erd->bled', xA, Bm) * scale
            return (xAB * w).sum(axis=2)
        scale = 1.0 / RANK
        logits = x @ W_router
        scores = jax.nn.sigmoid(logits)
        biased = scores + expert_bias
        _, topk_idx = jax.lax.top_k(biased, TOP_K)
        topk_scores = jnp.take_along_axis(scores, topk_idx, axis=-1)
        topk_w = topk_scores / (topk_scores.sum(-1, keepdims=True) + 1e-08)
        one_hot = jax.nn.one_hot(topk_idx, E, dtype=x.dtype)
        expert_weights = (one_hot * topk_w[..., None]).sum(axis=2)
        w = expert_weights[..., None]
        gate = x @ W_gate + _lora(x, sA_gate, sB_gate, scale) + _expert_lora(x, A_gate, B_gate, w, scale)
        up = x @ W_up + _lora(x, sA_up, sB_up, scale) + _expert_lora(x, A_up, B_up, w, scale)
        hidden = jax.nn.silu(gate) * up
        out = hidden @ W_down + _lora(hidden, sA_down, sB_down, scale) + _expert_lora(hidden, A_down, B_down, w, scale)
        return out

    def _L1_attn_ref(x, W_dq, W_uq, q_ln_g, q_ln_b, W_dkv, W_ukv, kv_ln_g, kv_ln_b, W_o):
        import jax, jax.numpy as jnp
        import numpy as np
        import math
        D_MODEL = 512
        N_HEADS = 16
        Q_PROJ = D_MODEL // 4
        KV_PROJ = D_MODEL // 4
        DH = D_MODEL // N_HEADS
        LN_EPS = 1e-05

        def _layernorm(x, gamma, beta):
            mu = jnp.mean(x, axis=-1, keepdims=True)
            var = jnp.var(x, axis=-1, keepdims=True)
            return (x - mu) * jax.lax.rsqrt(var + LN_EPS) * gamma + beta
        B, S, D = x.shape
        H, dh = (N_HEADS, DH)
        cq = _layernorm(x @ W_dq, q_ln_g, q_ln_b)
        Q = cq @ W_uq
        ckv = _layernorm(x @ W_dkv, kv_ln_g, kv_ln_b)
        KV = ckv @ W_ukv
        K, V = (KV[..., :D], KV[..., D:])
        q = Q.reshape(B, S, H, dh).transpose(0, 2, 1, 3)
        k = K.reshape(B, S, H, dh).transpose(0, 2, 1, 3)
        v = V.reshape(B, S, H, dh).transpose(0, 2, 1, 3)
        scores = jnp.einsum('bhqd,bhkd->bhqk', q, k) / math.sqrt(float(dh))
        causal = jnp.tril(jnp.ones((S, S), dtype=bool))
        scores = jnp.where(causal, scores, -jnp.inf)
        attn = jax.nn.softmax(scores, axis=-1)
        o = jnp.einsum('bhqk,bhkd->bhqd', attn, v)
        o = o.transpose(0, 2, 1, 3).reshape(B, S, D)
        return o @ W_o.T

    def _L1_xattn_ref(hidden_states, encoder_hidden_states, Wq, Wk, Wv, Wo, q_norm_w, k_norm_w):
        import jax, jax.numpy as jnp
        import numpy as np
        HIDDEN = 512
        N_HEADS = 16
        N_KV_HEADS = 4
        HEAD_DIM = 128
        EPS = 1e-06

        def rms_norm(x, w, eps=EPS):
            xf = x.astype(jnp.float32)
            var = jnp.mean(xf * xf, axis=-1, keepdims=True)
            return w * (xf * jax.lax.rsqrt(var + eps)).astype(x.dtype)
        B, S, _ = hidden_states.shape
        S_enc = encoder_hidden_states.shape[1]
        groups = N_HEADS // N_KV_HEADS
        scale = 1.0 / HEAD_DIM ** 0.5
        q = (hidden_states @ Wq).reshape(B, S, N_HEADS, HEAD_DIM)
        k = (encoder_hidden_states @ Wk).reshape(B, S_enc, N_KV_HEADS, HEAD_DIM)
        v = (encoder_hidden_states @ Wv).reshape(B, S_enc, N_KV_HEADS, HEAD_DIM)
        q = rms_norm(q, q_norm_w)
        k = rms_norm(k, k_norm_w)
        k = jnp.repeat(k, groups, axis=2)
        v = jnp.repeat(v, groups, axis=2)
        scores = jnp.einsum('bqhd,bkhd->bhqk', q, k) * scale
        probs = jax.nn.softmax(scores, axis=-1)
        out = jnp.einsum('bhqk,bkhd->bqhd', probs, v)
        out = out.reshape(B, S, N_HEADS * HEAD_DIM)
        return out @ Wo

    def _L1_ffn_ref(hidden_states, router_w, gate_w, up_w, down_w, shared_gate_w, shared_up_w, shared_down_w):
        import jax, jax.numpy as jnp
        import numpy as np
        SEQ, BS, D, F, E = (256, 2, 512, 512, 8)
        S, B, Dm = hidden_states.shape
        x = hidden_states.reshape(-1, Dm)
        logits = x @ router_w
        expert_idx = jnp.argmax(logits, axis=-1)
        score = jax.nn.sigmoid(jnp.max(logits, axis=-1))
        xs = x * score[:, None]
        n_experts = router_w.shape[1]
        out = jnp.zeros_like(x)
        for e in range(n_experts):
            m = (expert_idx == e)[:, None]
            xe = jnp.where(m, xs, 0.0)
            h = jax.nn.silu(xe @ gate_w[e]) * (xe @ up_w[e])
            out = out + jnp.where(m, h @ down_w[e], 0.0)
        shared = jax.nn.silu(x @ shared_gate_w) * (x @ shared_up_w) @ shared_down_w
        return (out + shared).reshape(S, B, Dm)
    x = _layernorm(x + _L0_attn_ref(x, L0_attn_q_out, L0_attn_k_out, L0_attn_v_out, L0_attn_w_out), axis=-1)
    x = _layernorm(x + _L0_xattn_ref(x, ctx_2048, mask_Bx1x2048_fk1, mask_Bx1x2048_fk1, L0_xattn_Wq, L0_xattn_bq, L0_xattn_Wk, L0_xattn_bk, L0_xattn_Wv, L0_xattn_bv), axis=-1)
    x = _layernorm(x + _L0_ffn_ref(x, L0_ffn_W_router, L0_ffn_W_gate, L0_ffn_W_up, L0_ffn_W_down, L0_ffn_sA_gate, L0_ffn_sB_gate, L0_ffn_sA_up, L0_ffn_sB_up, L0_ffn_sA_down, L0_ffn_sB_down, L0_ffn_A_gate, L0_ffn_B_gate, L0_ffn_A_up, L0_ffn_B_up, L0_ffn_A_down, L0_ffn_B_down, L0_ffn_expert_bias), axis=-1)
    x = _layernorm(x + _L1_attn_ref(x, L1_attn_W_dq, L1_attn_W_uq, L1_attn_q_ln_g, L1_attn_q_ln_b, L1_attn_W_dkv, L1_attn_W_ukv, L1_attn_kv_ln_g, L1_attn_kv_ln_b, L1_attn_W_o), axis=-1)
    x = _layernorm(x + _L1_xattn_ref(x, ctx_2048, L1_xattn_Wq, L1_xattn_Wk, L1_xattn_Wv, L1_xattn_Wo, L1_xattn_q_norm_w, L1_xattn_k_norm_w), axis=-1)
    x = _layernorm(x + _L1_ffn_ref(x, L1_ffn_router_w, L1_ffn_gate_w, L1_ffn_up_w, L1_ffn_down_w, L1_ffn_shared_gate_w, L1_ffn_shared_up_w, L1_ffn_shared_down_w), axis=-1)
    return x

_drawn_inputs = setup_inputs


def setup_inputs(seed=0):
    import zlib

    import numpy as np

    out = dict(_drawn_inputs(seed))
    spreads = {'L0_ffn_expert_bias': (0.0, 0.8),
     'L1_attn_q_ln_g': (1.0, 0.6),
     'L1_attn_q_ln_b': (0.0, 0.8),
     'L1_attn_kv_ln_g': (1.0, 0.6),
     'L1_attn_kv_ln_b': (0.0, 0.8),
     'L1_xattn_q_norm_w': (1.0, 0.6),
     'L1_xattn_k_norm_w': (1.0, 0.6)}
    factors = {'L0_xattn_bq': 8.0,
     'L0_xattn_bk': 8.0,
     'L0_xattn_bv': 8.0,
     'L0_ffn_W_router': 8.0,
     'L0_ffn_sA_gate': 8.0,
     'L0_ffn_sB_gate': 8.0,
     'L0_ffn_sA_up': 8.0,
     'L0_ffn_sB_up': 8.0,
     'L0_ffn_sA_down': 8.0,
     'L0_ffn_sB_down': 8.0,
     'L0_ffn_A_gate': 8.0,
     'L0_ffn_B_gate': 8.0,
     'L0_ffn_A_up': 8.0,
     'L0_ffn_B_up': 8.0,
     'L0_ffn_A_down': 8.0,
     'L0_ffn_B_down': 8.0,
     'L1_attn_W_dq': 8.0,
     'L1_attn_W_uq': 8.0,
     'L1_attn_W_dkv': 8.0,
     'L1_attn_W_ukv': 8.0,
     'L1_attn_W_o': 8.0,
     'L1_ffn_router_w': 2.839,
     'L1_ffn_gate_w': 2.708,
     'L1_ffn_up_w': 2.675,
     'L1_ffn_down_w': 2.682}
    for name, (base, spread) in spreads.items():
        noise = np.random.default_rng([zlib.crc32(name.encode()), seed]).standard_normal(out[name].shape)
        drawn = base * np.exp(spread * noise) if base else spread * noise
        out[name] = jnp.asarray(drawn.astype(out[name].dtype))
    for name, factor in factors.items():
        out[name] = (out[name] * factor).astype(out[name].dtype)
    return out
```

```python
from contextlib import ExitStack

import concourse.bass as bass
from concourse import mybir

F32 = mybir.dt.float32
BF16 = mybir.dt.bfloat16
ALU = mybir.AluOpType
ACT = mybir.ActivationFunctionType
AX = mybir.AxisListType

P = 128
B = 8
T = 256
D = 512
KC = D // P
TT = T // P
TURNS = B // 2
H = 16
DH = D // H
EPS = 1e-5
MASKED = -1e30


class BankUses:

    def __init__(self, base, turn, turns):
        self.base, self.per, self.at = base, [0] * 8, {}
        for use, bank in turn:
            self.at[use] = (bank, self.per[bank])
            self.per[bank] += 1
        self.after = [n + turns * per for n, per in zip(base, self.per)]

    def bank(self, use):
        return self.at[use][0]

    def before(self, use, turn):
        bank, nth = self.at[use]
        return turn * self.per[bank] + (self.base[bank] + nth)


class Core:

    def __init__(self, nc, ctx):
        self.nc, self.ctx = nc, ctx
        self.banks = ctx.enter_context(nc.psum_tensor("banks", [P, 8, 512], F32))
        self.psum = [self.banks[:, i, :] for i in range(8)]
        self.bank_full = [ctx.enter_context(nc.semaphore(f"bank_full{i}")) for i in range(8)]
        self.bank_free = [ctx.enter_context(nc.semaphore(f"bank_free{i}")) for i in range(8)]
        self.uses = [0] * 8
        self.ident = ctx.enter_context(nc.sbuf_tensor("ident", [P, P], F32))
        self.ident_bf = ctx.enter_context(nc.sbuf_tensor("ident_bf", [P, P], BF16))
        self.causal = ctx.enter_context(nc.sbuf_tensor("causal", [P, 4, P], BF16))
        self.minus_half = ctx.enter_context(nc.sbuf_tensor("minus_half", [P, 32], F32))


def constants(core):
    nc = core.nc
    with ExitStack() as ctx:
        filled = core.ctx.enter_context(nc.semaphore("constants_filled"))
        block = ctx.enter_context(nc.Block())

        @block.gpsimd
        def _(pool):
            for bank in range(8):
                pool.sem_inc(core.bank_free[bank], 1)
            pool.memset(core.ident[:, :], 0.0).then_inc(filled, 1)
            pool.memset(core.ident_bf[:, :], 0.0).then_inc(filled, 1)
            pool.memset(core.causal[:, :, :], 0.0).then_inc(filled, 1)
            pool.memset(core.minus_half[:, :], -0.5).then_inc(filled, 1)
            pool.wait_ge(filled, 4)
            pool.affine_select(out=core.ident[:, :], in_=core.ident[:, :], compare_op=ALU.not_equal, fill=1.0,
                               base=0, pattern=[[-1, P]], channel_multiplier=1).then_inc(filled, 1)
            pool.affine_select(out=core.ident_bf[:, :], in_=core.ident_bf[:, :], compare_op=ALU.not_equal,
                               fill=1.0, base=0, pattern=[[-1, P]], channel_multiplier=1).then_inc(filled, 1)
            pool.affine_select(out=core.causal[:, :, :], in_=core.causal[:, :, :], compare_op=ALU.is_ge,
                               fill=MASKED, base=0, pattern=[[0, 4], [-1, P]],
                               channel_multiplier=1).then_inc(filled, 1)
            pool.wait_ge(filled, 7)


class Norm:

    def __init__(self, core, name):
        nc, ctx = core.nc, core.ctx_stage
        self.x = ctx.enter_context(nc.sbuf_tensor(f"{name}_x", [P, 2, TT, D], F32))
        self.z = ctx.enter_context(nc.sbuf_tensor(f"{name}_z", [P, 2, TT, D], F32))
        self.stats = ctx.enter_context(nc.sbuf_tensor(f"{name}_stats", [P, TT, 6], F32))
        self.moments = ctx.enter_context(nc.sbuf_tensor(f"{name}_moments", [P, TT, 2], F32))
        self.vareps = ctx.enter_context(nc.sbuf_tensor(f"{name}_vareps", [P, TT], F32))
        self.rstd = ctx.enter_context(nc.sbuf_tensor(f"{name}_rstd", [P, TT], F32))
        self.loaded = [core.ctx.enter_context(nc.semaphore(f"{name}_x_loaded{u}")) for u in range(2)]
        self.moved = core.ctx.enter_context(nc.semaphore(f"{name}_moments_steps"))
        self.rstd_ready = core.ctx.enter_context(nc.semaphore(f"{name}_rstd_ready"))
        self.out_ready = core.ctx.enter_context(nc.semaphore(f"{name}_out_ready"))
        self.stored = [core.ctx.enter_context(nc.semaphore(f"{name}_stored{u}")) for u in range(2)]

    STEPS = 6


def norm_dve(core, norm, uses, turn, u):
    dve = core.nc.vector
    full, free = core.bank_full, core.bank_free
    y = [uses.bank(f"y{j}.{u}") for j in range(TT)]
    n = [uses.before(f"y{j}.{u}", turn) for j in range(TT)]
    s = (turn * 2 + u) * norm.STEPS
    z = norm.z[:, u]
    dve.wait_ge(full[y[0]], n[0] + 1)
    dve.wait_ge(norm.loaded[u], turn * 16 + 16)
    if u == 0:
        dve.wait_ge(norm.stored[0], turn * 16 + 1)
    else:
        dve.wait_ge(norm.stored[1], turn * 16 + 1)
    dve.tensor_tensor(z[:, 0, :], core.psum[y[0]][:, :], norm.x[:, u, 0, :], ALU.add).then_inc(free[y[0]], 1)
    dve.wait_ge(free[y[0]], n[0] + 2)
    dve.bn_stats(norm.stats[:, 0, :], z[:, 0, :]).then_inc(norm.moved, 1)
    dve.wait_ge(full[y[1]], n[1] + 1)
    dve.wait_ge(norm.moved, s + 1)
    dve.tensor_tensor(z[:, 1, :], core.psum[y[1]][:, :], norm.x[:, u, 1, :], ALU.add).then_inc(free[y[1]], 1)
    dve.bn_aggr(norm.moments[:, 0, :], norm.stats[:, 0, :]).then_inc(norm.moved, 1)
    dve.wait_ge(free[y[1]], n[1] + 2)
    dve.bn_stats(norm.stats[:, 1, :], z[:, 1, :]).then_inc(norm.moved, 1)
    dve.wait_ge(norm.moved, s + 3)
    dve.tensor_scalar(norm.vareps[:, 0:1], norm.moments[:, 0, 1:2], EPS, None, ALU.add).then_inc(norm.moved, 1)
    dve.bn_aggr(norm.moments[:, 1, :], norm.stats[:, 1, :]).then_inc(norm.moved, 1)
    dve.wait_ge(norm.moved, s + 5)
    dve.tensor_scalar(norm.vareps[:, 1:2], norm.moments[:, 1, 1:2], EPS, None, ALU.add).then_inc(norm.moved, 1)
    for j in range(TT):
        dve.wait_ge(norm.rstd_ready, turn * 2 + (u + 1))
        dve.tensor_scalar(z[:, j, :], z[:, j, :], norm.moments[:, j, 0:1], norm.rstd[:, j:j + 1],
                          ALU.subtract, ALU.mult).then_inc(norm.out_ready, 1)


def norm_pool(core, norm, turn, u, steps=Norm.STEPS):
    pool = core.nc.gpsimd
    pool.wait_ge(norm.moved, (turn * 2 + u) * steps + steps)
    pool.tensor_tensor(norm.rstd[:, :], norm.vareps[:, :], core.minus_half[:, 0:TT], ALU.pow)\
        .then_inc(norm.rstd_ready, 1)


def load_x(core, norm, x_src, b, u):
    core.nc.sync.dma_start(norm.x[:, u], x_src[b].rearrange("(j p) d -> p j d", p=P)).then_inc(norm.loaded[u], 16)


def store_x(core, norm, x_dst, b, turn, u):
    core.nc.sync.wait_ge(norm.out_ready, (turn * 2 + u) * TT + TT)
    core.nc.sync.dma_start(x_dst[b].rearrange("(j p) d -> p j d", p=P), norm.z[:, u]).then_inc(norm.stored[u], 16)


def rows_in_and_out(core, norm, uses, x_src, x_dst, load_context=None, context_free=None):
    sp = core.nc.sync

    def x_free(turn, u):
        bank, n = uses.bank(f"y1.{u}"), uses.before(f"y1.{u}", turn)
        sp.wait_ge(core.bank_free[bank], n + 2)

    for u in range(2):
        sp.sem_inc(norm.stored[u], 1)
        load_x(core, norm, x_src, u, u)
        if load_context:
            load_context(u, u)
    with sp.Fori(0, TURNS - 1) as turn:
        for u in range(2):
            if load_context:
                context_free(turn, u)
                load_context(turn * 2 + (u + 2), u)
            x_free(turn, u)
            load_x(core, norm, x_src, turn * 2 + (u + 2), u)
            store_x(core, norm, x_dst, turn * 2 + u, turn, u)
    for u in range(2):
        store_x(core, norm, x_dst, 2 * (TURNS - 1) + u, TURNS - 1, u)
    for u in range(2):
        sp.wait_ge(norm.stored[u], 16 * TURNS + 1)



UNITS = 12
LAG = 3
RANK = D // 4


def self_attention(core, name, x_src, x_dst, weights, latent):
    nc = core.nc
    turn_uses = []
    for u in range(2):
        turn_uses += [(f"xT0.{u}", 0), (f"xT1.{u}", 1)]
        if latent:
            turn_uses += [(f"low.{u}", 2), (f"lowT.{u}", 3), (f"q0.{u}", 4), (f"q1.{u}", 5),
                          (f"k0.{u}", 6), (f"k1.{u}", 7), (f"v0.{u}", 0), (f"v1.{u}", 1)]
        else:
            turn_uses += [(f"q0.{u}", 2), (f"q1.{u}", 3), (f"k0.{u}", 4), (f"k1.{u}", 5),
                          (f"v0.{u}", 6), (f"v1.{u}", 7)]
        for n in range(UNITS + LAG + 1):
            if n < UNITS:
                turn_uses.append((f"S{n}.{u}", n % 4))
            if LAG <= n < UNITS + LAG:
                turn_uses.append((f"T{n - LAG}.{u}", 4 + n % 2))
            m = n - LAG - 1
            if m >= 0 and m % 3 == 2:
                turn_uses += [(f"R{m // 3}.{u}", 7), (f"O{m // 3}.{u}", 6)]
        turn_uses += [(f"y0.{u}", 2), (f"y1.{u}", 3)]
    uses = BankUses(core.uses, turn_uses, TURNS)
    core.uses = uses.after
    full, free, psum = core.bank_full, core.bank_free, core.psum

    with ExitStack() as ctx:
        core.ctx_stage = ctx

        def sb(tag, shape, dtype=F32):
            return ctx.enter_context(nc.sbuf_tensor(f"{name}_{tag}", shape, dtype))

        def sem(tag):
            return core.ctx.enter_context(nc.semaphore(f"{name}_{tag}"))

        norm = Norm(core, name)
        if latent:
            w_down = sb("w_down", [P, KC, 2 * RANK])
            w_uq = sb("w_uq", [P, D])
            w_ukv = sb("w_ukv", [P, 2 * D])
            gamma = sb("gamma", [P, 2])
            beta = sb("beta", [P, 2])
            low_stats = sb("low_stats", [P, 4, 6])
            low_moments = sb("low_moments", [P, 4, 2])
            low_vareps = sb("low_vareps", [P, 4])
            low_rstd = sb("low_rstd", [P, 4])
            low = sb("low", [P, 4, RANK])
            lowT = sb("lowT", [P, 4, P])
            low_steps = sem("low_steps")
            low_rstd_ready = sem("low_rstd_ready")
        else:
            w_q = sb("w_q", [P, KC, D])
            w_k = sb("w_k", [P, KC, D])
            w_v = sb("w_v", [P, KC, D])
        w_o = sb("w_o", [P, KC, D])
        xT = sb("xT", [P, KC, T])
        qT = sb("qT", [P, 4, T])
        k_of_head = sb("k_of_head", [P, H, T])
        v = sb("v", [P, TT, D])
        minus_max = sb("minus_max", [P, UNITS, 4])
        sums = sb("sums", [P, 4, 8])
        inverse = sb("inverse", [P, 4, 8])
        inverse_rows = sb("inverse_rows", [P, 2, 8, DH])
        probs = sb("probs", [P, 3, 512])
        probsT = sb("probsT", [P, 2, 4, 3 * P])
        spread = sb("spread", [P, 2, T])
        ctxT = sb("ctxT", [P, 4, T])
        weights_loaded = sem("weights_loaded")
        k_cleared = sem("k_cleared")
        max_ready = sem("max_ready")
        inverse_ready = sem("inverse_ready")
        inverse_spread = sem("inverse_spread")
        N_WEIGHTS = len(weights)

        def wait_bank(engine, use, turn):
            engine.wait_ge(free[uses.bank(use)], uses.before(use, turn) + 1)

        def wait_full(engine, use, turn):
            engine.wait_ge(full[uses.bank(use)], uses.before(use, turn) + 1)

        def wait_free(engine, use, turn):
            engine.wait_ge(free[uses.bank(use)], uses.before(use, turn) + 2)

        block = ctx.enter_context(nc.Block())

        @block.sync
        def _(sp):
            rows_in_and_out(core, norm, uses, x_src, x_dst)

        @block.gpsimd
        def _(pool):
            if latent:
                pool.dma_start(w_down[:, :, 0:RANK], weights["dq"].rearrange("(c p) n -> p c n", p=P)).then_inc(weights_loaded, 16)
                pool.dma_start(w_down[:, :, RANK:], weights["dkv"].rearrange("(c p) n -> p c n", p=P)).then_inc(weights_loaded, 16)
                pool.dma_start(w_uq[:, :], weights["uq"]).then_inc(weights_loaded, 16)
                pool.dma_start(w_ukv[:, :], weights["ukv"]).then_inc(weights_loaded, 16)
                for j, key in enumerate(("q_g", "kv_g")):
                    pool.dma_start(gamma[:, j:j + 1], weights[key].rearrange("(p a) -> p a", a=1)).then_inc(weights_loaded, 16)
                for j, key in enumerate(("q_b", "kv_b")):
                    pool.dma_start(beta[:, j:j + 1], weights[key].rearrange("(p a) -> p a", a=1)).then_inc(weights_loaded, 16)
            else:
                for key, w in (("q", w_q), ("k", w_k), ("v", w_v)):
                    pool.dma_start(w[:, :, :], weights[key].rearrange("(c p) n -> p c n", p=P)).then_inc(weights_loaded, 16)
            pool.dma_start(w_o[:, :, :], weights["o"].rearrange("(c p) n -> p c n", p=P)).then_inc(weights_loaded, 16)
            pool.memset(k_of_head[:, :, :], 0.0).then_inc(k_cleared, 1)
            with pool.Fori(0, TURNS) as turn:
                for u in range(2):
                    if latent:
                        pool.wait_ge(low_steps, (turn * 2 + u) * 4 + 4)
                        pool.tensor_tensor(low_rstd[:, :], low_vareps[:, :], core.minus_half[:, 0:4], ALU.pow)\
                            .then_inc(low_rstd_ready, 1)
                    norm_pool(core, norm, turn, u)

        @block.scalar
        def _(act):
            with act.Fori(0, TURNS) as turn:
                for u in range(2):
                    b = turn * 2 + u
                    for j in range(2):
                        use = f"xT{j}.{u}"
                        wait_full(act, use, turn)
                        act.copy(xT[:, 2 * j:2 * j + 2, :], psum[uses.bank(use)][:, :].rearrange("p (c t) -> p c t", c=2))\
                            .then_inc(free[uses.bank(use)], 1)
                    if latent:
                        use = f"lowT.{u}"
                        wait_full(act, use, turn)
                        act.wait_ge(weights_loaded, 16 * N_WEIGHTS)
                        for j in range(2):
                            ins = act.activation(lowT[:, 2 * j:2 * j + 2, :],
                                           psum[uses.bank(use)][:, 2 * j * P:(2 * j + 2) * P].rearrange("p (c t) -> p c t", c=2),
                                           ACT.Identity, bias=beta[:, j:j + 1], scale=gamma[:, j:j + 1])
                        ins.then_inc(free[uses.bank(use)], 1)
                    for j in range(2):
                        use = f"q{j}.{u}"
                        wait_full(act, use, turn)
                        act.activation(qT[:, 2 * j:2 * j + 2, :], psum[uses.bank(use)][:, :].rearrange("p (c t) -> p c t", c=2),
                                       ACT.Copy, scale=float(DH) ** -0.5).then_inc(free[uses.bank(use)], 1)
                    for j in range(TT):
                        use = f"v{j}.{u}"
                        wait_full(act, use, turn)
                        act.copy(v[:, j, :], psum[uses.bank(use)][:, :]).then_inc(free[uses.bank(use)], 1)

                    def exps(n):
                        use, c, k = f"S{n}.{u}", n // 3, n % 3
                        act.wait_ge(max_ready, b * UNITS + (n + 1))
                        if n >= 3:
                            wait_full(act, f"T{n - 3}.{u}", turn)
                        heads, width = (4, P) if k == 0 else (2, T)
                        for i in range(heads):
                            at = i if k == 0 else 4 + 2 * (k - 1) + i
                            ins = act.activation(probs[:, n % 3, i * width:(i + 1) * width],
                                           psum[uses.bank(use)][:, i * width:(i + 1) * width], ACT.Exp,
                                           bias=minus_max[:, n, i:i + 1], accum_out=sums[:, c, at:at + 1])
                        ins.then_inc(free[uses.bank(use)], 1)

                    def spread_out(c):
                        use = f"R{c}.{u}"
                        wait_full(act, use, turn)
                        if c >= 2:
                            wait_free(act, f"O{c - 2}.{u}", turn)
                        act.copy(spread[:, c % 2, :], psum[uses.bank(use)][:, 0:T]).then_inc(free[uses.bank(use)], 1)

                    for n in range(UNITS + LAG + 1):
                        if n < UNITS:
                            exps(n)
                        m = n - LAG - 1
                        if m >= 0 and m % 3 == 2:
                            spread_out(m // 3)

        @block.vector
        def _(dve):
            with dve.Fori(0, TURNS) as turn:
                for u in range(2):
                    b = turn * 2 + u
                    if latent:
                        use = f"low.{u}"
                        bank = psum[uses.bank(use)]
                        s = b * 4
                        wait_full(dve, use, turn)
                        for part in range(4):
                            j, t = part // 2, part % 2
                            ins = dve.bn_stats(low_stats[:, part, :], bank[:, (2 * t + j) * P:(2 * t + j + 1) * P])
                        ins.then_inc(low_steps, 1)
                        dve.wait_ge(low_steps, s + 1)
                        dve.memset(low_vareps[:, :], EPS).then_inc(low_steps, 1)
                        for part in range(4):
                            ins = dve.bn_aggr(low_moments[:, part, :], low_stats[:, part, :])
                        ins.then_inc(low_steps, 1)
                        dve.wait_ge(low_steps, s + 3)
                        dve.tensor_scalar(low_vareps[:, :], low_moments[:, :, 1], EPS, None, ALU.add).then_inc(low_steps, 1)
                        dve.wait_ge(low_rstd_ready, b + 1)
                        for part in range(4):
                            j, t = part // 2, part % 2
                            ins = dve.tensor_scalar(low[:, part, :], bank[:, (2 * t + j) * P:(2 * t + j + 1) * P],
                                                    low_moments[:, part, 0:1], low_rstd[:, part:part + 1],
                                                    ALU.subtract, ALU.mult)
                        ins.then_inc(free[uses.bank(use)], 1)
                    dve.wait_ge(k_cleared, 1)
                    for j in range(2):
                        use = f"k{j}.{u}"
                        wait_full(dve, use, turn)
                        for i in range(4):
                            rows = slice(DH * i, DH * i + DH)
                            ins = dve.tensor_copy(k_of_head[rows, 8 * j + i:8 * j + i + 5:4, :],
                                                  psum[uses.bank(use)][rows, :].rearrange("p (c t) -> p c t", c=2))
                        ins.then_inc(free[uses.bank(use)], 1)

                    def row_max(n):
                        use, k = f"S{n}.{u}", n % 3
                        wait_full(dve, use, turn)
                        heads = 4 if k == 0 else 2
                        dve.tensor_reduce(minus_max[:, n, 0:heads],
                                          psum[uses.bank(use)][:, :].rearrange("p (h s) -> p h s", h=heads),
                                          AX.X, ALU.max, negate=True).then_inc(max_ready, 1)

                    def probs_out(n):
                        use, c, k = f"T{n}.{u}", n // 3, n % 3
                        wait_full(dve, use, turn)
                        if c >= 2:
                            wait_full(dve, f"O{c - 2}.{u}", turn)
                        if k == 0:
                            out = probsT[:, c % 2, :, 0:P]
                        else:
                            out = probsT[:, c % 2, 2 * (k - 1):2 * k, P:3 * P]
                        dve.tensor_copy(out, psum[uses.bank(use)][:, :].rearrange("p (h s) -> p h s", h=4 if k == 0 else 2))\
                            .then_inc(free[uses.bank(use)], 1)

                    def invert(c):
                        wait_free(dve, f"S{3 * c + 2}.{u}", turn)
                        dve.reciprocal(inverse[:, c, :], sums[:, c, :]).then_inc(inverse_ready, 1)
                        dve.wait_ge(inverse_ready, b * 4 + (c + 1))
                        if c >= 2:
                            wait_full(dve, f"R{c - 2}.{u}", turn)
                        dve.tensor_copy(inverse_rows[:, c % 2], inverse[:, c, :].unsqueeze(2).broadcast_to([P, 8, DH]))\
                            .then_inc(inverse_spread, 1)

                    def scale_ctx(c):
                        use = f"O{c}.{u}"
                        wait_full(dve, use, turn)
                        wait_free(dve, f"R{c}.{u}", turn)
                        dve.tensor_tensor(ctxT[:, c, :], psum[uses.bank(use)][:, 0:T], spread[:, c % 2, :], ALU.mult)\
                            .then_inc(free[uses.bank(use)], 1)

                    for n in range(UNITS + LAG + 1):
                        if n < UNITS:
                            row_max(n)
                        if LAG <= n < UNITS + LAG:
                            m = n - LAG
                            if m % 3 == 2:
                                invert(m // 3)
                            probs_out(m)
                        m = n - LAG - 1
                        if m >= 0 and m % 3 == 2:
                            scale_ctx(m // 3)
                    norm_dve(core, norm, uses, turn, u)

        @block.tensor
        def _(pe):
            pe.wait_ge(weights_loaded, 16 * N_WEIGHTS)
            with pe.Fori(0, TURNS) as turn:
                for u in range(2):
                    b = turn * 2 + u

                    def done(ins, use):
                        ins.then_inc(full[uses.bank(use)], 1)

                    pe.wait_ge(norm.loaded[u], turn * 16 + 16)
                    for j in range(2):
                        use = f"xT{j}.{u}"
                        wait_bank(pe, use, turn)
                        for c in range(2):
                            for t in range(TT):
                                d = 2 * j + c
                                ins = pe.transpose(psum[uses.bank(use)][:, (c * TT + t) * P:(c * TT + t + 1) * P],
                                                   norm.x[:, u, t, d * P:(d + 1) * P], core.ident[:, :])
                        done(ins, use)

                    for j in range(2):
                        wait_free(pe, f"xT{j}.{u}", turn)
                    if latent:
                        use = f"low.{u}"
                        wait_bank(pe, use, turn)
                        for t in range(TT):
                            for c in range(KC):
                                ins = pe.matmul(psum[uses.bank(use)][:, t * 2 * RANK:(t + 1) * 2 * RANK],
                                                xT[:, c, t * P:(t + 1) * P], w_down[:, c, :], start=c == 0, stop=c == KC - 1)
                        done(ins, use)
                        wait_free(pe, use, turn)
                        use = f"lowT.{u}"
                        wait_bank(pe, use, turn)
                        for part in range(4):
                            ins = pe.transpose(psum[uses.bank(use)][:, part * P:(part + 1) * P], low[:, part, :], core.ident[:, :])
                        done(ins, use)
                        wait_free(pe, use, turn)
                    for key in ("q", "k"):
                        for j in range(2):
                            use = f"{key}{j}.{u}"
                            wait_bank(pe, use, turn)
                            for m in range(2):
                                cols = slice((2 * j + m) * P, (2 * j + m + 1) * P)
                                out = psum[uses.bank(use)][:, m * T:(m + 1) * T]
                                if latent:
                                    w, low_x = (w_uq, lowT[:, 0:2, :]) if key == "q" else (w_ukv, lowT[:, 2:4, :])
                                    ins = pe.matmul(out, w[:, cols], low_x, start=True, stop=True)
                                else:
                                    w = w_q if key == "q" else w_k
                                    for c in range(KC):
                                        ins = pe.matmul(out, w[:, c, cols], xT[:, c, :], start=c == 0, stop=c == KC - 1)
                            done(ins, use)
                    for t in range(TT):
                        use = f"v{t}.{u}"
                        wait_bank(pe, use, turn)
                        if latent:
                            ins = pe.matmul(psum[uses.bank(use)][:, :], lowT[:, 2 + t, :], w_ukv[:, D:2 * D], start=True, stop=True)
                        else:
                            for c in range(KC):
                                ins = pe.matmul(psum[uses.bank(use)][:, :], xT[:, c, t * P:(t + 1) * P], w_v[:, c, :],
                                                start=c == 0, stop=c == KC - 1)
                        done(ins, use)

                    def scores(n):
                        use, c, k = f"S{n}.{u}", n // 3, n % 3
                        if n == 0:
                            for w in ("q0", "q1", "k0", "k1", "v0", "v1"):
                                wait_free(pe, f"{w}.{u}", turn)
                        wait_bank(pe, use, turn)
                        bank = psum[uses.bank(use)]
                        if k == 0:
                            pe.matmul(bank[:, :], qT[:, c, 0:P], k_of_head[:, 4 * c:4 * c + 4, 0:P], start=True, stop=False)
                            ins = pe.matmul(bank[:, :], core.ident_bf[:, :], core.causal[:, :, :], start=False, stop=True)
                        else:
                            h = 4 * c + 2 * (k - 1)
                            pe.matmul(bank[:, :], qT[:, c, P:T], k_of_head[:, h:h + 2, :], start=True, stop=False)
                            ins = pe.matmul(bank[:, :].rearrange("p (h s) -> p h s", h=2)[:, :, P:T], core.ident_bf[:, :],
                                            core.causal[:, 0:2, :], start=False, stop=True)
                        done(ins, use)

                    def transposes(n):
                        use, c, k = f"T{n}.{u}", n // 3, n % 3
                        wait_bank(pe, use, turn)
                        wait_free(pe, f"S{n}.{u}", turn)
                        for j in range(4):
                            ins = pe.transpose(psum[uses.bank(use)][:, j * P:(j + 1) * P],
                                               probs[:, n % 3, j * P:(j + 1) * P], core.ident[:, :])
                        done(ins, use)

                    def context(c):
                        use = f"R{c}.{u}"
                        wait_bank(pe, use, turn)
                        pe.wait_ge(inverse_spread, b * 4 + (c + 1))
                        for t in range(TT):
                            ins = pe.transpose(psum[uses.bank(use)][:, t * P:(t + 1) * P],
                                               inverse_rows[:, c % 2, 4 * t:4 * t + 4, :].rearrange("p h d -> p (h d)"),
                                               core.ident[:, :])
                        done(ins, use)
                        use = f"O{c}.{u}"
                        wait_bank(pe, use, turn)
                        for k in (1, 2):
                            wait_free(pe, f"T{3 * c + k}.{u}", turn)
                        for i in range(4):
                            pe.matmul(psum[uses.bank(use)][DH * i:DH * i + DH, 0:T], v[:, 0, (4 * c + i) * DH:(4 * c + i + 1) * DH],
                                      probsT[:, c % 2, i, 0:T], start=True, stop=False)
                        for i in range(4):
                            ins = pe.matmul(psum[uses.bank(use)][DH * i:DH * i + DH, P:T], v[:, 1, (4 * c + i) * DH:(4 * c + i + 1) * DH],
                                            probsT[:, c % 2, i, T:3 * P], start=False, stop=True)
                        done(ins, use)

                    for n in range(UNITS + LAG + 1):
                        if n < UNITS:
                            scores(n)
                        if LAG <= n < UNITS + LAG:
                            transposes(n - LAG)
                        m = n - LAG - 1
                        if m >= 0 and m % 3 == 2:
                            context(m // 3)
                    for t in range(TT):
                        use = f"y{t}.{u}"
                        wait_bank(pe, use, turn)
                        if t == 0:
                            wait_free(pe, f"O3.{u}", turn)
                        for c in range(4):
                            ins = pe.matmul(psum[uses.bank(use)][:, :], ctxT[:, c, t * P:(t + 1) * P], w_o[:, c, :],
                                            start=c == 0, stop=c == 3)
                        done(ins, use)



SIZE = T
CH = SIZE // H
POS = D
PT = POS // P
PARTS = 3
PAIRS = [(0, 0), (0, 1), (1, 0), (0, 2), (1, 1), (2, 0)]
MASK_ROW = CH * len(PAIRS)
MAX_ROW = MASK_ROW + len(PAIRS)
ROWS = MAX_ROW + PARTS
SCALE = float(CH) ** -0.5
NEG = 1e6
UNIT_LEAD = 22
SLOTS = 4 * 16


def xattn_constants():
    import numpy as np
    m = np.zeros((P, 4, P), np.float32)
    for half in range(2):
        for i in range(4):
            for d in range(CH):
                m[32 * i + d, half, 64 * half + CH * i + d] = 1.0
                m[32 * i + CH, 2 + half, 64 * half + CH * i + d] = 1.0
    return m


def xattn_schedule(has_next, only_lead=False):
    steps = []
    lead = [q for q in range(SLOTS - UNIT_LEAD, SLOTS)]
    for q in (lead if only_lead else range(SLOTS + 4)):
        if q < SLOTS and not only_lead:
            steps.append(("exp", q))
        n = q + UNIT_LEAD
        if n % 2 == 0 and q < SLOTS:
            if n // 2 < 32:
                steps.append(("score", n // 2))
            elif has_next:
                steps.append(("score'", n // 2 - 32))
        if q in (11, 27, 43) and not only_lead:
            steps.append(("shift", (q + 5) // 16))
        if q == SLOTS - 5 and has_next:
            steps.append(("shift'", 0))
        if has_next and not only_lead:
            for w, start in (("q", 8), ("k", 13)):
                if start <= q < start + 5:
                    steps.append(("project " + w, q - start))
            if q == 18:
                steps.append(("project v", 0))
        if q >= 5 and (q - 5) % 4 == 0 and not only_lead:
            steps.append(("context", (q - 5) // 4))
        if q in (37, SLOTS + 3) and not only_lead:
            steps.append(("finish", 0 if q == 37 else 1))
    return steps


def cross_attention_masked(core, name, x_src, ctx_src, x_dst, mask, mask_cols, onehot, weights):
    nc = core.nc

    def listed(tag, steps, ring):
        out = []
        for kind, n in steps:
            if kind in ("score", "score'", "project v") or (kind.startswith("project") and n == 0):
                out.append((f"{tag}{kind}{n}", (0, 2)[ring[0] % 2]))
                ring[0] += 1
            elif kind == "exp":
                out.append((f"{tag}exp{n}", 4 + n % 2))
            elif kind in ("shift", "shift'"):
                out.append((f"{tag}{kind}{n}", 7))
            elif kind == "context" and n % 4 == 0:
                out.append((f"{tag}context{n // 4}", 6))
            elif kind == "finish":
                out += [(f"{tag}sum{n}", 7), (f"{tag}y{n}", (0, 2)[ring[0] % 2])]
                ring[0] += 1
        return out

    first_steps = [("project q", k) for k in range(5)] + [("project k", k) for k in range(5)] + [("project v", 0)]
    first_steps += xattn_schedule(True, only_lead=True)
    middle, last = xattn_schedule(True), xattn_schedule(False)
    ring = [0]
    before = BankUses(core.uses, listed("a", first_steps, ring), 1)
    looped = BankUses(before.after, listed("0", middle, ring) + listed("1", middle, ring), TURNS - 1)
    ending = BankUses(looped.after, listed("0", middle, ring) + listed("1", last, ring), 1)
    core.uses = ending.after
    full, free, psum = core.bank_full, core.bank_free, core.psum

    with ExitStack() as ctx:
        core.ctx_stage = ctx

        def sb(tag, shape, dtype=F32):
            return ctx.enter_context(nc.sbuf_tensor(f"{name}_{tag}", shape, dtype))

        def sem(tag):
            return core.ctx.enter_context(nc.semaphore(f"{name}_{tag}"))

        norm = Norm(core, name)
        context = sb("context", [P, 2, TT, POS])
        target_mask = sb("target_mask", [P, 2, POS])
        source_mask = sb("source_mask", [P, B, PT])
        mask_rows = sb("mask_rows", [B, POS])
        mask_rest = sb("mask_rest", [B, 2, 2, POS])
        mask_parts = sb("mask_parts", [B, 2, PARTS, POS], BF16)
        gather = sb("gather", [P, 4, P])
        w_q = sb("w_q", [P, TT, SIZE])
        w_k = sb("w_k", [P, TT, SIZE])
        w_v = sb("w_v", [P, TT, SIZE])
        b_q = sb("b_q", [P, TT])
        b_k = sb("b_k", [P, TT])
        b_v = sb("b_v", [P, 2, SIZE])
        whole = sb("whole", [P, TT, POS])
        rest = sb("rest", [P, TT, POS])
        parts = sb("parts", [P, 2, PARTS, TT, POS], BF16)
        stacked = [[sb(f"stacked_{w}{u}", [ROWS, H, POS], BF16) for u in range(2)] for w in "qk"]
        v_biased = sb("v_biased", [P, 2, 2, SIZE])
        v = sb("v", [P, 2, PT, H, 2 * CH])
        minus_max = sb("minus_max", [P, 2, 4, PT])
        max_rest = sb("max_rest", [P, PT, 4])
        max_parts = sb("max_parts", [P, PT, PARTS, 4], BF16)
        max_rows = sb("max_rows", [PARTS * 4, 2, POS], BF16)
        probs = sb("probs", [P, 8, POS])
        heads_out = sb("heads_out", [P, 2, POS])
        inverse = sb("inverse", [P, POS])
        scaled = sb("scaled", [P, POS])
        masked = sb("masked", [P, POS])
        parts_dram = nc.dram_tensor(f"{name}_parts_dram", (2, 2, PARTS, SIZE, POS), BF16).ap()
        mask_dram = nc.dram_tensor(f"{name}_mask_parts_dram", (2, B, len(PAIRS), POS), BF16).ap()
        constants_loaded = sem("constants_loaded")
        masks_loaded = sem("masks_loaded")
        mask_split = sem("mask_split")
        mask_written = sem("mask_written")
        cleared = sem("cleared")
        context_loaded = [sem(f"context_loaded{u}") for u in range(2)]
        part_ready = [sem(f"part{k}_ready") for k in range(PARTS)]
        rest_ready = sem("rest_ready")
        parts_written = sem("parts_written")
        stacked_ready = [[sem(f"stacked_ready_{w}{u}") for u in range(2)] for w in "qk"]
        v_ready = sem("v_ready")
        max_steps = sem("max_steps")
        shift_ready = [sem(f"shift_ready{k}") for k in range(2)]
        context_done = sem("context_done")
        finish_steps = sem("finish_steps")
        finish_z = sem("finish_z")
        NORM_STEPS = 5
        CONSTANTS = 16 * 8

        class At:

            def __init__(self, uses, tag, turn, b, u):
                self.uses, self.tag, self.turn, self.b, self.u = uses, tag, turn, b, u

            def bank(self, use):
                return self.uses.bank(self.tag + use)

            def wait_bank(self, engine, use):
                engine.wait_ge(free[self.bank(use)], self.uses.before(self.tag + use, self.turn) + 1)

            def wait_full(self, engine, use):
                engine.wait_ge(full[self.bank(use)], self.uses.before(self.tag + use, self.turn) + 1)

            def wait_free(self, engine, use):
                engine.wait_ge(free[self.bank(use)], self.uses.before(self.tag + use, self.turn) + 2)

            def pair(self, use):
                return core.banks[:, self.bank(use):self.bank(use) + 2, :]

        def every_sequence(engine, run):
            run(first_steps, At(before, "a", 0, -1, 1), -1, 1)
            with engine.Fori(0, TURNS - 1) as turn:
                for u in range(2):
                    run(middle, At(looped, str(u), turn, turn * 2 + u, u), turn * 2 + u, u)
            for u in range(2):
                b = 2 * (TURNS - 1) + u
                run((middle, last)[u], At(ending, str(u), 0, b, u), b, u)

        block = ctx.enter_context(nc.Block())

        @block.sync
        def _(sp):
            for u in range(2):
                sp.sem_inc(norm.stored[u], 1)
            sp.dma_start(mask_rows[:, :], mask).then_inc(masks_loaded, 16)
            sp.dma_start(source_mask[:, :, :], mask_cols).then_inc(constants_loaded, 16)
            sp.dma_start(gather[:, :, :], onehot).then_inc(constants_loaded, 16)
            for key, w in (("q", w_q), ("k", w_k), ("v", w_v)):
                sp.dma_start(w[:, :, :], weights[key].rearrange("(c p) n -> p c n", p=P)).then_inc(constants_loaded, 16)
            sp.dma_start(b_q[:, :], weights["bq"]).then_inc(constants_loaded, 16)
            sp.dma_start(b_k[:, :], weights["bk"]).then_inc(constants_loaded, 16)
            sp.dma_start(b_v[:, :, :], weights["bv"].rearrange("(a b n) -> a b n", a=1, b=1).broadcast_to([P, 2, SIZE]))\
                .then_inc(constants_loaded, 16)

            def load(b, u):
                sp.dma_start(context[:, u], ctx_src[b].rearrange("(j p) d -> p j d", p=P)).then_inc(context_loaded[u], 16)
                sp.dma_start(target_mask[:, u, :], mask[b].unsqueeze(0).broadcast_to([P, POS])).then_inc(context_loaded[u], 16)
                load_x(core, norm, x_src, b, u)

            def store(b, u):
                sp.wait_ge(norm.out_ready, b * TT + TT)
                sp.dma_start(x_dst[b].rearrange("(j p) d -> p j d", p=P), norm.z[:, u]).then_inc(norm.stored[u], 16)

            def stack(w, b, u):
                sp.wait_ge(part_ready[2], b * 2 + (w + 1))
                sp.wait_ge(part_ready[1], b * 2 + (w + 1))
                sp.dma_start(parts_dram[w, u].rearrange("k (c p) s -> p k c s", p=P), parts[:, w]).then_inc(parts_written, 16)
                sp.wait_ge(parts_written, (b * 2 + (w + 1)) * 16)
                for j, pair in enumerate(PAIRS):
                    sp.dma_start(stacked[w][u][CH * j:CH * (j + 1)], parts_dram[w, u, pair[w]].rearrange("(h d) s -> d h s", d=CH))\
                        .then_inc(stacked_ready[w][u], 16)
                if w == 1:
                    sp.wait_ge(cleared, 2)
                sp.dma_start(stacked[w][u][MASK_ROW:MAX_ROW],
                             mask_dram[w, b].unsqueeze(1).broadcast_to([len(PAIRS), H, POS])).then_inc(stacked_ready[w][u], 16)

            sp.wait_ge(mask_split, 7)
            for w in range(2):
                for j, pair in enumerate(PAIRS):
                    sp.dma_start(mask_dram[w, :, j, :], mask_parts[:, w, pair[w], :]).then_inc(mask_written, 16)
            sp.wait_ge(mask_written, 16 * 2 * len(PAIRS))
            load(0, 0)
            stack(0, 0, 0)
            stack(1, 0, 0)
            load(1, 1)

            def turn_of(b, u, count):
                for w in range(2):
                    stack(w, b + 1, 1 - u)
                store(b, u)
                load(b + 2, u)

            with sp.Fori(0, TURNS - 1) as turn:
                for u in range(2):
                    turn_of(turn * 2 + u, u, turn)
            for w in range(2):
                stack(w, B - 1, 1)
            store(B - 2, 0)
            store(B - 1, 1)
            for u in range(2):
                sp.wait_ge(norm.stored[u], 16 * TURNS + 1)

        @block.gpsimd
        def _(pool):
            for u in range(2):
                pool.memset(stacked[1][u][MASK_ROW:ROWS], 1.0).then_inc(cleared, 1)
            for u in range(2):
                pool.wait_ge(cleared, 2 + 2 * u)
                pool.memset(v[:, u, :, :, CH:2 * CH], 0.0).then_inc(cleared, 1)
                pool.wait_ge(cleared, 3 + 2 * u)
                pool.memset(v[:, u, :, :, CH:CH + 1], 1.0).then_inc(cleared, 1)
            with pool.Fori(0, TURNS) as turn:
                for u in range(2):
                    norm_pool(core, norm, turn, u, NORM_STEPS)

        @block.scalar
        def _(act):
            act.wait_ge(cleared, 6)
            act.wait_ge(constants_loaded, CONSTANTS)

            def run(steps, at, b, u):
                for kind, n in steps:
                    if kind == "exp":
                        if n >= 8:
                            c, s = divmod((n - 8) // 4, PT)
                            if s == PT - 1:
                                at.wait_full(act, f"context{c}")
                            else:
                                act.wait_ge(context_done, b * (4 * (PT - 1)) + (c * (PT - 1) + s + 1))
                        at.wait_full(act, f"exp{n}")
                        act.activation(probs[:, n % 8, :], psum[at.bank(f"exp{n}")], ACT.Exp, scale=SCALE)\
                            .then_inc(free[at.bank(f"exp{n}")], 1)
                    if kind in ("shift", "shift'"):
                        owner, to = (b, u) if kind == "shift" else (b + 1, 1 - u)
                        use = f"{kind}{n}"
                        at.wait_full(act, use)
                        act.copy(max_rows[:, n % 2, :], psum[7].bitcast(BF16)[0:PARTS * 4, 0:POS]).then_inc(free[7], 1)
                        at.wait_free(act, use)
                        for k in range(PARTS):
                            act.dma_start(stacked[0][to][MAX_ROW + k:MAX_ROW + k + 1, 4 * n:4 * n + 4, :],
                                          max_rows[4 * k:4 * k + 4, n % 2, :]).then_inc(shift_ready[n % 2], 16)
                    if kind in ("project q", "project k") and n in (1, 3):
                        w, part = "qk".index(kind[-1]), n // 2
                        if part == 0:
                            at.wait_free(act, f"{kind}0")
                        else:
                            act.wait_ge(rest_ready, (b + 1) * 2 + (w + 1))
                        act.copy(parts[:, w, part], (whole, rest)[part][:, :, :]).then_inc(part_ready[part], 1)
                    if kind == "project v":
                        at.wait_free(act, "project v0")
                        for s in range(PT):
                            ins = act.activation(v[:, 1 - u, s, :, 0:CH], v_biased[:, s // 2, s % 2, :].rearrange("p (h d) -> p h d", h=H),
                                                 ACT.Copy, scale=source_mask[:, b + 1, s:s + 1])
                        ins.then_inc(v_ready, 1)
                    if kind == "context" and n % 4 == 3:
                        c = n // 4
                        at.wait_full(act, f"context{c}")
                        act.copy(heads_out[:, c % 2, :], psum[6]).then_inc(free[6], 1)

            every_sequence(act, run)

        @block.vector
        def _(dve):
            dve.wait_ge(masks_loaded, 16)
            dve.tensor_scalar(mask_rest[:, 0, 0], mask_rows[:, :], NEG / SCALE, None, ALU.mult).then_inc(mask_split, 1)
            dve.tensor_scalar(mask_rest[:, 1, 0], mask_rows[:, :], 1.0, None, ALU.subtract).then_inc(mask_split, 1)
            for k in range(PARTS):
                dve.wait_ge(mask_split, 2 + 2 * k)
                dve.tensor_copy(mask_parts[:, :, k, :], mask_rest[:, :, k % 2, :]).then_inc(mask_split, 1)
                if k < PARTS - 1:
                    dve.wait_ge(mask_split, 3 + 2 * k)
                    dve.tensor_tensor(mask_rest[:, :, 1 - k % 2, :], mask_rest[:, :, k % 2, :], mask_parts[:, :, k, :], ALU.subtract)\
                        .then_inc(mask_split, 1)
            dve.wait_ge(constants_loaded, CONSTANTS)

            def run(steps, at, b, u):
                nb = b + 1
                for kind, n in steps:
                    if kind in ("score", "score'"):
                        use, h, c = f"{kind}{n}", n // 2, n // 8
                        at.wait_full(dve, use)
                        dve.tensor_reduce(minus_max[:, c % 2, h % 4, 2 * (n % 2):2 * (n % 2) + 2], at.pair(use), AX.X, ALU.max, negate=True)\
                            .then_inc(free[at.bank(use)], 1)
                    if kind in ("shift", "shift'"):
                        owner = b if kind == "shift" else nb
                        s = (owner * 4 + n) * 4
                        by_tile = minus_max[:, n % 2].rearrange("p h t -> p t h")
                        at.wait_free(dve, (f"score{8 * n + 7}" if kind == "shift" and 8 * n + 7 >= 11 else f"score'{7}"))
                        dve.tensor_copy(max_parts[:, :, 0, :], by_tile).then_inc(max_steps, 1)
                        dve.wait_ge(max_steps, s + 1)
                        dve.tensor_tensor(max_rest[:, :, :], by_tile, max_parts[:, :, 0, :], ALU.subtract).then_inc(max_steps, 1)
                        dve.wait_ge(max_steps, s + 2)
                        dve.tensor_copy(max_parts[:, :, 1, :], max_rest[:, :, :]).then_inc(max_steps, 1)
                        dve.wait_ge(max_steps, s + 3)
                        dve.tensor_tensor(max_parts[:, :, 2, :], max_rest[:, :, :], max_parts[:, :, 1, :], ALU.subtract).then_inc(max_steps, 1)
                    if kind in ("project q", "project k"):
                        w = "qk".index(kind[-1])
                        count = nb * 2 + (w + 1)
                        if n == 0:
                            use = f"{kind}0"
                            at.wait_full(dve, use)
                            dve.wait_ge(context_loaded[1 - u], (nb_turns(at, nb)) * 32)
                            for m in range(TT):
                                ins = dve.scalar_tensor_tensor(out=whole[:, m, :], in0=at.pair(use)[:, m, :],
                                                               scalar=(b_q, b_k)[w][:, m:m + 1], in1=target_mask[:, 1 - u, :],
                                                               op0=ALU.add, op1=ALU.mult)
                            ins.then_inc(free[at.bank(use)], 1)
                        if n == 2:
                            dve.wait_ge(part_ready[0], count)
                            dve.tensor_tensor(rest[:, :, :], whole[:, :, :], parts[:, w, 0], ALU.subtract).then_inc(rest_ready, 1)
                        if n == 4:
                            dve.wait_ge(part_ready[1], count)
                            dve.tensor_tensor(parts[:, w, 2], rest[:, :, :], parts[:, w, 1], ALU.subtract).then_inc(part_ready[2], 1)
                            dve.wait_ge(part_ready[2], count)
                    if kind == "project v":
                        use = "project v0"
                        at.wait_full(dve, use)
                        for k in range(2):
                            ins = dve.tensor_tensor(v_biased[:, k], at.pair(use)[:, k, :].rearrange("p (s n) -> p s n", s=2), b_v[:, :, :], ALU.add)
                        ins.then_inc(free[at.bank(use)], 1)
                    if kind == "finish":
                        s = (b * 2 + n) * 2
                        at.wait_full(dve, f"sum{n}")
                        dve.reciprocal(inverse[:, :], psum[7]).then_inc(free[7], 1)
                        use = f"y{n}"
                        at.wait_full(dve, use)
                        at.wait_free(dve, f"sum{n}")
                        dve.tensor_tensor(scaled[:, :], psum[at.bank(use)], inverse[:, :], ALU.mult).then_inc(free[at.bank(use)], 1)
                        at.wait_free(dve, use)
                        dve.tensor_tensor(masked[:, :], scaled[:, :], target_mask[:, u, :], ALU.mult).then_inc(finish_steps, 1)
                        dve.wait_ge(finish_steps, b * 2 + (n + 1))
                        if n == 0:
                            dve.wait_ge(norm.stored[u], stored_before(at, b))
                        dve.tensor_tensor(norm.z[:, u, n, :], masked[:, :], norm.x[:, u, n, :], ALU.add).then_inc(finish_z, 1)
                        dve.wait_ge(finish_z, b * 2 + (n + 1))
                        dve.bn_stats(norm.stats[:, n, :], norm.z[:, u, n, :]).then_inc(norm.moved, 1)
                        if n == 1:
                            m = b * NORM_STEPS
                            dve.wait_ge(norm.moved, m + 2)
                            dve.memset(norm.vareps[:, :], EPS).then_inc(norm.moved, 1)
                            for t in range(TT):
                                ins = dve.bn_aggr(norm.moments[:, t, :], norm.stats[:, t, :])
                            ins.then_inc(norm.moved, 1)
                            dve.wait_ge(norm.moved, m + 4)
                            dve.tensor_scalar(norm.vareps[:, :], norm.moments[:, :, 1], EPS, None, ALU.add).then_inc(norm.moved, 1)
                            for t in range(TT):
                                dve.wait_ge(norm.rstd_ready, b + 1)
                                dve.tensor_scalar(norm.z[:, u, t, :], norm.z[:, u, t, :], norm.moments[:, t, 0:1], norm.rstd[:, t:t + 1],
                                                  ALU.subtract, ALU.mult).then_inc(norm.out_ready, 1)

            def nb_turns(at, nb):
                if isinstance(nb, int):
                    return nb // 2 + 1
                return at.turn + (1 if at.u == 0 else 2)

            def stored_before(at, b):
                return (b // 2 if isinstance(b, int) else at.turn) * 16 + 1

            every_sequence(dve, run)

        @block.tensor
        def _(pe):
            pe.wait_ge(constants_loaded, CONSTANTS)
            pe.wait_ge(cleared, 6)

            def parity_count(at, b, ahead):
                if isinstance(b, int):
                    return (b + ahead) // 2 + 1
                return at.turn + (1 if at.u + ahead < 2 else 2)

            def run(steps, at, b, u):
                nb = b + 1
                for kind, n in steps:
                    if kind in ("score", "score'"):
                        use, h = f"{kind}{n}", n // 2
                        ahead = 1 if kind == "score'" else 0
                        to = u ^ ahead
                        at.wait_bank(pe, use)
                        if n == 0:
                            for w in range(2):
                                pe.wait_ge(stacked_ready[w][to], parity_count(at, b, ahead) * 7 * 16)
                        for k in range(2):
                            t = 2 * (n % 2) + k
                            ins = pe.matmul(at.pair(use)[:, k, :], stacked[0][to][0:MAX_ROW, h, t * P:(t + 1) * P],
                                            stacked[1][to][0:MAX_ROW, h, :], start=True, stop=True)
                        ins.then_inc(full[at.bank(use)], 1)
                    if kind in ("shift", "shift'"):
                        owner = b if kind == "shift" else nb
                        use = f"{kind}{n}"
                        at.wait_bank(pe, use)
                        pe.wait_ge(max_steps, (owner * 4 + (n + 1)) * 4)
                        for t in range(PT):
                            ins = pe.transpose(psum[7].bitcast(BF16)[0:PARTS * 4, t * P:(t + 1) * P],
                                               max_parts[:, t].rearrange("p k h -> p (k h)"), core.ident_bf[:, :])
                        ins.then_inc(full[7], 1)
                    if kind == "exp":
                        use, c, s, h = f"exp{n}", n // 16, n % 16 // 4, n // 16 * 4 + n % 4
                        at.wait_bank(pe, use)
                        if n % 16 == 0:
                            pe.wait_ge(shift_ready[c % 2], (b * 2 + (c // 2 + 1)) * PARTS * 16)
                        ins = pe.matmul(psum[at.bank(use)], stacked[1][u][:, h, s * P:(s + 1) * P], stacked[0][u][:, h, :], start=True, stop=True)
                        ins.then_inc(full[at.bank(use)], 1)
                    if kind == "context":
                        c, s = n // 4, n % 4
                        if s == 0:
                            at.wait_bank(pe, f"context{c}")
                        if n == 0:
                            pe.wait_ge(v_ready, b + 1)
                        for i in (2, 3):
                            at.wait_free(pe, f"exp{4 * n + i}")
                        for i in range(4):
                            ins = pe.matmul(psum[6][32 * i:32 * i + 32, :], v[:, u, s, 4 * c + i, :], probs[:, (4 * n + i) % 8, :],
                                            start=s == 0, stop=s == PT - 1)
                        ins.then_inc(full[6] if s == PT - 1 else context_done, 1)
                    if kind in ("project q", "project k") and n == 0:
                        w, use = "qk".index(kind[-1]), f"{kind}0"
                        at.wait_bank(pe, use)
                        if w == 0:
                            pe.wait_ge(norm.loaded[1 - u], parity_count(at, b, 1) * 16)
                        else:
                            pe.wait_ge(context_loaded[1 - u], parity_count(at, b, 1) * 32)
                        src = (norm.x, context)[w]
                        for m in range(TT):
                            for c in range(TT):
                                ins = pe.matmul(at.pair(use)[:, m, :], (w_q, w_k)[w][:, c, m * P:(m + 1) * P], src[:, 1 - u, c, :],
                                                start=c == 0, stop=c == TT - 1)
                        ins.then_inc(full[at.bank(use)], 1)
                    if kind == "project v":
                        use = "project v0"
                        at.wait_bank(pe, use)
                        for s in range(PT):
                            for c in range(TT):
                                ins = pe.matmul(at.pair(use)[:, s // 2, s % 2 * SIZE:(s % 2 + 1) * SIZE], context[:, 1 - u, c, s * P:(s + 1) * P],
                                                w_v[:, c, :], start=c == 0, stop=c == TT - 1)
                        ins.then_inc(full[at.bank(use)], 1)
                    if kind == "finish":
                        at.wait_bank(pe, f"sum{n}")
                        at.wait_free(pe, f"context{2 * n + 1}")
                        for half in range(2):
                            ins = pe.matmul(psum[7], gather[:, 2 + half, :], heads_out[:, half, :], start=half == 0, stop=half == 1)
                        ins.then_inc(full[7], 1)
                        at.wait_bank(pe, f"y{n}")
                        for half in range(2):
                            ins = pe.matmul(psum[at.bank(f"y{n}")], gather[:, half, :], heads_out[:, half, :], start=half == 0, stop=half == 1)
                        ins.then_inc(full[at.bank(f"y{n}")], 1)

            every_sequence(pe, run)



E = 8
RL = 8
F0 = 1376
FT = -(-F0 // P)
NL = (E + 1) * RL
NLP = 96
AHEAD = 3


def ffn0_layout(inputs):
    import numpy as np

    def tall(name):
        a = np.asarray(inputs[f"L0_ffn_A_{name}"])
        return np.concatenate([a.transpose(1, 0, 2).reshape(a.shape[1], E * RL),
                               np.asarray(inputs[f"L0_ffn_sA_{name}"])], axis=1)

    def wide(name):
        b = np.asarray(inputs[f"L0_ffn_B_{name}"])
        whole = np.zeros((NLP, b.shape[2]), b.dtype)
        whole[0:E * RL] = b.reshape(E * RL, b.shape[2])
        whole[E * RL:NL] = np.asarray(inputs[f"L0_ffn_sB_{name}"])
        return whole

    down = np.zeros((F0, NLP), np.asarray(inputs["L0_ffn_A_down"]).dtype)
    down[:, 0:NL] = tall("down")
    return {
        "first": np.concatenate([tall("gate"), tall("up"), np.asarray(inputs["L0_ffn_W_router"])], axis=1),
        "gate": np.asarray(inputs["L0_ffn_W_gate"]), "up": np.asarray(inputs["L0_ffn_W_up"]),
        "down": np.asarray(inputs["L0_ffn_W_down"]), "B_gate": wide("gate"), "B_up": wide("up"),
        "A_down": down, "B_down": wide("down"), "bias": np.asarray(inputs["L0_ffn_expert_bias"]),
    }


def feed_forward_lora(core, name, x_src, x_dst, weights):
    nc = core.nc
    FIRST = 2 * NL + E
    ring = [6, 7, 0, 3, 1, 2, 4, 5, 6, 7, 0]
    turn_uses = []
    for u in range(2):
        turn_uses += [(f"xT0.{u}", 0), (f"xT1.{u}", 3), (f"low.{u}", 4)]
        turn_uses += [(f"h{j}.{u}", ring[j]) for j in range(AHEAD)]
        turn_uses += [(f"lowT.{u}", 5)]
        turn_uses += [(f"h{j}.{u}", ring[j]) for j in range(AHEAD, FT)]
        turn_uses += [(f"hA.{u}", 3), (f"hAT.{u}", 4), (f"y0.{u}", 1), (f"y1.{u}", 2)]
    uses = BankUses(core.uses, turn_uses, TURNS)
    core.uses = uses.after
    full, free, psum = core.bank_full, core.bank_free, core.psum

    with ExitStack() as ctx:
        core.ctx_stage = ctx

        def sb(tag, shape, dtype=F32):
            return ctx.enter_context(nc.sbuf_tensor(f"{name}_{tag}", shape, dtype))

        def sem(tag):
            return core.ctx.enter_context(nc.semaphore(f"{name}_{tag}"))

        norm = Norm(core, name)
        w_first = sb("w_first", [P, KC, FIRST])
        w_gate = sb("w_gate", [P, KC, F0])
        w_up = sb("w_up", [P, KC, F0])
        w_down = sb("w_down", [P, FT, D])
        b_gate = sb("b_gate", [NLP, F0])
        b_up = sb("b_up", [NLP, F0])
        b_down = sb("b_down", [NLP, D])
        a_down = sb("a_down", [P, FT, NLP])
        bias = sb("bias", [P, E])
        order = sb("order", [P, E])
        xT = sb("xT", [P, KC, T])
        scores = sb("scores", [P, TT, E])
        biased = sb("biased", [P, TT, E])
        rank = sb("rank", [P, TT, E])
        top = sb("top", [P, TT])
        chosen = sb("chosen", [P, 2, TT, E])
        share = sb("share", [P, TT, E])
        total = sb("total", [P, TT])
        low = sb("low", [P, TT, 2, NLP])
        lowT = sb("lowT", [NLP, 2, T])
        silu = sb("silu", [P, 3, T])
        hT = sb("hT", [P, FT, T])
        hA = sb("hA", [P, TT, NLP])
        hAT = sb("hAT", [NLP, T])
        first_loaded = sem("first_loaded")
        hidden_loaded = [sem(f"hidden_loaded{k}") for k in range(3)]
        down_loaded = sem("down_loaded")
        padded = sem("padded")
        scored = sem("scored")
        routed = sem("routed")
        silu_ready = sem("silu_ready")
        ROUTE = 19
        SPLIT = [0, 4 * P, 8 * P, F0]
        whole = (FT - 1) * P

        def wait_bank(engine, use, turn):
            engine.wait_ge(free[uses.bank(use)], uses.before(use, turn) + 1)

        def wait_full(engine, use, turn):
            engine.wait_ge(full[uses.bank(use)], uses.before(use, turn) + 1)

        def wait_free(engine, use, turn):
            engine.wait_ge(free[uses.bank(use)], uses.before(use, turn) + 2)

        def width(j):
            return P if j < FT - 1 else F0 - whole

        block = ctx.enter_context(nc.Block())

        @block.sync
        def _(sp):
            rows_in_and_out(core, norm, uses, x_src, x_dst)

        @block.gpsimd
        def _(pool):
            pool.memset(low[:, :, :, :], 0.0).then_inc(padded, 1)
            pool.memset(hA[:, :, :], 0.0).then_inc(padded, 1)
            pool.iota(order[:, :], pattern=[[-1, E]], base=E, channel_multiplier=0,
                      allow_small_or_imprecise_dtypes=True).then_inc(padded, 1)
            with pool.Fori(0, TURNS) as turn:
                for u in range(2):
                    norm_pool(core, norm, turn, u)

        @block.scalar
        def _(act):
            act.dma_start(w_first[:, :, :], weights["first"].rearrange("(c p) n -> p c n", p=P)).then_inc(first_loaded, 16)
            act.dma_start(bias[:, :], weights["bias"].rearrange("(a e) -> a e", a=1).broadcast_to([P, E])).then_inc(first_loaded, 16)
            for k in range(3):
                cols = slice(SPLIT[k], SPLIT[k + 1])
                for key, w in (("gate", w_gate), ("up", w_up)):
                    act.dma_start(w[:, :, cols], weights[key].rearrange("(c p) n -> p c n", p=P)[:, :, cols]).then_inc(hidden_loaded[k], 16)
                for key, w in (("B_gate", b_gate), ("B_up", b_up)):
                    act.dma_start(w[:, cols], weights[key][:, cols]).then_inc(hidden_loaded[k], 16)
            act.dma_start(a_down[:, 0:FT - 1, :], weights["A_down"][0:whole].rearrange("(c p) n -> p c n", p=P)).then_inc(down_loaded, 16)
            act.dma_start(a_down[0:F0 - whole, FT - 1, :], weights["A_down"][whole:F0]).then_inc(down_loaded, 16)
            act.dma_start(w_down[:, 0:FT - 1, :], weights["down"][0:whole].rearrange("(c p) n -> p c n", p=P)).then_inc(down_loaded, 16)
            act.dma_start(w_down[0:F0 - whole, FT - 1, :], weights["down"][whole:F0]).then_inc(down_loaded, 16)
            act.dma_start(b_down[:, :], weights["B_down"]).then_inc(down_loaded, 16)
            with act.Fori(0, TURNS) as turn:
                for u in range(2):
                    for j in range(2):
                        use = f"xT{j}.{u}"
                        wait_full(act, use, turn)
                        act.copy(xT[:, 2 * j:2 * j + 2, :], psum[uses.bank(use)][:, :].rearrange("p (c t) -> p c t", c=2))\
                            .then_inc(free[uses.bank(use)], 1)
                    wait_full(act, f"low.{u}", turn)
                    act.activation(scores[:, :, :],
                                   psum[uses.bank(f"low.{u}")][:, :].rearrange("p (t n) -> p t n", t=TT)[:, :, 2 * NL:FIRST],
                                   ACT.Sigmoid).then_inc(scored, 1)
                    use = f"lowT.{u}"
                    wait_full(act, use, turn)
                    act.copy(lowT[:, :, :], psum[uses.bank(use)][0:NLP, :].rearrange("p (g t) -> p g t", g=2))\
                        .then_inc(free[uses.bank(use)], 1)
                    for j in range(FT):
                        use, m = f"h{j}.{u}", width(j)
                        wait_full(act, use, turn)
                        if j >= 3:
                            wait_free(act, f"h{j - 3}.{u}", turn)
                        act.activation(silu[0:m, j % 3, :], psum[uses.bank(use)][0:m, 0:T], ACT.Silu).then_inc(silu_ready, 1)
                    use = f"hAT.{u}"
                    wait_full(act, use, turn)
                    act.copy(hAT[:, :], psum[uses.bank(use)][0:NLP, 0:T]).then_inc(free[uses.bank(use)], 1)

        @block.vector
        def _(dve):
            dve.wait_ge(padded, 3)
            dve.wait_ge(first_loaded, 32)
            with dve.Fori(0, TURNS) as turn:
                for u in range(2):
                    b = turn * 2 + u

                    def step(ins, n):
                        ins.then_inc(routed, 1)
                        if n < ROUTE:
                            dve.wait_ge(routed, b * ROUTE + n)

                    def per_row(a):
                        return a.unsqueeze(2).broadcast_to([P, TT, E])

                    dve.wait_ge(scored, b + 1)
                    step(dve.tensor_tensor(biased[:, :, :], scores[:, :, :],
                                           bias[:, :].unsqueeze(1).broadcast_to([P, TT, E]), ALU.add), 1)
                    for k in range(2):
                        s = 1 + 6 * k
                        step(dve.tensor_reduce(top[:, :], biased[:, :, :], AX.X, ALU.max), s + 1)
                        step(dve.tensor_tensor(rank[:, :, :], biased[:, :, :], per_row(top[:, :]), ALU.is_equal), s + 2)
                        step(dve.tensor_tensor(rank[:, :, :], rank[:, :, :],
                                               order[:, :].unsqueeze(1).broadcast_to([P, TT, E]), ALU.mult), s + 3)
                        step(dve.tensor_reduce(top[:, :], rank[:, :, :], AX.X, ALU.max), s + 4)
                        step(dve.tensor_tensor(chosen[:, k], rank[:, :, :], per_row(top[:, :]), ALU.is_equal), s + 5)
                        if k == 0:
                            step(dve.scalar_tensor_tensor(out=biased[:, :, :], in0=chosen[:, 0], scalar=-1e30,
                                                          in1=biased[:, :, :], op0=ALU.mult, op1=ALU.add), s + 6)
                        else:
                            step(dve.tensor_tensor(share[:, :, :], chosen[:, 0], chosen[:, 1], ALU.add), s + 6)
                    step(dve.tensor_tensor(share[:, :, :], share[:, :, :], scores[:, :, :], ALU.mult), 14)
                    step(dve.tensor_reduce(total[:, :], share[:, :, :], AX.X, ALU.add), 15)
                    step(dve.tensor_scalar(total[:, :], total[:, :], 1e-8, float(RL), ALU.add, ALU.mult), 16)
                    step(dve.reciprocal(total[:, :], total[:, :]), 17)
                    step(dve.tensor_tensor(share[:, :, :], share[:, :, :], per_row(total[:, :]), ALU.mult), 18)
                    use = f"low.{u}"
                    bank = psum[uses.bank(use)]
                    wait_full(dve, use, turn)
                    for t in range(TT):
                        dve.tensor_tensor(low[:, t, :, 0:E * RL].rearrange("p g (e r) -> p g e r", r=RL),
                                          bank[:, t * T:t * T + 2 * NL].rearrange("p (g n) -> p g n", g=2)[:, :, 0:E * RL]
                                          .rearrange("p g (e r) -> p g e r", r=RL),
                                          share[:, t, :].unsqueeze(1).unsqueeze(3).broadcast_to([P, 2, E, RL]), ALU.mult)
                        ins = dve.tensor_scalar(low[:, t, :, E * RL:NL],
                                                bank[:, t * T:t * T + 2 * NL].rearrange("p (g n) -> p g n", g=2)[:, :, E * RL:NL],
                                                1.0 / RL, None, ALU.mult)
                        if t == 0:
                            step(ins, ROUTE)
                    ins.then_inc(free[uses.bank(use)], 1)
                    for j in range(FT):
                        use, m = f"h{j}.{u}", width(j)
                        dve.wait_ge(silu_ready, b * FT + (j + 1))
                        dve.tensor_tensor(hT[0:m, j, :], psum[uses.bank(use)][0:m, T:2 * T], silu[0:m, j % 3, :], ALU.mult)\
                            .then_inc(free[uses.bank(use)], 1)
                    use = f"hA.{u}"
                    wait_full(dve, use, turn)
                    bank = psum[uses.bank(use)][:, 0:TT * NLP].rearrange("p (t n) -> p t n", t=TT)
                    dve.tensor_tensor(hA[:, :, 0:E * RL].rearrange("p t (e r) -> p t e r", r=RL),
                                      bank[:, :, 0:E * RL].rearrange("p t (e r) -> p t e r", r=RL),
                                      share[:, :, :].unsqueeze(3).broadcast_to([P, TT, E, RL]), ALU.mult)
                    dve.tensor_scalar(hA[:, :, E * RL:NL], bank[:, :, E * RL:NL], 1.0 / RL, None, ALU.mult)\
                        .then_inc(free[uses.bank(use)], 1)
                    norm_dve(core, norm, uses, turn, u)

        @block.tensor
        def _(pe):
            pe.wait_ge(first_loaded, 32)
            with pe.Fori(0, TURNS) as turn:
                for u in range(2):
                    def done(ins, use):
                        ins.then_inc(full[uses.bank(use)], 1)

                    pe.wait_ge(norm.loaded[u], turn * 16 + 16)
                    for j in range(2):
                        use = f"xT{j}.{u}"
                        wait_bank(pe, use, turn)
                        for c in range(2):
                            for t in range(TT):
                                d = 2 * j + c
                                ins = pe.transpose(psum[uses.bank(use)][:, (c * TT + t) * P:(c * TT + t + 1) * P],
                                                   norm.x[:, u, t, d * P:(d + 1) * P], core.ident[:, :])
                        done(ins, use)
                    for j in range(2):
                        wait_free(pe, f"xT{j}.{u}", turn)
                    use = f"low.{u}"
                    wait_bank(pe, use, turn)
                    for t in range(TT):
                        for c in range(KC):
                            ins = pe.matmul(psum[uses.bank(use)][:, t * T:t * T + FIRST], xT[:, c, t * P:(t + 1) * P],
                                            w_first[:, c, :], start=c == 0, stop=c == KC - 1)
                    done(ins, use)

                    def dense(j):
                        use, m = f"h{j}.{u}", width(j)
                        if j in (0, 4, 8):
                            pe.wait_ge(hidden_loaded[j // 4], 64)
                        wait_bank(pe, use, turn)
                        for g, w in enumerate((w_gate, w_up)):
                            for c in range(KC):
                                pe.matmul(psum[uses.bank(use)][0:m, g * T:(g + 1) * T], w[:, c, j * P:j * P + m], xT[:, c, :],
                                          start=g == 0 and c == 0, stop=False, skip_group_check=True)

                    def low_rank(j):
                        use, m = f"h{j}.{u}", width(j)
                        for g, w in enumerate((b_gate, b_up)):
                            ins = pe.matmul(psum[uses.bank(use)][0:m, g * T:(g + 1) * T], w[:, j * P:j * P + m], lowT[:, g, :],
                                            start=False, stop=True, skip_group_check=True)
                        done(ins, use)

                    for j in range(AHEAD):
                        dense(j)
                    use = f"lowT.{u}"
                    wait_bank(pe, use, turn)
                    wait_free(pe, f"low.{u}", turn)
                    for g in range(2):
                        for t in range(TT):
                            ins = pe.transpose(psum[uses.bank(use)][0:NLP, g * T + t * P:g * T + (t + 1) * P], low[:, t, g, :], core.ident[:, :])
                    done(ins, use)
                    wait_free(pe, use, turn)
                    for j in range(AHEAD):
                        low_rank(j)
                    for j in range(AHEAD, FT):
                        dense(j)
                        low_rank(j)
                    use = f"hA.{u}"
                    wait_bank(pe, use, turn)
                    pe.wait_ge(down_loaded, 80)
                    wait_free(pe, f"h{FT - 1}.{u}", turn)
                    for t in range(TT):
                        for j in range(FT):
                            m = width(j)
                            ins = pe.matmul(psum[uses.bank(use)][:, t * NLP:(t + 1) * NLP], hT[0:m, j, t * P:(t + 1) * P],
                                            a_down[0:m, j, :], start=j == 0, stop=j == FT - 1)
                    done(ins, use)
                    for t in range(TT):
                        use = f"y{t}.{u}"
                        if t == 0:
                            wait_bank(pe, "hAT." + str(u), turn)
                        wait_bank(pe, use, turn)
                        for j in range(FT):
                            m = width(j)
                            pe.matmul(psum[uses.bank(use)][:, :], hT[0:m, j, t * P:(t + 1) * P], w_down[0:m, j, :],
                                      start=j == 0, stop=False, skip_group_check=True)
                        if t == 0:
                            wait_free(pe, f"hA.{u}", turn)
                            for k in range(TT):
                                ins = pe.transpose(psum[uses.bank(f"hAT.{u}")][0:NLP, k * P:(k + 1) * P], hA[:, k, :], core.ident[:, :])
                            done(ins, f"hAT.{u}")
                            wait_free(pe, f"hAT.{u}", turn)
                        ins = pe.matmul(psum[uses.bank(use)][:, :], hAT[:, t * P:(t + 1) * P], b_down[:, :], start=False, stop=True,
                                        skip_group_check=True)
                        done(ins, use)



HD = 128
G = 4
HG = H // G
S1 = 256
QUEUE = 3


def cross_attention_grouped(core, name, x_src, ctxT_src, x_dst, weights):
    nc = core.nc
    turn_uses = []
    for u in range(2):
        turn_uses += [(f"xT0.{u}", 0), (f"xT1.{u}", 1), (f"q0_0.{u}", 2), (f"q0_1.{u}", 3), (f"k0.{u}", 4), (f"k1.{u}", 5),
                      (f"v0.{u}", 6), (f"v1.{u}", 7), (f"kT0.{u}", 4), (f"kT1.{u}", 5), (f"qT0_0.{u}", 0), (f"qT0_1.{u}", 1)]
        for s in range(H + 2):
            if s < H:
                turn_uses.append((f"S{s}.{u}", 2 + s % 2))
                if s < H - HG:
                    turn_uses.append(((f"q{s // HG + 1}_{s % HG}.{u}", s % HG) if s % HG < 2
                                      else (f"qT{s // HG + 1}_{s % HG - 2}.{u}", s % HG - 2)))
            if 1 <= s <= H:
                turn_uses.append((f"T{s - 1}.{u}", 4 + (s - 1) % 2))
            if s >= 2:
                turn_uses += [(f"R{s - 2}.{u}", 7), (f"O{s - 2}.{u}", 6)]
        turn_uses += [(f"y0.{u}", 2), (f"y1.{u}", 3)]
    uses = BankUses(core.uses, turn_uses, TURNS)
    core.uses = uses.after
    full, free, psum = core.bank_full, core.bank_free, core.psum

    with ExitStack() as ctx:
        core.ctx_stage = ctx

        def sb(tag, shape, dtype=F32):
            return ctx.enter_context(nc.sbuf_tensor(f"{name}_{tag}", shape, dtype))

        def sem(tag):
            return core.ctx.enter_context(nc.semaphore(f"{name}_{tag}"))

        norm = Norm(core, name)
        w_q = sb("w_q", [P, KC, H * HD])
        w_k = sb("w_k", [P, KC, G * HD])
        w_v = sb("w_v", [P, KC, G * HD])
        w_o = sb("w_o", [P, H, D])
        gains = sb("gains", [P, 2])
        gain = sb("gain", [P, 1])
        context = sb("context", [P, 2, KC, S1])
        xT = sb("xT", [P, KC, T])
        squares = sb("squares", [P, QUEUE, 512])
        square_sums = sb("square_sums", [P, 5, HG, TT])
        mean_squares = sb("mean_squares", [P, 5, HG, TT])
        rroot = sb("rroot", [P, 5, HG, TT])
        q_rows = sb("q_rows", [P, 2, TT, HG * HD])
        qT = sb("qT", [P, 2, HG, T])
        k_rows = sb("k_rows", [P, TT, G * HD])
        kT = sb("kT", [P, G, S1])
        v = sb("v", [P, TT, G * HD])
        row_max = sb("row_max", [P, H, TT])
        minus_max = sb("minus_max", [P, H, TT])
        probs = sb("probs", [P, QUEUE, TT, S1])
        probsT = sb("probsT", [P, QUEUE, TT, T])
        sums = sb("sums", [P, H, TT])
        inverse = sb("inverse", [P, H, TT])
        inverse_rows = sb("inverse_rows", [P, QUEUE, TT, P])
        spread = sb("spread", [P, 2, T])
        ctxT = sb("ctxT", [P, H, T])
        q_weights = [sem(f"q_weights{k}") for k in range(2)]
        kv_weights = sem("kv_weights")
        o_weights = sem("o_weights")
        gain_ready = sem("gain_ready")
        context_loaded = [sem(f"context_loaded{u}") for u in range(2)]
        squared = sem("squared")
        summed = sem("summed")
        mean_ready = sem("mean_ready")
        rroot_ready = sem("rroot_ready")
        max_found = sem("max_found")
        max_ready = sem("max_ready")
        inverted = sem("inverted")
        inverse_spread = sem("inverse_spread")

        def wait_bank(engine, use, turn):
            engine.wait_ge(free[uses.bank(use)], uses.before(use, turn) + 1)

        def wait_full(engine, use, turn):
            engine.wait_ge(full[uses.bank(use)], uses.before(use, turn) + 1)

        def wait_free(engine, use, turn):
            engine.wait_ge(free[uses.bank(use)], uses.before(use, turn) + 2)

        block = ctx.enter_context(nc.Block())

        @block.sync
        def _(sp):
            def load_context(b, u):
                sp.dma_start(context[:, u], ctxT_src[b].rearrange("(c p) s -> p c s", p=P)).then_inc(context_loaded[u], 16)

            rows_in_and_out(core, norm, uses, x_src, x_dst, load_context,
                            lambda turn, u: wait_full(sp, f"v1.{u}", turn))

        @block.gpsimd
        def _(pool):
            with pool.Fori(0, TURNS) as turn:
                for u in range(2):
                    for n, part in enumerate((0, 4, 1, 2, 3)):
                        pool.wait_ge(mean_ready, (turn * 2 + u) * 5 + (n + 1))
                        pool.tensor_tensor(rroot[:, part], mean_squares[:, part],
                                           core.minus_half[:, 0:HG * TT].rearrange("p (h t) -> p h t", t=TT), ALU.pow)\
                            .then_inc(rroot_ready, 1)
                    norm_pool(core, norm, turn, u)

        @block.scalar
        def _(act):
            wq = weights["q"].rearrange("(c p) n -> p c n", p=P)
            act.dma_start(w_q[:, :, 0:512], wq[:, :, 0:512]).then_inc(q_weights[0], 16)
            act.dma_start(gains[:, 0:1], weights["qn"].rearrange("(p a) -> p a", a=1)).then_inc(kv_weights, 16)
            act.dma_start(gains[:, 1:2], weights["kn"].rearrange("(p a) -> p a", a=1)).then_inc(kv_weights, 16)
            act.dma_start(w_k[:, :, :], weights["k"].rearrange("(c p) n -> p c n", p=P)).then_inc(kv_weights, 16)
            act.dma_start(w_v[:, :, :], weights["v"].rearrange("(c p) n -> p c n", p=P)).then_inc(kv_weights, 16)
            act.dma_start(w_q[:, :, 512:], wq[:, :, 512:]).then_inc(q_weights[1], 16)
            act.dma_start(w_o[:, :, :], weights["o"].rearrange("(c p) n -> p c n", p=P)).then_inc(o_weights, 16)
            act.wait_ge(gain_ready, 2)
            with act.Fori(0, TURNS) as turn:
                for u in range(2):
                    b = turn * 2 + u

                    def square(use, n):
                        wait_full(act, use, turn)
                        if n < QUEUE:
                            act.wait_ge(summed, b * 10 + 1)
                        else:
                            act.wait_ge(summed, b * 10 + (n - QUEUE + 2))
                        return act.activation(squares[:, n % QUEUE, :], psum[uses.bank(use)][:, :], ACT.Square).then_inc(squared, 1)

                    def q_out(g, t, n):
                        use = f"q{g}_{t}.{u}"
                        square(use, n)
                        act.copy(q_rows[:, g % 2, t, :], psum[uses.bank(use)][:, :]).then_inc(free[uses.bank(use)], 1)

                    def qT_out(g, j):
                        use = f"qT{g}_{j}.{u}"
                        wait_full(act, use, turn)
                        act.copy(qT[:, g % 2, 2 * j:2 * j + 2, :], psum[uses.bank(use)][:, :].rearrange("p (h t) -> p h t", h=2))\
                            .then_inc(free[uses.bank(use)], 1)

                    for j in range(2):
                        use = f"xT{j}.{u}"
                        wait_full(act, use, turn)
                        act.copy(xT[:, 2 * j:2 * j + 2, :], psum[uses.bank(use)][:, :].rearrange("p (c t) -> p c t", c=2))\
                            .then_inc(free[uses.bank(use)], 1)
                    q_out(0, 0, 0)
                    q_out(0, 1, 1)
                    square(f"k0.{u}", 2)
                    square(f"k1.{u}", 3)
                    for t in range(TT):
                        use = f"v{t}.{u}"
                        wait_full(act, use, turn)
                        act.copy(v[:, t, :], psum[uses.bank(use)][:, :]).then_inc(free[uses.bank(use)], 1)
                    for j in range(2):
                        use = f"kT{j}.{u}"
                        wait_full(act, use, turn)
                        act.activation(kT[:, 2 * j:2 * j + 2, :], psum[uses.bank(use)][:, :].rearrange("p (h t) -> p h t", h=2),
                                       ACT.Copy, scale=gain[:, 0:1]).then_inc(free[uses.bank(use)], 1)
                    for j in range(2):
                        qT_out(0, j)
                    for s in range(H + 2):
                        if s < H:
                            use = f"S{s}.{u}"
                            act.wait_ge(max_ready, b * H + (s + 1))
                            if s >= QUEUE:
                                wait_full(act, f"T{s - QUEUE}.{u}", turn)
                            for t in range(TT):
                                ins = act.activation(probs[:, s % QUEUE, t, :], psum[uses.bank(use)][:, t * S1:(t + 1) * S1], ACT.Exp,
                                                     bias=minus_max[:, s, t:t + 1], scale=rroot[:, s // HG, s % HG, t:t + 1],
                                                     accum_out=sums[:, s, t:t + 1])
                            ins.then_inc(free[uses.bank(use)], 1)
                            if s < H - HG:
                                g, i = s // HG + 1, s % HG
                                if i < 2:
                                    q_out(g, i, 4 + 2 * (g - 1) + i)
                                else:
                                    qT_out(g, i - 2)
                        if s >= 2:
                            use = f"R{s - 2}.{u}"
                            wait_full(act, use, turn)
                            if s >= 4:
                                wait_free(act, f"O{s - 4}.{u}", turn)
                            act.copy(spread[:, s % 2, :], psum[uses.bank(use)][:, 0:T]).then_inc(free[uses.bank(use)], 1)

        @block.vector
        def _(dve):
            dve.sem_inc(summed, 1)
            dve.wait_ge(kv_weights, 64)
            dve.tensor_tensor(gain[:, :], gains[:, 0:1], gains[:, 1:2], ALU.mult).then_inc(gain_ready, 1)
            dve.wait_ge(gain_ready, 1)
            dve.tensor_scalar(gain[:, :], gain[:, :], float(HD) ** -0.5, None, ALU.mult).then_inc(gain_ready, 1)
            with dve.Fori(0, TURNS) as turn:
                for u in range(2):
                    b = turn * 2 + u

                    def sum_squares(part, t, n):
                        dve.wait_ge(squared, b * 10 + (n + 1))
                        dve.tensor_reduce(square_sums[:, part, :, t], squares[:, n % QUEUE, :].rearrange("p (h d) -> p h d", h=HG),
                                          AX.X, ALU.add).then_inc(summed, 1)

                    def mean_square(part, n):
                        dve.wait_ge(summed, b * 10 + n + 1)
                        dve.tensor_scalar(mean_squares[:, part], square_sums[:, part], 1.0 / HD, 1e-6, ALU.mult, ALU.add)\
                            .then_inc(mean_ready, 1)

                    sum_squares(0, 0, 0)
                    sum_squares(0, 1, 1)
                    mean_square(0, 2)
                    sum_squares(4, 0, 2)
                    sum_squares(4, 1, 3)
                    mean_square(4, 4)
                    for t in range(TT):
                        use = f"k{t}.{u}"
                        dve.wait_ge(rroot_ready, b * 5 + 2)
                        dve.tensor_tensor(k_rows[:, t, :].rearrange("p (h d) -> p h d", h=G),
                                          psum[uses.bank(use)][:, :].rearrange("p (h d) -> p h d", h=G),
                                          rroot[:, 4, :, t].unsqueeze(2).broadcast_to([P, G, HD]), ALU.mult)\
                            .then_inc(free[uses.bank(use)], 1)
                    for s in range(H + 2):
                        if s < H:
                            use = f"S{s}.{u}"
                            wait_full(dve, use, turn)
                            dve.tensor_reduce(row_max[:, s, :], psum[uses.bank(use)][:, :].rearrange("p (t s) -> p t s", t=TT),
                                              AX.X, ALU.max).then_inc(max_found, 1)
                            dve.wait_ge(max_found, b * H + (s + 1))
                            if s % HG == 0:
                                g = s // HG
                                dve.wait_ge(rroot_ready, b * 5 + (1 if g == 0 else g + 2))
                            dve.scalar_tensor_tensor(out=minus_max[:, s, :], in0=row_max[:, s, :], scalar=-1.0,
                                                     in1=rroot[:, s // HG, s % HG, :], op0=ALU.mult, op1=ALU.mult)\
                                .then_inc(max_ready, 1)
                            if s < H - HG:
                                g, i = s // HG + 1, s % HG
                                if i < 2:
                                    sum_squares(g, i, 4 + 2 * (g - 1) + i)
                                if i == 2:
                                    mean_square(g, 4 + 2 * g)
                        if 1 <= s <= H:
                            h = s - 1
                            wait_free(dve, f"S{h}.{u}", turn)
                            dve.reciprocal(inverse[:, h, :], sums[:, h, :]).then_inc(inverted, 1)
                            use = f"T{h}.{u}"
                            wait_full(dve, use, turn)
                            if h >= QUEUE:
                                wait_full(dve, f"O{h - QUEUE}.{u}", turn)
                            dve.tensor_copy(probsT[:, h % QUEUE], psum[uses.bank(use)][:, :].rearrange("p (s t) -> p s t", s=TT))\
                                .then_inc(free[uses.bank(use)], 1)
                            dve.wait_ge(inverted, b * H + (h + 1))
                            dve.tensor_copy(inverse_rows[:, h % QUEUE], inverse[:, h, :].unsqueeze(2).broadcast_to([P, TT, P]))\
                                .then_inc(inverse_spread, 1)
                        if s >= 2:
                            use = f"O{s - 2}.{u}"
                            wait_full(dve, use, turn)
                            wait_free(dve, f"R{s - 2}.{u}", turn)
                            dve.tensor_tensor(ctxT[:, s - 2, :], psum[uses.bank(use)][:, 0:T], spread[:, s % 2, :], ALU.mult)\
                                .then_inc(free[uses.bank(use)], 1)
                    norm_dve(core, norm, uses, turn, u)

        @block.tensor
        def _(pe):
            with pe.Fori(0, TURNS) as turn:
                for u in range(2):
                    b = turn * 2 + u

                    def done(ins, use):
                        ins.then_inc(full[uses.bank(use)], 1)

                    def rows(use, left, w, cols):
                        wait_bank(pe, use, turn)
                        for c in range(KC):
                            ins = pe.matmul(psum[uses.bank(use)][:, :], left(c), w[:, c, cols], start=c == 0, stop=c == KC - 1)
                        done(ins, use)

                    def q_group(g, t):
                        if g == 1 and t == 0:
                            pe.wait_ge(q_weights[1], 16)
                        rows(f"q{g}_{t}.{u}", lambda c: xT[:, c, t * P:(t + 1) * P], w_q, slice(g * 512, (g + 1) * 512))

                    def transpose_q(g, j):
                        use = f"qT{g}_{j}.{u}"
                        wait_bank(pe, use, turn)
                        if j == 0:
                            wait_free(pe, f"q{g}_1.{u}", turn)
                        for i in range(2):
                            for t in range(TT):
                                h = 2 * j + i
                                ins = pe.transpose(psum[uses.bank(use)][:, (i * TT + t) * P:(i * TT + t + 1) * P],
                                                   q_rows[:, g % 2, t, h * HD:(h + 1) * HD], core.ident[:, :])
                        done(ins, use)

                    pe.wait_ge(norm.loaded[u], turn * 16 + 16)
                    for j in range(2):
                        use = f"xT{j}.{u}"
                        wait_bank(pe, use, turn)
                        for c in range(2):
                            for t in range(TT):
                                d = 2 * j + c
                                ins = pe.transpose(psum[uses.bank(use)][:, (c * TT + t) * P:(c * TT + t + 1) * P],
                                                   norm.x[:, u, t, d * P:(d + 1) * P], core.ident[:, :])
                        done(ins, use)
                    for j in range(2):
                        wait_free(pe, f"xT{j}.{u}", turn)
                    pe.wait_ge(q_weights[0], 16)
                    for t in range(TT):
                        q_group(0, t)
                    pe.wait_ge(kv_weights, 64)
                    pe.wait_ge(context_loaded[u], turn * 16 + 16)
                    for key, w in (("k", w_k), ("v", w_v)):
                        for t in range(TT):
                            rows(f"{key}{t}.{u}", lambda c: context[:, u, c, t * P:(t + 1) * P], w, slice(0, G * HD))
                    for j in range(2):
                        use = f"kT{j}.{u}"
                        wait_bank(pe, use, turn)
                        for t in range(TT):
                            if j == 0:
                                wait_free(pe, f"k{t}.{u}", turn)
                        for i in range(2):
                            for t in range(TT):
                                g = 2 * j + i
                                ins = pe.transpose(psum[uses.bank(use)][:, (i * TT + t) * P:(i * TT + t + 1) * P],
                                                   k_rows[:, t, g * HD:(g + 1) * HD], core.ident[:, :])
                        done(ins, use)
                    for j in range(2):
                        transpose_q(0, j)
                    for j in range(2):
                        wait_free(pe, f"kT{j}.{u}", turn)
                        wait_free(pe, f"v{j}.{u}", turn)
                    for s in range(H + 2):
                        if s < H:
                            use, g = f"S{s}.{u}", s // HG
                            wait_bank(pe, use, turn)
                            if s % HG in (0, 2):
                                wait_free(pe, f"qT{g}_{s % HG // 2}.{u}", turn)
                            for t in range(TT):
                                ins = pe.matmul(psum[uses.bank(use)][:, t * S1:(t + 1) * S1], qT[:, g % 2, s % HG, t * P:(t + 1) * P],
                                                kT[:, g, :], start=True, stop=True)
                            done(ins, use)
                            if s < H - HG:
                                if s % HG < 2:
                                    q_group(g + 1, s % HG)
                                else:
                                    transpose_q(g + 1, s % HG - 2)
                        if 1 <= s <= H:
                            h = s - 1
                            use = f"T{h}.{u}"
                            wait_bank(pe, use, turn)
                            wait_free(pe, f"S{h}.{u}", turn)
                            for k in range(TT):
                                for t in range(TT):
                                    ins = pe.transpose(psum[uses.bank(use)][:, k * T + t * P:k * T + (t + 1) * P],
                                                       probs[:, h % QUEUE, t, k * P:(k + 1) * P], core.ident[:, :])
                            done(ins, use)
                        if s >= 2:
                            h = s - 2
                            use = f"R{h}.{u}"
                            wait_bank(pe, use, turn)
                            pe.wait_ge(inverse_spread, b * H + (h + 1))
                            for t in range(TT):
                                ins = pe.transpose(psum[uses.bank(use)][:, t * P:(t + 1) * P], inverse_rows[:, h % QUEUE, t, :], core.ident[:, :])
                            done(ins, use)
                            use = f"O{h}.{u}"
                            wait_bank(pe, use, turn)
                            wait_free(pe, f"T{h}.{u}", turn)
                            for k in range(TT):
                                ins = pe.matmul(psum[uses.bank(use)][:, 0:T], v[:, k, (h // HG) * HD:(h // HG + 1) * HD],
                                                probsT[:, h % QUEUE, k, :], start=k == 0, stop=k == TT - 1)
                            done(ins, use)
                    pe.wait_ge(o_weights, 16)
                    for t in range(TT):
                        use = f"y{t}.{u}"
                        wait_bank(pe, use, turn)
                        for h in range(H):
                            if t == 0 and h == H - 1:
                                wait_free(pe, f"O{h}.{u}", turn)
                            elif t == 0 and h == 0:
                                wait_free(pe, f"O{H - 2}.{u}", turn)
                            ins = pe.matmul(psum[uses.bank(use)][:, :], ctxT[:, h, t * P:(t + 1) * P], w_o[:, h, :],
                                            start=h == 0, stop=h == H - 1)
                        done(ins, use)



ALL_ROWS = B * T
NT = ALL_ROWS // P
NS = NT + E - 1
ROUTER = 96
COPIES = 48


def mixture_constants():
    import numpy as np
    buffer = [0] + [1 if e % 2 else -1 for e in range(1, E)]
    even = [COPIES * (e % 2 == 0) + (e == 0) for e in range(E)]
    odd = [COPIES * (e % 2 == 1) + (e == 0) for e in range(E)]
    row = np.concatenate([P * np.arange(NT), np.arange(NS), buffer, even, odd]).astype(np.float32)
    return np.tile(row[None, :], (P, 1))


def mixture(core, name, x_src, x_dst, slot_x, slot_y, weights):
    nc, psum = core.nc, core.psum
    XT, GATE, UP, DOWN = 0, 2, 4, 6
    LAST = NT + NS - 1

    with ExitStack() as ctx:
        def sb(tag, shape, dtype=F32):
            return ctx.enter_context(nc.sbuf_tensor(f"{name}_{tag}", shape, dtype))

        def sem(tag):
            return core.ctx.enter_context(nc.semaphore(f"{name}_{tag}"))

        rows = sb("rows", [P, NT + NS, D])
        w = sb("w", [P, 3, 3, KC, D])
        SHARED = 2
        router = sb("router", [P, KC, ROUTER])
        table = sb("table", [P, NT + NS + 3 * E])
        x_in = sb("x_in", [P, 2, D])
        xT = sb("xT", [P, 2, KC, P])
        silu = sb("silu", [P, 2, D])
        h = sb("h", [P, 2, D])
        hT = sb("hT", [P, 2, KC, P])
        scaled_x = sb("scaled_x", [P, 2, D])
        before = sb("before", [P, P], BF16)
        ones = sb("ones", [P, P], BF16)
        order = sb("order", [P, E])
        logits = sb("logits", [P, NT, E])
        top = sb("top", [P, NT])
        score = sb("score", [P, NT])
        rank = sb("rank", [P, NT, E])
        chosen = sb("chosen", [P, NT, E])
        chosen_bf = sb("chosen_bf", [P, NT, E], BF16)
        HALF = NT // 2
        running = [sb(f"running{k}", [P, HALF + NT, E]) for k in range(2)]
        starts = [sb(f"starts{k}", [P, E // 2 + E]) for k in range(2)]
        above = sb("above", [P, E, NT])
        position = sb("position", [P, NT])
        index = sb("index", [P, NT], mybir.dt.uint32)
        reached = sb("reached", [P, NS, E])
        parts = sb("parts", [P, 3, NS, E])
        facts = sb("facts", [P, 3, NS])
        slot_facts = sb("slot_facts", [P, 3, NS], mybir.dt.int32)
        expert_end = sb("expert_end", [P, E], mybir.dt.int32)
        stats = sb("stats", [P, NT, 6])
        moments = sb("moments", [P, NT, 2])
        vareps = sb("vareps", [P, NT])
        rstd = sb("rstd", [P, NT])

        x_loaded = [sem(f"x_loaded{k}") for k in range(2)]
        table_loaded = sem("table_loaded")
        router_loaded = sem("router_loaded")
        shared_loaded = sem("shared_loaded")
        expert_loaded = [sem(f"expert_loaded{k}") for k in range(2)]
        filled = sem("filled")
        zeros_stored = sem("zeros_stored")
        first_in = sem("first_in")
        first_full = sem("first_full")
        first_ready = sem("first_ready")
        logits_full = sem("logits_full")
        logits_ready = sem("logits_ready")
        counts_full = sem("counts_full")
        routed = sem("routed")
        score_ready = sem("score_ready")
        scaled = sem("scaled")
        scattered = [sem(f"scattered{k}") for k in range(2)]
        slots_loaded = sem("slots_loaded")
        in_ready = sem("in_ready")
        xT_full = sem("xT_full")
        xT_ready = sem("xT_ready")
        gate_full = sem("gate_full")
        silu_ready = sem("silu_ready")
        up_full = sem("up_full")
        h_ready = sem("h_ready")
        hT_full = sem("hT_full")
        hT_ready = sem("hT_ready")
        y_full = sem("y_full")
        y_ready = sem("y_ready")
        y_stored = sem("y_stored")
        gathered = [sem(f"gathered{k}") for k in range(4)]
        z_ready = sem("z_ready")
        z_stats = sem("z_stats")
        moved = sem("moved")
        rstd_ready = sem("rstd_ready")
        out_ready = sem("out_ready")
        stored = sem("stored")
        src = x_src.rearrange("b (j p) d -> p (b j) d", p=P)
        dst = x_dst.rearrange("b (j p) d -> p (b j) d", p=P)
        GROUP = 4
        CUTS = [0, 8, 16, 20, NS]
        ROUTED = 25

        block = ctx.enter_context(nc.Block())

        @block.sync
        def _(sp):
            for counted in (first_full, logits_full, logits_ready, y_ready, *expert_loaded):
                sp.sem_inc(counted, 1)
            for k in range(2):
                sp.dma_start(rows[:, k * HALF:(k + 1) * HALF, :], src[:, k * HALF:(k + 1) * HALF, :]).then_inc(x_loaded[k], 16)
            for m, key in enumerate(("sg", "su", "sd")):
                sp.dma_start(w[:, SHARED, m], weights[key].rearrange("(c p) n -> p c n", p=P)).then_inc(shared_loaded, 16)
            sp.wait_ge(filled, 2)
            sp.dma_start(slot_x.rearrange("(g p) d -> p g d", p=P), rows[:, NT:NT + NS, :]).then_inc(zeros_stored, 16)
            done = []
            for e in range(E):
                if e == 2:
                    sp.wait_ge(routed, ROUTED)
                    done = [sp.value_load(expert_end[0:1, k:k + 1], min_val=NT, max_val=NT + NS) for k in range(E - 2)]
                if e >= 2:
                    sp.wait_ge(y_full, done[e - 2])
                for m, key in enumerate(("g", "u", "d")):
                    sp.dma_start(w[:, e % 2, m], weights[key][e].rearrange("(c p) n -> p c n", p=P))\
                        .then_inc(expert_loaded[e % 2], 16)
            for k in range(NT // GROUP):
                sp.wait_ge(out_ready, (k + 1) * GROUP)
                sp.dma_start(dst[:, k * GROUP:(k + 1) * GROUP, :], rows[:, k * GROUP:(k + 1) * GROUP, :]).then_inc(stored, 16)
            sp.wait_ge(stored, 16 * (NT // GROUP))

        @block.gpsimd
        def _(pool):
            pool.memset(rows[:, NT:NT + HALF, :], 0.0).then_inc(filled, 1)
            pool.memset(rows[:, NT + HALF:NT + NS, :], 0.0).then_inc(filled, 1)
            pool.memset(before[:, :], 0.0).then_inc(filled, 1)
            pool.memset(ones[:, :], 1.0).then_inc(filled, 1)
            for k in range(2):
                pool.memset(running[k][:, :, :], 0.0).then_inc(filled, 1)
                pool.memset(starts[k][:, :], 0.0).then_inc(filled, 1)
            pool.iota(order[:, :], pattern=[[-1, E]], base=E, channel_multiplier=0,
                      allow_small_or_imprecise_dtypes=True).then_inc(filled, 1)
            pool.wait_ge(filled, 3)
            pool.affine_select(out=before[:, :], in_=before[:, :], compare_op=ALU.is_ge, fill=1.0, base=0,
                               pattern=[[-1, P]], channel_multiplier=1).then_inc(filled, 1)
            pool.wait_ge(score_ready, 1)
            pool.wait_ge(x_loaded[0], 16)
            pool.wait_ge(x_loaded[1], 16)
            for t in range(NT):
                if t >= 2:
                    pool.wait_ge(scattered[t % 2], 16 * (t // 2))
                pool.tensor_tensor(scaled_x[:, t % 2, :], rows[:, t, :], score[:, t:t + 1].broadcast_to([P, D]), ALU.mult)\
                    .then_inc(scaled, 1)
                if t == 0:
                    pool.wait_ge(routed, ROUTED)
                    pool.wait_ge(zeros_stored, 16)
                pool.wait_ge(scaled, t + 1)
                pool.indirect_dma_start(out=slot_x, out_offset=bass.IndirectOffsetOnAxis(ap=index[:, t:t + 1], axis=0),
                                        in_=scaled_x[:, t % 2, :], in_offset=None).then_inc(scattered[t % 2], 16)
            for k in range(2):
                pool.wait_ge(scattered[k], 16 * HALF)
            pool.dma_start(rows[:, NT:NT + NS, :], slot_x.rearrange("(g p) d -> p g d", p=P)).then_inc(slots_loaded, 16)
            for k in range(len(CUTS) - 1):
                pool.wait_ge(y_ready, 1 + NT + CUTS[k + 1])
                pool.dma_start(slot_y.rearrange("(g p) d -> p g d", p=P)[:, CUTS[k]:CUTS[k + 1], :],
                               rows[:, NT + CUTS[k]:NT + CUTS[k + 1], :]).then_inc(y_stored, 16)
            pool.wait_ge(y_stored, 16 * (len(CUTS) - 1))
            for t in range(NT):
                pool.indirect_dma_start(out=rows[:, NT + t, :], out_offset=None, in_=slot_y,
                                        in_offset=bass.IndirectOffsetOnAxis(ap=index[:, t:t + 1], axis=0))\
                    .then_inc(gathered[t // GROUP], 16)
            for k in range(NT // GROUP):
                cols = slice(k * GROUP, (k + 1) * GROUP)
                pool.wait_ge(moved, (k + 1) * (GROUP + 1))
                pool.tensor_tensor(rstd[:, cols], vareps[:, cols], core.minus_half[:, 0:GROUP], ALU.pow).then_inc(rstd_ready, 1)

        @block.scalar
        def _(act):
            act.dma_start(router[:, :, :], weights["r"].rearrange("(c p) n -> p c n", p=P)).then_inc(router_loaded, 16)
            act.dma_start(table[:, :], weights["table"]).then_inc(table_loaded, 16)
            with act.Fori(0, HALF) as pair:
                for u in range(2):
                    act.wait_ge(first_full, pair * 2 + (u + 2))
                    act.wait_ge(logits_full, pair * 2 + 1)
                    act.copy(xT[:, u], psum[XT + u].rearrange("p (c t) -> p c t", c=KC)).then_inc(first_ready, 1)
            act.wait_ge(routed, 1)
            act.activation(score[:, :], top[:, :], ACT.Sigmoid).then_inc(score_ready, 1)

            def take_xT(t, u, first=False):
                act.wait_ge(xT_full, t + 1)
                if not first:
                    act.wait_ge(up_full, t - 1)
                act.copy(xT[:, u], psum[XT + u].rearrange("p (c t) -> p c t", c=KC)).then_inc(xT_ready, 1)

            def step(t, u, first=False, last=False):
                if not last:
                    take_xT(t + 1, 1 - u, first and u == 0)
                act.wait_ge(gate_full, t + 1)
                if not first:
                    act.wait_ge(h_ready, t - 1)
                act.activation(silu[:, u, :], psum[GATE + u], ACT.Silu).then_inc(silu_ready, 1)
                act.wait_ge(hT_full, t + 1)
                if not first:
                    act.wait_ge(y_full, t - 1)
                act.copy(hT[:, u], psum[XT + u].rearrange("p (c t) -> p c t", c=KC)).then_inc(hT_ready, 1)

            act.wait_ge(logits_full, NT + 1)
            take_xT(0, 0, True)
            step(0, 0, True)
            step(1, 1, True)
            with act.Fori(0, (LAST - 2) // 2) as turn:
                step(turn * 2 + 2, 0)
                step(turn * 2 + 3, 1)
            step(LAST, 0, last=True)

        @block.vector
        def _(dve):
            for k in range(2):
                dve.wait_ge(x_loaded[k], 16)
                with dve.Fori(0, HALF // 2) as pair:
                    for u in range(2):
                        dve.wait_ge(first_full, pair * 2 + (k * HALF + 1))
                        dve.tensor_copy(x_in[:, u, :], rows[:, bass.ds(pair * 2 + (k * HALF + u), 1), :]
                                        .rearrange("p a d -> p (a d)")).then_inc(first_in, 1)
                    for u in range(2):
                        dve.wait_ge(logits_full, pair * 2 + (k * HALF + u + 2))
                        dve.tensor_copy(logits[:, bass.ds(pair * 2 + (k * HALF + u), 1), :].rearrange("p a e -> p (a e)"),
                                        psum[GATE + u][:, 0:E]).then_inc(logits_ready, 1)

            steps = [0]

            def step(ins):
                ins.then_inc(routed, 1)
                steps[0] += 1
                dve.wait_ge(routed, steps[0])

            def per_tile(a):
                return a.unsqueeze(2).broadcast_to([P, NT, E])

            multiples = table[:, 0:NT]
            numbers = table[:, NT:NT + NS]
            shares = table[:, NT + NS:NT + NS + 3 * E].rearrange("p (k e) -> p k e", k=3)
            dve.wait_ge(filled, 10)
            dve.wait_ge(table_loaded, 16)
            dve.wait_ge(logits_ready, NT + 1)
            step(dve.tensor_reduce(top[:, :], logits[:, :, :], AX.X, ALU.max))
            step(dve.tensor_tensor(rank[:, :, :], logits[:, :, :], per_tile(top[:, :]), ALU.is_equal))
            step(dve.tensor_tensor(rank[:, :, :], rank[:, :, :], order[:, :].unsqueeze(1).broadcast_to([P, NT, E]), ALU.mult))
            step(dve.tensor_reduce(position[:, :], rank[:, :, :], AX.X, ALU.max))
            step(dve.tensor_tensor(chosen[:, :, :], rank[:, :, :], per_tile(position[:, :]), ALU.is_equal))
            step(dve.tensor_copy(chosen_bf[:, :, :], chosen[:, :, :]))
            dve.wait_ge(counts_full, 2)
            step(dve.tensor_copy(running[0][:, HALF:, :], psum[UP][:, 0:P].rearrange("p (t e) -> p t e", t=NT)))
            for k in range(4):
                a, b = running[k % 2], running[1 - k % 2]
                step(dve.tensor_tensor(b[:, HALF:, :], a[:, HALF:, :], a[:, HALF - 2 ** k:HALF + NT - 2 ** k, :], ALU.add))
            step(dve.tensor_tensor(above[:, :, :], running[0][:, HALF + NT - 1, :].unsqueeze(2).broadcast_to([P, E, NT]),
                                   multiples.unsqueeze(1).broadcast_to([P, E, NT]), ALU.is_gt))
            PAD = E // 2
            step(dve.tensor_reduce(starts[0][:, PAD:], above[:, :, :], AX.X, ALU.add))
            for k in range(3):
                a, b = starts[k % 2], starts[1 - k % 2]
                step(dve.tensor_tensor(b[:, PAD:], a[:, PAD:], a[:, PAD - 2 ** k:PAD + E - 2 ** k], ALU.add))
            first_slot = starts[1][:, PAD - 1:PAD + E - 1]
            step(dve.scalar_tensor_tensor(out=rank[:, :, :], in0=first_slot.unsqueeze(1).broadcast_to([P, NT, E]),
                                          scalar=float(P), in1=running[0][:, HALF - 1:HALF + NT - 1, :], op0=ALU.mult, op1=ALU.add))
            step(dve.tensor_tensor(rank[:, :, :], psum[DOWN][:, 0:P].rearrange("p (t e) -> p t e", t=NT), rank[:, :, :], ALU.add))
            step(dve.tensor_tensor(rank[:, :, :], rank[:, :, :], chosen[:, :, :], ALU.mult))
            step(dve.tensor_reduce(position[:, :], rank[:, :, :], AX.X, ALU.add))
            step(dve.tensor_copy(index[:, :], position[:, :]))
            step(dve.tensor_tensor(reached[:, :, :], first_slot.unsqueeze(1).broadcast_to([P, NS, E]),
                                   numbers.unsqueeze(2).broadcast_to([P, NS, E]), ALU.is_le))
            for k in range(3):
                ins = dve.tensor_tensor(parts[:, k], reached[:, :, :], shares[:, k, :].unsqueeze(1).broadcast_to([P, NS, E]), ALU.mult)
            step(ins)
            step(dve.tensor_reduce(facts[:, :, :], parts[:, :, :, :], AX.X, ALU.add))
            dve.tensor_copy(slot_facts[:, :, :], facts[:, :, :])
            step(dve.tensor_scalar(expert_end[:, :], starts[1][:, PAD:], float(NT), None, ALU.add))
            assert steps[0] == ROUTED, steps[0]

            def take_x(t, u):
                dve.tensor_copy(x_in[:, u, :], rows[:, bass.ds(t, 1), :].rearrange("p a d -> p (a d)")
                                if not isinstance(t, int) else rows[:, t, :]).then_inc(in_ready, 1)

            def give_y(t, u, slot):
                y = rows[:, t, :] if isinstance(t, int) else rows[:, bass.ds(t, 1), :].rearrange("p a d -> p (a d)")
                dve.wait_ge(y_full, t + 1)
                if slot:
                    dve.tensor_copy(y, psum[DOWN + u]).then_inc(y_ready, 1)
                else:
                    dve.wait_ge(scaled, t + 1)
                    dve.tensor_tensor(y, psum[DOWN + u], y, ALU.add).then_inc(y_ready, 1)

            def work(t, u, first=False, last=False, slot=False):
                dve.wait_ge(silu_ready, t + 1)
                dve.wait_ge(up_full, t + 1)
                if not first:
                    dve.wait_ge(hT_full, t - 1)
                dve.tensor_tensor(h[:, u, :], psum[UP + u], silu[:, u, :], ALU.mult).then_inc(h_ready, 1)
                if not (first and u == 0):
                    give_y(t - 1, 1 - u, slot)
                if not last:
                    dve.wait_ge(xT_full, t + 1)
                    take_x(t + 2, u)

            take_x(0, 0)
            take_x(1, 1)
            work(0, 0, first=True)
            work(1, 1, first=True)
            with dve.Fori(0, (NT - 4) // 2) as turn:
                work(turn * 2 + 2, 0)
                work(turn * 2 + 3, 1)
            dve.wait_ge(slots_loaded, 16)
            work(NT - 2, 0)
            work(NT - 1, 1)
            work(NT, 0)
            with dve.Fori(0, (NS - 3) // 2) as turn:
                work(turn * 2 + (NT + 1), 1, slot=True)
                work(turn * 2 + (NT + 2), 0, slot=True)
            work(LAST - 1, 1, last=True, slot=True)
            work(LAST, 0, last=True, slot=True)
            give_y(LAST, 0, True)

            def normalise(k):
                for t in range(k * GROUP, (k + 1) * GROUP):
                    if t == k * GROUP:
                        dve.wait_ge(rstd_ready, k + 1)
                    dve.tensor_scalar(rows[:, t, :], rows[:, t, :], moments[:, t, 0:1], rstd[:, t:t + 1],
                                      ALU.subtract, ALU.mult).then_inc(out_ready, 1)

            for k in range(NT // GROUP):
                for t in range(k * GROUP, (k + 1) * GROUP):
                    dve.wait_ge(gathered[k], 16 * GROUP)
                    if t == 0:
                        dve.wait_ge(y_ready, NT + 1)
                    dve.tensor_tensor(rows[:, t, :], rows[:, t, :], rows[:, NT + t, :], ALU.add).then_inc(z_ready, 1)
                    dve.wait_ge(z_ready, t + 1)
                    dve.bn_stats(stats[:, t, :], rows[:, t, :]).then_inc(z_stats, 1)
                for t in range(k * GROUP, (k + 1) * GROUP):
                    dve.wait_ge(z_stats, t + 1)
                    dve.bn_aggr(moments[:, t, :], stats[:, t, :]).then_inc(moved, 1)
                cols = slice(k * GROUP, (k + 1) * GROUP)
                dve.wait_ge(moved, k * (GROUP + 1) + GROUP)
                dve.tensor_scalar(vareps[:, cols], moments[:, cols, 1], EPS, None, ALU.add).then_inc(moved, 1)
                if k >= 1:
                    normalise(k - 1)
            normalise(NT // GROUP - 1)

        @block.tensor
        def _(pe):
            for k in range(2):
                with pe.Fori(0, HALF // 2) as pair:
                    for u in range(2):
                        pe.wait_ge(first_in, pair * 2 + (k * HALF + u + 1))
                        for c in range(KC):
                            ins = pe.transpose(psum[XT + u][:, c * P:(c + 1) * P], x_in[:, u, c * P:(c + 1) * P], core.ident[:, :])
                        ins.then_inc(first_full, 1)
                    for u in range(2):
                        if k == 0 and u == 0:
                            pe.wait_ge(router_loaded, 16)
                        pe.wait_ge(first_ready, pair * 2 + (k * HALF + u + 1))
                        pe.wait_ge(logits_ready, pair * 2 + (k * HALF + 1))
                        for c in range(KC):
                            ins = pe.matmul(psum[GATE + u][:, 0:ROUTER], xT[:, u, c, :], router[:, c, :], start=c == 0, stop=c == KC - 1)
                        ins.then_inc(logits_full, 1)
            pe.wait_ge(routed, 6)
            pe.wait_ge(filled, 10)
            chosen_flat = chosen_bf[:, :, :].rearrange("p t e -> p (t e)")
            pe.matmul(psum[UP][:, 0:P], ones[:, :], chosen_flat, start=True, stop=True).then_inc(counts_full, 1)
            pe.matmul(psum[DOWN][:, 0:P], before[:, :], chosen_flat, start=True, stop=True).then_inc(counts_full, 1)

            def transpose_x(t, u, first=False):
                pe.wait_ge(in_ready, t + 1)
                if not first:
                    pe.wait_ge(hT_ready, t - 1)
                for c in range(KC):
                    ins = pe.transpose(psum[XT + u][:, c * P:(c + 1) * P], x_in[:, u, c * P:(c + 1) * P], core.ident[:, :])
                ins.then_inc(xT_full, 1)

            def weight(slot, m, c):
                if slot is None:
                    return w[:, SHARED, m, c, :]
                return w[:, bass.ds(slot, 1), m, c, :].rearrange("p a n -> p (a n)")

            def buffer_of(g):
                return pe.value_load(slot_facts[0:1, 0, g:g + 1] if isinstance(g, int) else slot_facts[0:1, 0, bass.ds(g, 1)],
                                     min_val=0, max_val=1)

            def down(t, u, buffer, first=False):
                pe.wait_ge(hT_ready, t + 1)
                if not first:
                    pe.wait_ge(y_ready, t)
                for c in range(KC):
                    ins = pe.matmul(psum[DOWN + u], hT[:, u, c, :], weight(buffer, 2, c), start=c == 0, stop=c == KC - 1)
                ins.then_inc(y_full, 1)

            def step(t, u, buffer=None, previous=None, needs=None, first=False, last=False):
                if not last:
                    transpose_x(t + 1, 1 - u, first and u == 0)
                pe.wait_ge(xT_ready, t + 1)
                if not first:
                    pe.wait_ge(silu_ready, t - 1)
                if needs:
                    for k in range(2):
                        pe.wait_ge(expert_loaded[k], needs[k])
                for c in range(KC):
                    ins = pe.matmul(psum[GATE + u], xT[:, u, c, :], weight(buffer, 0, c), start=c == 0, stop=c == KC - 1)
                ins.then_inc(gate_full, 1)
                if not first:
                    pe.wait_ge(h_ready, t - 1)
                for c in range(KC):
                    ins = pe.matmul(psum[UP + u], xT[:, u, c, :], weight(buffer, 1, c), start=c == 0, stop=c == KC - 1)
                ins.then_inc(up_full, 1)
                if not (first and u == 0):
                    down(t - 1, 1 - u, previous, first=first)
                pe.wait_ge(h_ready, t + 1)
                for c in range(KC):
                    ins = pe.transpose(psum[XT + u][:, c * P:(c + 1) * P], h[:, u, c * P:(c + 1) * P], core.ident[:, :])
                ins.then_inc(hT_full, 1)

            def slot_step(t, u, g, last=False, shared_before=False):
                def fact(k, at):
                    ap = slot_facts[0:1, k, at:at + 1] if isinstance(at, int) else slot_facts[0:1, k, bass.ds(at, 1)]
                    return pe.value_load(ap, min_val=min(k, 1), max_val=(1, COPIES * E // 2 + 1, COPIES * E // 2 + 1)[k])
                needs = [fact(1, g), fact(2, g)]
                step(t, u, fact(0, g), None if shared_before else fact(0, g - 1), needs, last=last)

            transpose_x(0, 0, True)
            pe.wait_ge(shared_loaded, 48)
            step(0, 0, first=True)
            step(1, 1, first=True)
            with pe.Fori(0, (NT - 2) // 2) as turn:
                step(turn * 2 + 2, 0)
                step(turn * 2 + 3, 1)
            pe.wait_ge(routed, ROUTED)
            slot_step(NT, 0, 0, shared_before=True)
            with pe.Fori(0, (NS - 3) // 2) as turn:
                slot_step(turn * 2 + (NT + 1), 1, turn * 2 + 1)
                slot_step(turn * 2 + (NT + 2), 0, turn * 2 + 2)
            slot_step(LAST - 1, 1, NS - 2)
            slot_step(LAST, 0, NS - 1, last=True)
            down(LAST, 0, buffer_of(NS - 1))



def decoder_layers(nc, a, x, result):
    between = [nc.dram_tensor(f"x_after_{k}", (B, T, D), F32).ap() for k in range(1, 6)]
    slot_x = nc.dram_tensor("slot_x", (NS * P, D), F32).ap()
    slot_y = nc.dram_tensor("slot_y", (NS * P, D), F32).ap()

    def group(prefix, *keys):
        return {key: a[f"{prefix}_{key}"] for key in keys}

    with ExitStack() as ctx:
        core = Core(nc, ctx)
        constants(core)
        self_attention(core, "a0", x, between[0], group("a0", "q", "k", "v", "o"), False)
        cross_attention_masked(core, "x0", between[0], a["ctx"], between[1], a["mask"], a["mask_cols"],
                               a["x0_onehot"], group("x0", "q", "k", "v", "bq", "bk", "bv"))
        feed_forward_lora(core, "f0", between[1], between[2],
                          group("f0", "first", "gate", "up", "down", "B_gate", "B_up", "A_down", "B_down", "bias"))
        self_attention(core, "a1", between[2], between[3],
                       group("a1", "dq", "dkv", "uq", "ukv", "q_g", "q_b", "kv_g", "kv_b", "o"), True)
        cross_attention_grouped(core, "x1", between[3], a["ctxT"], between[4], group("x1", "q", "k", "v", "o", "qn", "kn"))
        mixture(core, "m1", between[4], result, slot_x, slot_y, group("m1", "r", "g", "u", "d", "sg", "su", "sd", "table"))


def layout(inputs):
    import numpy as np
    i = {name: np.asarray(value) for name, value in inputs.items()}
    mask = i["mask_Bx1x2048_fk1"].reshape(B, D)
    padded_router = np.zeros((D, ROUTER), i["L1_ffn_router_w"].dtype)
    padded_router[:, 0:E] = i["L1_ffn_router_w"]
    laid = {
        "x": i["x"], "ctx": i["ctx_2048"], "ctxT": i["ctx_2048"].transpose(0, 2, 1),
        "mask": mask, "mask_cols": mask.reshape(B, KC, P).transpose(2, 0, 1), "x0_onehot": xattn_constants(),
        "x0_q": i["L0_xattn_Wq"].T, "x0_k": i["L0_xattn_Wk"].T, "x0_v": i["L0_xattn_Wv"].T,
        "x0_bq": i["L0_xattn_bq"].reshape(-1, P).T, "x0_bk": i["L0_xattn_bk"].reshape(-1, P).T,
        "x0_bv": i["L0_xattn_bv"],
        "a1_o": i["L1_attn_W_o"].T,
        "m1_r": padded_router, "m1_table": mixture_constants(),
    }
    natural = {
        "a0": ("L0_attn_", dict(q="q_out", k="k_out", v="v_out", o="w_out")),
        "a1": ("L1_attn_", dict(dq="W_dq", dkv="W_dkv", uq="W_uq", ukv="W_ukv", q_g="q_ln_g", q_b="q_ln_b",
                                kv_g="kv_ln_g", kv_b="kv_ln_b")),
        "x1": ("L1_xattn_", dict(q="Wq", k="Wk", v="Wv", o="Wo", qn="q_norm_w", kn="k_norm_w")),
        "m1": ("L1_ffn_", dict(g="gate_w", u="up_w", d="down_w", sg="shared_gate_w", su="shared_up_w",
                               sd="shared_down_w")),
    }
    for short, (prefix, names) in natural.items():
        for key, name in names.items():
            laid[f"{short}_{key}"] = i[prefix + name]
    for key, value in ffn0_layout(i).items():
        laid[f"f0_{key}"] = value
    return {name: np.ascontiguousarray(value) for name, value in laid.items()}


def kernel(**inputs):
    import concourse.bacc as bacc
    from concourse.bass_utils import run_bass_kernel_spmd

    nc = bacc.Bacc("TRN2", target_bir_lowering=False, num_devices=1)
    arrays = layout(inputs)
    aps = {name: nc.dram_tensor(f"in_{name}", value.shape, mybir.dt.from_np(value.dtype), kind="ExternalInput").ap()
           for name, value in arrays.items()}
    result = nc.dram_tensor("result", (B, T, D), F32, kind="ExternalOutput").ap()
    decoder_layers(nc, aps, aps["x"], result)
    ran = run_bass_kernel_spmd(nc, [{f"in_{name}": value for name, value in arrays.items()}], core_ids=[0])
    return ran.results[0]["result"]
```

```python
from contextlib import ExitStack

import concourse.bass as bass
from concourse import mybir

F32 = mybir.dt.float32
BF16 = mybir.dt.bfloat16
F32R = mybir.dt.float32r
ALU = mybir.AluOpType
ACT = mybir.ActivationFunctionType
AX = mybir.AxisListType

P = 128
B = 8
T = 256
D = 512
KC = D // P
TT = T // P
TURNS = B // 2
H = 16
DH = D // H
EPS = 1e-5
MASKED = -1e30


class BankUses:

    def __init__(self, base, turn, turns, first=0):
        self.base, self.per, self.at, self.first = base, [0] * 8, {}, first
        for use, bank in turn:
            self.at[use] = (bank, self.per[bank])
            self.per[bank] += 1
        self.after = [n + turns * per for n, per in zip(base, self.per)]

    def bank(self, use):
        return self.at[use][0]

    def before(self, use, turn):
        bank, nth = self.at[use]
        return turn * self.per[bank] + (self.base[bank] + nth - self.first * self.per[bank])


class Segments:

    def __init__(self, base, first_front, turn, last_turn):
        self.before_loop = BankUses(base, first_front, 1)
        self.loop = BankUses(self.before_loop.after, turn, TURNS - 1)
        self.last = BankUses(self.loop.after, last_turn, 1, first=TURNS - 1)
        self.after, self.now = self.last.after, self.loop

    def bank(self, use):
        return self.now.bank(use)

    def before(self, use, turn):
        return self.now.before(use, turn)

    def walk(self, engine, front, sequence):
        self.now = self.before_loop
        front(0, 0, 0)
        self.now = self.loop
        with engine.Fori(0, TURNS - 1) as turn:
            sequence(turn, 0, (turn, 1, turn))
            sequence(turn, 1, (turn, 0, turn + 1))
        self.now = self.last
        sequence(TURNS - 1, 0, (TURNS - 1, 1, TURNS - 1))
        sequence(TURNS - 1, 1, None)
        self.now = self.loop


def high_part(engine, out, x):
    return engine.tensor_copy(out.bitcast(F32R), x)


def subtract(engine, out, x, part):
    return engine.tensor_tensor(out.bitcast(F32R), x, part, ALU.subtract)


def split_matmul(pe, out, stationary, moving, start, stop, **more):
    pairs = [(0, 0), (0, 1), (1, 0)]
    for k, (a, b) in enumerate(pairs):
        ins = pe.matmul(out, stationary[a].bitcast(F32R), moving[b].bitcast(F32R), start=start and k == 0,
                        stop=stop and k == len(pairs) - 1, **more)
    return ins


class Core:

    def __init__(self, nc, ctx):
        self.nc, self.ctx = nc, ctx
        self.banks = ctx.enter_context(nc.psum_tensor("banks", [P, 8, 512], F32))
        self.psum = [self.banks[:, i, :] for i in range(8)]
        self.bank_full = [ctx.enter_context(nc.semaphore(f"bank_full{i}")) for i in range(8)]
        self.bank_free = [ctx.enter_context(nc.semaphore(f"bank_free{i}")) for i in range(8)]
        self.uses = [0] * 8
        self.held, self.held_ctx = [], ctx.enter_context(ExitStack())
        self.ident = ctx.enter_context(nc.sbuf_tensor("ident", [P, P], F32))
        self.ident_bf = ctx.enter_context(nc.sbuf_tensor("ident_bf", [P, P], BF16))
        self.causal = ctx.enter_context(nc.sbuf_tensor("causal", [P, 4, P], BF16))
        self.minus_half = ctx.enter_context(nc.sbuf_tensor("minus_half", [P, 32], F32))

    def semaphore(self, name):
        self.held.append(self.held_ctx.enter_context(self.nc.semaphore(name)))
        return self.held[-1]

    def release_semaphores(self):
        with self.nc.Block() as block:
            @block.gpsimd
            def _(pool):
                for semaphore in self.held:
                    pool.sem_clear(semaphore)
        self.held_ctx.close()
        self.held = []


def constants(core):
    nc = core.nc
    with ExitStack() as ctx:
        filled = core.semaphore("constants_filled")
        block = ctx.enter_context(nc.Block())

        @block.gpsimd
        def _(pool):
            for bank in range(8):
                pool.sem_inc(core.bank_free[bank], 1)
            pool.memset(core.ident[:, :], 0.0).then_inc(filled, 1)
            pool.memset(core.ident_bf[:, :], 0.0).then_inc(filled, 1)
            pool.memset(core.causal[:, :, :], 0.0).then_inc(filled, 1)
            pool.memset(core.minus_half[:, :], -0.5).then_inc(filled, 1)
            pool.wait_ge(filled, 4)
            pool.affine_select(out=core.ident[:, :], in_=core.ident[:, :], compare_op=ALU.not_equal, fill=1.0,
                               base=0, pattern=[[-1, P]], channel_multiplier=1).then_inc(filled, 1)
            pool.affine_select(out=core.ident_bf[:, :], in_=core.ident_bf[:, :], compare_op=ALU.not_equal,
                               fill=1.0, base=0, pattern=[[-1, P]], channel_multiplier=1).then_inc(filled, 1)
            pool.affine_select(out=core.causal[:, :, :], in_=core.causal[:, :, :], compare_op=ALU.is_ge,
                               fill=MASKED, base=0, pattern=[[0, 4], [-1, P]],
                               channel_multiplier=1).then_inc(filled, 1)
            pool.wait_ge(filled, 7)


class Norm:

    def __init__(self, core, name):
        nc, ctx = core.nc, core.ctx_stage
        self.x = ctx.enter_context(nc.sbuf_tensor(f"{name}_x", [P, 2, TT, D], F32))
        self.z = ctx.enter_context(nc.sbuf_tensor(f"{name}_z", [P, 2, TT, D], F32))
        self.stats = ctx.enter_context(nc.sbuf_tensor(f"{name}_stats", [P, TT, 6], F32))
        self.moments = ctx.enter_context(nc.sbuf_tensor(f"{name}_moments", [P, TT, 2], F32))
        self.vareps = ctx.enter_context(nc.sbuf_tensor(f"{name}_vareps", [P, TT], F32))
        self.rstd = ctx.enter_context(nc.sbuf_tensor(f"{name}_rstd", [P, TT], F32))
        self.loaded = [core.semaphore(f"{name}_x_loaded{u}") for u in range(2)]
        self.moved = core.semaphore(f"{name}_moments_steps")
        self.rstd_ready = core.semaphore(f"{name}_rstd_ready")
        self.out_ready = core.semaphore(f"{name}_out_ready")
        self.stored = [core.semaphore(f"{name}_stored{u}") for u in range(2)]

    STEPS = 6


def norm_dve(core, norm, uses, turn, u):
    dve = core.nc.vector
    full, free = core.bank_full, core.bank_free
    y = [uses.bank(f"y{j}.{u}") for j in range(TT)]
    n = [uses.before(f"y{j}.{u}", turn) for j in range(TT)]
    s = (turn * 2 + u) * norm.STEPS
    z = norm.z[:, u]
    dve.wait_ge(full[y[0]], n[0] + 1)
    dve.wait_ge(norm.loaded[u], turn * 16 + 16)
    if u == 0:
        dve.wait_ge(norm.stored[0], turn * 16 + 1)
    else:
        dve.wait_ge(norm.stored[1], turn * 16 + 1)
    dve.tensor_tensor(z[:, 0, :], core.psum[y[0]][:, :], norm.x[:, u, 0, :], ALU.add).then_inc(free[y[0]], 1)
    dve.wait_ge(free[y[0]], n[0] + 2)
    dve.bn_stats(norm.stats[:, 0, :], z[:, 0, :]).then_inc(norm.moved, 1)
    dve.wait_ge(full[y[1]], n[1] + 1)
    dve.wait_ge(norm.moved, s + 1)
    dve.tensor_tensor(z[:, 1, :], core.psum[y[1]][:, :], norm.x[:, u, 1, :], ALU.add).then_inc(free[y[1]], 1)
    dve.bn_aggr(norm.moments[:, 0, :], norm.stats[:, 0, :]).then_inc(norm.moved, 1)
    dve.wait_ge(free[y[1]], n[1] + 2)
    dve.bn_stats(norm.stats[:, 1, :], z[:, 1, :]).then_inc(norm.moved, 1)
    dve.wait_ge(norm.moved, s + 3)
    dve.tensor_scalar(norm.vareps[:, 0:1], norm.moments[:, 0, 1:2], EPS, None, ALU.add).then_inc(norm.moved, 1)
    dve.bn_aggr(norm.moments[:, 1, :], norm.stats[:, 1, :]).then_inc(norm.moved, 1)
    dve.wait_ge(norm.moved, s + 5)
    dve.tensor_scalar(norm.vareps[:, 1:2], norm.moments[:, 1, 1:2], EPS, None, ALU.add).then_inc(norm.moved, 1)
    for j in range(TT):
        dve.wait_ge(norm.rstd_ready, turn * 2 + (u + 1))
        dve.tensor_scalar(z[:, j, :], z[:, j, :], norm.moments[:, j, 0:1], norm.rstd[:, j:j + 1],
                          ALU.subtract, ALU.mult).then_inc(norm.out_ready, 1)


def norm_pool(core, norm, turn, u, steps=Norm.STEPS):
    pool = core.nc.gpsimd
    pool.wait_ge(norm.moved, (turn * 2 + u) * steps + steps)
    pool.tensor_tensor(norm.rstd[:, :], norm.vareps[:, :], core.minus_half[:, 0:TT], ALU.pow)\
        .then_inc(norm.rstd_ready, 1)


def load_x(core, norm, x_src, b, u):
    core.nc.sync.dma_start(norm.x[:, u], x_src[b].rearrange("(j p) d -> p j d", p=P)).then_inc(norm.loaded[u], 16)


def store_x(core, norm, x_dst, b, turn, u):
    core.nc.sync.wait_ge(norm.out_ready, (turn * 2 + u) * TT + TT)
    core.nc.sync.dma_start(x_dst[b].rearrange("(j p) d -> p j d", p=P), norm.z[:, u]).then_inc(norm.stored[u], 16)


def rows_in_and_out(core, norm, uses, x_src, x_dst, load_context=None, context_free=None):
    sp = core.nc.sync

    def x_free(turn, u):
        bank, n = uses.bank(f"y1.{u}"), uses.before(f"y1.{u}", turn)
        sp.wait_ge(core.bank_free[bank], n + 2)

    for u in range(2):
        sp.sem_inc(norm.stored[u], 1)
        load_x(core, norm, x_src, u, u)
        if load_context:
            load_context(u, u)
    with sp.Fori(0, TURNS - 1) as turn:
        for u in range(2):
            if load_context:
                context_free(turn, u)
                load_context(turn * 2 + (u + 2), u)
            x_free(turn, u)
            load_x(core, norm, x_src, turn * 2 + (u + 2), u)
            store_x(core, norm, x_dst, turn * 2 + u, turn, u)
    for u in range(2):
        store_x(core, norm, x_dst, 2 * (TURNS - 1) + u, TURNS - 1, u)
    for u in range(2):
        sp.wait_ge(norm.stored[u], 16 * TURNS + 1)



UNITS = 12
LAG = 3
FRONT_AT = UNITS + 1
RANK = D // 4


def self_attention(core, name, x_src, x_dst, weights, latent):
    nc = core.nc

    def front_uses(u):
        xT = [(f"xT0.{u}", 0), (f"xT1.{u}", 1)]
        return (xT, [(f"low.{u}", 2)], [(f"lowT.{u}", 3)]) if latent else (xT, [], [])

    def sequence_uses(u, following):
        out = [(f"q0.{u}", 6), (f"q1.{u}", 7), (f"k0.{u}", 0), (f"k1.{u}", 1), (f"v0.{u}", 2), (f"v1.{u}", 3)]
        xT, low, lowT = front_uses(1 - u) if following else ([], [], [])
        for n in range(UNITS + LAG + 1):
            if n < UNITS:
                out.append((f"S{n}.{u}", n % 4))
            if LAG <= n < UNITS + LAG:
                out.append((f"T{n - LAG}.{u}", 4 + n % 2))
            m = n - LAG - 1
            if m >= 0 and m % 3 == 2:
                out += [(f"R{m // 3}.{u}", 7), (f"O{m // 3}.{u}", 6)]
            if n == FRONT_AT:
                out += xT
        return out + low + [(f"y0.{u}", 4), (f"y1.{u}", 5)] + lowT

    uses = Segments(core.uses, [use for group in front_uses(0) for use in group],
                    sequence_uses(0, True) + sequence_uses(1, True), sequence_uses(0, True) + sequence_uses(1, False))
    core.uses = uses.after
    full, free, psum = core.bank_full, core.bank_free, core.psum

    with ExitStack() as ctx:
        core.ctx_stage = ctx

        def sb(tag, shape, dtype=F32):
            return ctx.enter_context(nc.sbuf_tensor(f"{name}_{tag}", shape, dtype))

        def sem(tag):
            return core.semaphore(f"{name}_{tag}")

        norm = Norm(core, name)
        if latent:
            w_down = sb("w_down", [P, KC, 2 * RANK])
            w_uq = sb("w_uq", [P, D])
            w_ukv = sb("w_ukv", [P, 2 * D])
            gamma = sb("gamma", [P, 2])
            beta = sb("beta", [P, 2])
            low_stats = sb("low_stats", [P, 4, 6])
            low_moments = sb("low_moments", [P, 4, 2])
            low_vareps = sb("low_vareps", [P, 4])
            low_rstd = sb("low_rstd", [P, 4])
            low = sb("low", [P, 4, RANK])
            lowT = sb("lowT", [P, 4, P])
            low_steps = sem("low_steps")
            low_rstd_ready = sem("low_rstd_ready")
        else:
            w_q = sb("w_q", [P, KC, D])
            w_k = sb("w_k", [P, KC, D])
            w_v = sb("w_v", [P, KC, D])
            x_high = sb("x_high", [P, KC, T])
            x_rest = sb("x_rest", [P, KC, T])
            x_steps = sem("x_steps")
        w_o = sb("w_o", [P, KC, D])
        xT = sb("xT", [P, KC, T])
        qT = sb("qT", [P, 4, T])
        k_of_head = sb("k_of_head", [P, H, T])
        v = sb("v", [P, TT, D])
        minus_max = sb("minus_max", [P, UNITS, 4])
        sums = sb("sums", [P, 4, 8])
        inverse = sb("inverse", [P, 4, 8])
        inverse_rows = sb("inverse_rows", [P, 2, 8, DH])
        probs = sb("probs", [P, 3, 512])
        probsT = sb("probsT", [P, 2, 4, 3 * P])
        spread = sb("spread", [P, 2, T])
        ctxT = sb("ctxT", [P, 4, T])
        if not latent:
            ctx_high = sb("ctx_high", [P, 4, T])
            ctx_rest = sb("ctx_rest", [P, 4, T])
            ctx_steps = sem("ctx_steps")
        whole_w = {} if latent else {"q": w_q, "k": w_k, "v": w_v, "o": w_o}
        high_w = {key: sb(f"w_{key}_high", [P, KC, D]) for key in whole_w}
        rest_w = {key: sb(f"w_{key}_rest", [P, KC, D]) for key in whole_w}
        loaded = {key: sem(f"w_{key}_loaded") for key in {**whole_w, "o": w_o}}
        if not latent:
            rounded = sem("w_rounded")
            split_by = [sem("w_split_by_dve"), sem("w_split_by_pool")]

        def split_of(key):
            n = "qkvo".index(key)
            return split_by[n // 2], n % 2 + 1
        weights_loaded = sem("weights_loaded")
        k_cleared = sem("k_cleared")
        max_ready = sem("max_ready")
        inverse_ready = sem("inverse_ready")
        inverse_spread = sem("inverse_spread")
        SMALL = 8

        def wait_bank(engine, use, turn):
            engine.wait_ge(free[uses.bank(use)], uses.before(use, turn) + 1)

        def wait_full(engine, use, turn):
            engine.wait_ge(full[uses.bank(use)], uses.before(use, turn) + 1)

        def wait_free(engine, use, turn):
            engine.wait_ge(free[uses.bank(use)], uses.before(use, turn) + 2)

        block = ctx.enter_context(nc.Block())

        def split_weight(engine, key):
            engine.wait_ge(rounded, "qkvo".index(key) + 1)
            subtract(engine, rest_w[key][:, :, :], whole_w[key][:, :, :], high_w[key][:, :, :]).then_inc(split_of(key)[0], 1)

        @block.sync
        def _(sp):
            rows_in_and_out(core, norm, uses, x_src, x_dst)

        @block.gpsimd
        def _(pool):
            if latent:
                pool.dma_start(w_down[:, :, 0:RANK], weights["dq"].rearrange("(c p) n -> p c n", p=P)).then_inc(weights_loaded, 16)
                pool.dma_start(w_down[:, :, RANK:], weights["dkv"].rearrange("(c p) n -> p c n", p=P)).then_inc(weights_loaded, 16)
                pool.dma_start(w_uq[:, :], weights["uq"]).then_inc(weights_loaded, 16)
                pool.dma_start(w_ukv[:, :], weights["ukv"]).then_inc(weights_loaded, 16)
                for j, key in enumerate(("q_g", "kv_g")):
                    pool.dma_start(gamma[:, j:j + 1], weights[key].rearrange("(p a) -> p a", a=1)).then_inc(weights_loaded, 16)
                for j, key in enumerate(("q_b", "kv_b")):
                    pool.dma_start(beta[:, j:j + 1], weights[key].rearrange("(p a) -> p a", a=1)).then_inc(weights_loaded, 16)
            pool.memset(k_of_head[:, :, :], 0.0).then_inc(k_cleared, 1)
            for key in ("v", "o"):
                if key in whole_w:
                    split_weight(pool, key)

            def front(turn, u, own):
                if latent:
                    pool.wait_ge(low_steps, (own * 2 + u) * 4 + 4)
                    pool.tensor_tensor(low_rstd[:, :], low_vareps[:, :], core.minus_half[:, 0:4], ALU.pow)\
                        .then_inc(low_rstd_ready, 1)

            def sequence(turn, u, following):
                if following:
                    front(*following)
                norm_pool(core, norm, turn, u)

            uses.walk(pool, front, sequence)

        @block.scalar
        def _(act):
            for key, w in {**whole_w, "o": w_o}.items():
                act.dma_start(w[:, :, :], weights[key].rearrange("(c p) n -> p c n", p=P)).then_inc(loaded[key], 16)

            def take_xT(turn, u, own):
                for j in range(2):
                    use = f"xT{j}.{u}"
                    wait_full(act, use, turn)
                    act.copy(xT[:, 2 * j:2 * j + 2, :], psum[uses.bank(use)][:, :].rearrange("p (c t) -> p c t", c=2))\
                        .then_inc(free[uses.bank(use)], 1)

            def take_lowT(turn, u, own):
                use = f"lowT.{u}"
                wait_full(act, use, turn)
                act.wait_ge(weights_loaded, 16 * SMALL)
                for j in range(2):
                    ins = act.activation(lowT[:, 2 * j:2 * j + 2, :],
                                         psum[uses.bank(use)][:, 2 * j * P:(2 * j + 2) * P].rearrange("p (c t) -> p c t", c=2),
                                         ACT.Identity, bias=beta[:, j:j + 1], scale=gamma[:, j:j + 1])
                ins.then_inc(free[uses.bank(use)], 1)

            def front(turn, u, own):
                take_xT(turn, u, own)
                if latent:
                    take_lowT(turn, u, own)

            def sequence(turn, u, following):
                b = turn * 2 + u
                for j in range(2):
                    use = f"q{j}.{u}"
                    wait_full(act, use, turn)
                    act.activation(qT[:, 2 * j:2 * j + 2, :], psum[uses.bank(use)][:, :].rearrange("p (c t) -> p c t", c=2),
                                   ACT.Copy, scale=float(DH) ** -0.5).then_inc(free[uses.bank(use)], 1)
                for j in range(TT):
                    use = f"v{j}.{u}"
                    wait_full(act, use, turn)
                    act.copy(v[:, j, :], psum[uses.bank(use)][:, :]).then_inc(free[uses.bank(use)], 1)

                def exps(n):
                    use, c, k = f"S{n}.{u}", n // 3, n % 3
                    act.wait_ge(max_ready, b * UNITS + (n + 1))
                    if n >= 3:
                        wait_full(act, f"T{n - 3}.{u}", turn)
                    heads, width = (4, P) if k == 0 else (2, T)
                    for i in range(heads):
                        at = i if k == 0 else 4 + 2 * (k - 1) + i
                        ins = act.activation(probs[:, n % 3, i * width:(i + 1) * width],
                                       psum[uses.bank(use)][:, i * width:(i + 1) * width], ACT.Exp,
                                       bias=minus_max[:, n, i:i + 1], accum_out=sums[:, c, at:at + 1])
                    ins.then_inc(free[uses.bank(use)], 1)

                def spread_out(c):
                    use = f"R{c}.{u}"
                    wait_full(act, use, turn)
                    if c >= 2:
                        wait_free(act, f"O{c - 2}.{u}", turn)
                    act.copy(spread[:, c % 2, :], psum[uses.bank(use)][:, 0:T]).then_inc(free[uses.bank(use)], 1)

                for n in range(UNITS + LAG + 1):
                    if n < UNITS:
                        exps(n)
                    m = n - LAG - 1
                    if m >= 0 and m % 3 == 2:
                        spread_out(m // 3)
                    if n == FRONT_AT and following:
                        take_xT(*following)
                if latent and following:
                    take_lowT(*following)

            uses.walk(act, front, sequence)

        @block.vector
        def _(dve):
            for key in whole_w:
                dve.wait_ge(loaded[key], 16)
                high_part(dve, high_w[key][:, :, :], whole_w[key][:, :, :]).then_inc(rounded, 1)
                if key in ("q", "k"):
                    split_weight(dve, key)

            def front(turn, u, own):
                b = own * 2 + u
                if not latent:
                    for j in range(2):
                        wait_free(dve, f"xT{j}.{u}", turn)
                    high_part(dve, x_high[:, :, :], xT[:, :, :]).then_inc(x_steps, 1)
                    dve.wait_ge(x_steps, b * 2 + 1)
                    subtract(dve, x_rest[:, :, :], xT[:, :, :], x_high[:, :, :]).then_inc(x_steps, 1)
                    return
                use = f"low.{u}"
                bank = psum[uses.bank(use)]
                s = b * 4
                wait_full(dve, use, turn)
                for part in range(4):
                    j, t = part // 2, part % 2
                    ins = dve.bn_stats(low_stats[:, part, :], bank[:, (2 * t + j) * P:(2 * t + j + 1) * P])
                ins.then_inc(low_steps, 1)
                dve.wait_ge(low_steps, s + 1)
                dve.memset(low_vareps[:, :], EPS).then_inc(low_steps, 1)
                for part in range(4):
                    ins = dve.bn_aggr(low_moments[:, part, :], low_stats[:, part, :])
                ins.then_inc(low_steps, 1)
                dve.wait_ge(low_steps, s + 3)
                dve.tensor_scalar(low_vareps[:, :], low_moments[:, :, 1], EPS, None, ALU.add).then_inc(low_steps, 1)
                dve.wait_ge(low_rstd_ready, b + 1)
                for part in range(4):
                    j, t = part // 2, part % 2
                    ins = dve.tensor_scalar(low[:, part, :], bank[:, (2 * t + j) * P:(2 * t + j + 1) * P],
                                            low_moments[:, part, 0:1], low_rstd[:, part:part + 1],
                                            ALU.subtract, ALU.mult)
                ins.then_inc(free[uses.bank(use)], 1)

            def sequence(turn, u, following):
                b = turn * 2 + u
                dve.wait_ge(k_cleared, 1)
                for j in range(2):
                    use = f"k{j}.{u}"
                    wait_full(dve, use, turn)
                    for i in range(4):
                        rows = slice(DH * i, DH * i + DH)
                        ins = dve.tensor_copy(k_of_head[rows, 8 * j + i:8 * j + i + 5:4, :],
                                              psum[uses.bank(use)][rows, :].rearrange("p (c t) -> p c t", c=2))
                    ins.then_inc(free[uses.bank(use)], 1)

                def row_max(n):
                    use, k = f"S{n}.{u}", n % 3
                    wait_full(dve, use, turn)
                    heads = 4 if k == 0 else 2
                    dve.tensor_reduce(minus_max[:, n, 0:heads],
                                      psum[uses.bank(use)][:, :].rearrange("p (h s) -> p h s", h=heads),
                                      AX.X, ALU.max, negate=True).then_inc(max_ready, 1)

                def probs_out(n):
                    use, c, k = f"T{n}.{u}", n // 3, n % 3
                    wait_full(dve, use, turn)
                    if c >= 2:
                        wait_full(dve, f"O{c - 2}.{u}", turn)
                    if k == 0:
                        out = probsT[:, c % 2, :, 0:P]
                    else:
                        out = probsT[:, c % 2, 2 * (k - 1):2 * k, P:3 * P]
                    dve.tensor_copy(out, psum[uses.bank(use)][:, :].rearrange("p (h s) -> p h s", h=4 if k == 0 else 2))\
                        .then_inc(free[uses.bank(use)], 1)

                def invert(c):
                    wait_free(dve, f"S{3 * c + 2}.{u}", turn)
                    dve.reciprocal(inverse[:, c, :], sums[:, c, :]).then_inc(inverse_ready, 1)
                    dve.wait_ge(inverse_ready, b * 4 + (c + 1))
                    if c >= 2:
                        wait_full(dve, f"R{c - 2}.{u}", turn)
                    dve.tensor_copy(inverse_rows[:, c % 2], inverse[:, c, :].unsqueeze(2).broadcast_to([P, 8, DH]))\
                        .then_inc(inverse_spread, 1)

                def scale_ctx(c):
                    use = f"O{c}.{u}"
                    wait_full(dve, use, turn)
                    wait_free(dve, f"R{c}.{u}", turn)
                    dve.tensor_tensor(ctxT[:, c, :], psum[uses.bank(use)][:, 0:T], spread[:, c % 2, :], ALU.mult)\
                        .then_inc(free[uses.bank(use)], 1)
                    if latent:
                        return
                    wait_free(dve, use, turn)
                    high_part(dve, ctx_high[:, c, :], ctxT[:, c, :]).then_inc(ctx_steps, 1)
                    dve.wait_ge(ctx_steps, b * 8 + (2 * c + 1))
                    subtract(dve, ctx_rest[:, c, :], ctxT[:, c, :], ctx_high[:, c, :]).then_inc(ctx_steps, 1)

                for n in range(UNITS + LAG + 1):
                    if n < UNITS:
                        row_max(n)
                    if LAG <= n < UNITS + LAG:
                        m = n - LAG
                        if m % 3 == 2:
                            invert(m // 3)
                        probs_out(m)
                    m = n - LAG - 1
                    if m >= 0 and m % 3 == 2:
                        scale_ctx(m // 3)
                if following:
                    front(*following)
                norm_dve(core, norm, uses, turn, u)

            uses.walk(dve, front, sequence)

        @block.tensor
        def _(pe):
            if latent:
                pe.wait_ge(weights_loaded, 16 * SMALL)
            def done(ins, use):
                ins.then_inc(full[uses.bank(use)], 1)

            def wait_split(key):
                pe.wait_ge(*split_of(key))

            def transpose_x(turn, u, own):
                pe.wait_ge(norm.loaded[u], own * 16 + 16)
                for j in range(2):
                    use = f"xT{j}.{u}"
                    wait_bank(pe, use, turn)
                    for c in range(2):
                        for t in range(TT):
                            d = 2 * j + c
                            ins = pe.transpose(psum[uses.bank(use)][:, (c * TT + t) * P:(c * TT + t + 1) * P],
                                               norm.x[:, u, t, d * P:(d + 1) * P], core.ident[:, :])
                    done(ins, use)

            def low_product(turn, u, own):
                for j in range(2):
                    wait_free(pe, f"xT{j}.{u}", turn)
                use = f"low.{u}"
                wait_bank(pe, use, turn)
                for t in range(TT):
                    for c in range(KC):
                        ins = pe.matmul(psum[uses.bank(use)][:, t * 2 * RANK:(t + 1) * 2 * RANK],
                                        xT[:, c, t * P:(t + 1) * P], w_down[:, c, :], start=c == 0, stop=c == KC - 1)
                done(ins, use)

            def transpose_low(turn, u, own):
                use = f"low.{u}"
                wait_free(pe, use, turn)
                use = f"lowT.{u}"
                wait_bank(pe, use, turn)
                for part in range(4):
                    ins = pe.transpose(psum[uses.bank(use)][:, part * P:(part + 1) * P], low[:, part, :], core.ident[:, :])
                done(ins, use)

            def front(turn, u, own):
                transpose_x(turn, u, own)
                if latent:
                    low_product(turn, u, own)
                    transpose_low(turn, u, own)

            def sequence(turn, u, following):
                b = turn * 2 + u
                if latent:
                    wait_bank(pe, f"v1.{u}", turn)
                else:
                    pe.wait_ge(x_steps, b * 2 + 2)
                for key in ("q", "k"):
                    for j in range(2):
                        use = f"{key}{j}.{u}"
                        wait_bank(pe, use, turn)
                        for m in range(2):
                            cols = slice((2 * j + m) * P, (2 * j + m + 1) * P)
                            out = psum[uses.bank(use)][:, m * T:(m + 1) * T]
                            if latent:
                                w, low_x = (w_uq, lowT[:, 0:2, :]) if key == "q" else (w_ukv, lowT[:, 2:4, :])
                                ins = pe.matmul(out, w[:, cols], low_x, start=True, stop=True)
                            else:
                                if j == 0 and m == 0:
                                    wait_split(key)
                                w = (high_w[key], rest_w[key])
                                for c in range(KC):
                                    ins = split_matmul(pe, out, [part[:, c, cols] for part in w],
                                                       (x_high[:, c, :], x_rest[:, c, :]), start=c == 0, stop=c == KC - 1)
                        done(ins, use)
                for t in range(TT):
                    use = f"v{t}.{u}"
                    wait_bank(pe, use, turn)
                    if latent:
                        ins = pe.matmul(psum[uses.bank(use)][:, :], lowT[:, 2 + t, :], w_ukv[:, D:2 * D], start=True, stop=True)
                    else:
                        wait_split("v")
                        for c in range(KC):
                            ins = split_matmul(pe, psum[uses.bank(use)][:, :], [part[:, c, t * P:(t + 1) * P] for part in (x_high, x_rest)],
                                               (high_w["v"][:, c, :], rest_w["v"][:, c, :]), start=c == 0, stop=c == KC - 1)
                    done(ins, use)

                def scores(n):
                    use, c, k = f"S{n}.{u}", n // 3, n % 3
                    if n == 0:
                        for w in ("q0", "q1", "k0", "k1", "v0", "v1"):
                            wait_free(pe, f"{w}.{u}", turn)
                    wait_bank(pe, use, turn)
                    bank = psum[uses.bank(use)]
                    if k == 0:
                        pe.matmul(bank[:, :], qT[:, c, 0:P], k_of_head[:, 4 * c:4 * c + 4, 0:P], start=True, stop=False)
                        ins = pe.matmul(bank[:, :], core.ident_bf[:, :], core.causal[:, :, :], start=False, stop=True)
                    else:
                        h = 4 * c + 2 * (k - 1)
                        pe.matmul(bank[:, :], qT[:, c, P:T], k_of_head[:, h:h + 2, :], start=True, stop=False)
                        ins = pe.matmul(bank[:, :].rearrange("p (h s) -> p h s", h=2)[:, :, P:T], core.ident_bf[:, :],
                                        core.causal[:, 0:2, :], start=False, stop=True)
                    done(ins, use)

                def transposes(n):
                    use, c, k = f"T{n}.{u}", n // 3, n % 3
                    wait_bank(pe, use, turn)
                    wait_free(pe, f"S{n}.{u}", turn)
                    for j in range(4):
                        ins = pe.transpose(psum[uses.bank(use)][:, j * P:(j + 1) * P],
                                           probs[:, n % 3, j * P:(j + 1) * P], core.ident[:, :])
                    done(ins, use)

                def context(c):
                    use = f"R{c}.{u}"
                    wait_bank(pe, use, turn)
                    pe.wait_ge(inverse_spread, b * 4 + (c + 1))
                    for t in range(TT):
                        ins = pe.transpose(psum[uses.bank(use)][:, t * P:(t + 1) * P],
                                           inverse_rows[:, c % 2, 4 * t:4 * t + 4, :].rearrange("p h d -> p (h d)"),
                                           core.ident[:, :])
                    done(ins, use)
                    use = f"O{c}.{u}"
                    wait_bank(pe, use, turn)
                    for k in (1, 2):
                        wait_free(pe, f"T{3 * c + k}.{u}", turn)
                    for i in range(4):
                        pe.matmul(psum[uses.bank(use)][DH * i:DH * i + DH, 0:T], v[:, 0, (4 * c + i) * DH:(4 * c + i + 1) * DH],
                                  probsT[:, c % 2, i, 0:T], start=True, stop=False)
                    for i in range(4):
                        ins = pe.matmul(psum[uses.bank(use)][DH * i:DH * i + DH, P:T], v[:, 1, (4 * c + i) * DH:(4 * c + i + 1) * DH],
                                        probsT[:, c % 2, i, T:3 * P], start=False, stop=True)
                    done(ins, use)

                for n in range(UNITS + LAG + 1):
                    if n < UNITS:
                        scores(n)
                    if LAG <= n < UNITS + LAG:
                        transposes(n - LAG)
                    m = n - LAG - 1
                    if m >= 0 and m % 3 == 2:
                        context(m // 3)
                    if n == FRONT_AT and following:
                        transpose_x(*following)
                if latent and following:
                    low_product(*following)
                for t in range(TT):
                    use = f"y{t}.{u}"
                    wait_bank(pe, use, turn)
                    if latent:
                        pe.wait_ge(loaded["o"], 16)
                        if t == 0:
                            wait_free(pe, f"O3.{u}", turn)
                    else:
                        wait_split("o")
                    for c in range(4):
                        if latent:
                            ins = pe.matmul(psum[uses.bank(use)][:, :], ctxT[:, c, t * P:(t + 1) * P], w_o[:, c, :],
                                            start=c == 0, stop=c == 3)
                            continue
                        if t == 0 and c >= 2:
                            pe.wait_ge(ctx_steps, b * 8 + (2 * c + 2))
                        ins = split_matmul(pe, psum[uses.bank(use)][:, :], [part[:, c, t * P:(t + 1) * P] for part in (ctx_high, ctx_rest)],
                                           (high_w["o"][:, c, :], rest_w["o"][:, c, :]), start=c == 0, stop=c == 3)
                    done(ins, use)
                if latent and following:
                    transpose_low(*following)

            uses.walk(pe, front, sequence)



SIZE = T
CH = SIZE // H
POS = D
PT = POS // P
PARTS = 3
PAIRS = [(0, 0), (0, 1), (1, 0), (0, 2), (1, 1), (2, 0)]
MASK_ROW = CH * len(PAIRS)
MAX_ROW = MASK_ROW + len(PAIRS)
ROWS = MAX_ROW + PARTS
SCALE = float(CH) ** -0.5
NEG = 1e6
UNIT_LEAD = 22
UNITS_IN_TAIL = 1
MAXIMA_AT = 9
SHIFT_AT = 11
SLOTS = 4 * 16


def xattn_constants():
    import numpy as np
    m = np.zeros((P, 4, P), np.float32)
    for half in range(2):
        for i in range(4):
            for d in range(CH):
                m[32 * i + d, half, 64 * half + CH * i + d] = 1.0
                m[32 * i + CH, 2 + half, 64 * half + CH * i + d] = 1.0
    return m


def xattn_schedule(has_next, only_lead=False):
    steps = []

    def add(step):
        primed = step[0].endswith("'") or step[0].startswith("project")
        if has_next if primed else not only_lead:
            steps.append(step)

    for q in range(SLOTS + 4):
        if q < SLOTS:
            add(("exp", q))
            n = (q + UNIT_LEAD) // 2
            if q % 2 == 0 and q >= 2 * UNITS_IN_TAIL:
                add(("score", n) if n < 32 else ("score'", n - 32))
        for kind, at in (("maxima", MAXIMA_AT), ("shift", SHIFT_AT)):
            if q in (at, at + 16, at + 32):
                add((kind, (q - at) // 16 + 1))
            if q == at + 48:
                add((kind + "'", 0))
        for w, start in (("q", 12), ("k", 17)):
            if start <= q < start + 5:
                add(("project " + w, q - start))
        if q == 23:
            add(("project v", 0))
        if q >= 5 and (q - 5) % 4 == 0:
            add(("context", (q - 5) // 4))
        if q in (36, SLOTS + 3):
            add(("finish", 0 if q == 36 else 1))
    for n in range(UNITS_IN_TAIL):
        add(("score'", UNIT_LEAD // 2 + n))
    add(("normalise", 0))
    if only_lead:
        steps = [step for step in steps if not step[0].startswith("project")]
    return steps


def cross_attention_masked(core, name, x_src, ctx_src, x_dst, mask, mask_cols, onehot, weights):
    nc = core.nc

    def listed(tag, steps, ring):
        out = []
        for kind, n in steps:
            if kind in ("score", "score'", "project v") or (kind.startswith("project") and n == 0):
                out.append((f"{tag}{kind}{n}", (0, 2)[ring[0] % 2]))
                ring[0] += 1
            elif kind == "exp":
                out.append((f"{tag}exp{n}", 4 + n % 2))
            elif kind in ("shift", "shift'"):
                out.append((f"{tag}{kind}{n}", 7))
            elif kind == "context" and n % 4 == 0:
                out.append((f"{tag}context{n // 4}", 6))
            elif kind == "finish":
                out += [(f"{tag}sum{n}", 7), (f"{tag}y{n}", (0, 2)[ring[0] % 2])]
                ring[0] += 1
        return out

    first_steps = [("project q", k) for k in range(5)] + [("project k", k) for k in range(5)] + [("project v", 0)]
    first_steps += xattn_schedule(True, only_lead=True)
    middle, last = xattn_schedule(True), xattn_schedule(False)
    ring = [0]
    before = BankUses(core.uses, listed("a", first_steps, ring), 1)
    looped = BankUses(before.after, listed("0", middle, ring) + listed("1", middle, ring), TURNS - 1)
    ending = BankUses(looped.after, listed("0", middle, ring) + listed("1", last, ring), 1)
    core.uses = ending.after
    full, free, psum = core.bank_full, core.bank_free, core.psum

    with ExitStack() as ctx:
        core.ctx_stage = ctx

        def sb(tag, shape, dtype=F32):
            return ctx.enter_context(nc.sbuf_tensor(f"{name}_{tag}", shape, dtype))

        def sem(tag):
            return core.semaphore(f"{name}_{tag}")

        norm = Norm(core, name)
        context = sb("context", [P, 2, TT, POS])
        target_mask = sb("target_mask", [P, 2, POS])
        source_mask = sb("source_mask", [P, B, PT])
        mask_rows = sb("mask_rows", [B, POS])
        mask_rest = sb("mask_rest", [B, 2, 2, POS])
        mask_parts = sb("mask_parts", [B, 2, PARTS, POS], BF16)
        gather = sb("gather", [P, 4, P])
        w_q = sb("w_q", [P, TT, SIZE])
        w_k = sb("w_k", [P, TT, SIZE])
        w_v = sb("w_v", [P, TT, SIZE])
        b_q = sb("b_q", [P, TT])
        b_k = sb("b_k", [P, TT])
        b_v = sb("b_v", [P, 2, SIZE])
        whole = sb("whole", [P, TT, POS])
        rest = sb("rest", [P, TT, POS])
        parts = sb("parts", [P, 2, PARTS, TT, POS], BF16)
        stacked = [[sb(f"stacked_{w}{u}", [ROWS, H, POS], BF16) for u in range(2)] for w in "qk"]
        v_biased = sb("v_biased", [P, 2, 2, SIZE])
        v = sb("v", [P, 2, PT, H, 2 * CH])
        minus_max = sb("minus_max", [P, 2, 4, PT])
        max_rest = sb("max_rest", [P, PT, 4])
        max_parts = sb("max_parts", [P, PT, PARTS, 4], BF16)
        max_rows = sb("max_rows", [PARTS * 4, 2, POS], BF16)
        probs = sb("probs", [P, 8, POS])
        heads_out = sb("heads_out", [P, 2, POS])
        inverse = sb("inverse", [P, POS])
        scaled = sb("scaled", [P, POS])
        masked = sb("masked", [P, POS])
        parts_dram = nc.dram_tensor(f"{name}_parts_dram", (2, 2, PARTS, SIZE, POS), BF16).ap()
        mask_dram = nc.dram_tensor(f"{name}_mask_parts_dram", (2, B, len(PAIRS), POS), BF16).ap()
        constants_loaded = sem("constants_loaded")
        masks_loaded = sem("masks_loaded")
        mask_split = sem("mask_split")
        mask_written = sem("mask_written")
        cleared = sem("cleared")
        context_loaded = [sem(f"context_loaded{u}") for u in range(2)]
        part_ready = [sem(f"part{k}_ready") for k in range(PARTS)]
        rest_ready = sem("rest_ready")
        parts_written = sem("parts_written")
        stacked_ready = [[sem(f"stacked_ready_{w}{u}") for u in range(2)] for w in "qk"]
        v_ready = sem("v_ready")
        max_steps = sem("max_steps")
        shift_ready = [sem(f"shift_ready{k}") for k in range(2)]
        context_done = sem("context_done")
        finish_steps = sem("finish_steps")
        finish_z = sem("finish_z")
        NORM_STEPS = 5
        CONSTANTS = 16 * 8

        class At:

            def __init__(self, uses, tag, turn, b, u):
                self.uses, self.tag, self.turn, self.b, self.u = uses, tag, turn, b, u

            def bank(self, use):
                return self.uses.bank(self.tag + use)

            def wait_bank(self, engine, use):
                engine.wait_ge(free[self.bank(use)], self.uses.before(self.tag + use, self.turn) + 1)

            def wait_full(self, engine, use):
                engine.wait_ge(full[self.bank(use)], self.uses.before(self.tag + use, self.turn) + 1)

            def wait_free(self, engine, use):
                engine.wait_ge(free[self.bank(use)], self.uses.before(self.tag + use, self.turn) + 2)

            def pair(self, use):
                return core.banks[:, self.bank(use):self.bank(use) + 2, :]

        def every_sequence(engine, run):
            run(first_steps, At(before, "a", 0, -1, 1), -1, 1)
            with engine.Fori(0, TURNS - 1) as turn:
                for u in range(2):
                    run(middle, At(looped, str(u), turn, turn * 2 + u, u), turn * 2 + u, u)
            for u in range(2):
                b = 2 * (TURNS - 1) + u
                run((middle, last)[u], At(ending, str(u), 0, b, u), b, u)

        block = ctx.enter_context(nc.Block())

        @block.sync
        def _(sp):
            for u in range(2):
                sp.sem_inc(norm.stored[u], 1)
            sp.dma_start(mask_rows[:, :], mask).then_inc(masks_loaded, 16)
            for key, w in (("q", w_q), ("k", w_k), ("v", w_v)):
                sp.dma_start(w[:, :, :], weights[key].rearrange("(c p) n -> p c n", p=P)).then_inc(constants_loaded, 16)

            def load(b, u):
                sp.dma_start(context[:, u], ctx_src[b].rearrange("(j p) d -> p j d", p=P)).then_inc(context_loaded[u], 16)
                sp.dma_start(target_mask[:, u, :], mask[b].unsqueeze(0).broadcast_to([P, POS])).then_inc(context_loaded[u], 16)
                load_x(core, norm, x_src, b, u)

            def store(b, u):
                sp.wait_ge(norm.out_ready, b * TT + TT)
                sp.dma_start(x_dst[b].rearrange("(j p) d -> p j d", p=P), norm.z[:, u]).then_inc(norm.stored[u], 16)

            def stack(w, b, u):
                sp.wait_ge(part_ready[2], b * 2 + (w + 1))
                sp.wait_ge(part_ready[1], b * 2 + (w + 1))
                sp.dma_start(parts_dram[w, u].rearrange("k (c p) s -> p k c s", p=P), parts[:, w]).then_inc(parts_written, 16)
                sp.wait_ge(parts_written, (b * 2 + (w + 1)) * 16)
                for j, pair in enumerate(PAIRS):
                    sp.dma_start(stacked[w][u][CH * j:CH * (j + 1)], parts_dram[w, u, pair[w]].rearrange("(h d) s -> d h s", d=CH))\
                        .then_inc(stacked_ready[w][u], 16)
                if w == 1:
                    sp.wait_ge(cleared, 2)
                sp.dma_start(stacked[w][u][MASK_ROW:MAX_ROW],
                             mask_dram[w, b].unsqueeze(1).broadcast_to([len(PAIRS), H, POS])).then_inc(stacked_ready[w][u], 16)

            load(0, 0)
            sp.wait_ge(mask_split, 7)
            for w in range(2):
                for j, pair in enumerate(PAIRS):
                    sp.dma_start(mask_dram[w, :, j, :], mask_parts[:, w, pair[w], :]).then_inc(mask_written, 16)
            sp.wait_ge(mask_written, 16 * 2 * len(PAIRS))
            stack(0, 0, 0)
            stack(1, 0, 0)
            load(1, 1)

            def turn_of(b, u, count):
                for w in range(2):
                    stack(w, b + 1, 1 - u)
                store(b, u)
                load(b + 2, u)

            with sp.Fori(0, TURNS - 1) as turn:
                for u in range(2):
                    turn_of(turn * 2 + u, u, turn)
            for w in range(2):
                stack(w, B - 1, 1)
            store(B - 2, 0)
            store(B - 1, 1)
            for u in range(2):
                sp.wait_ge(norm.stored[u], 16 * TURNS + 1)

        @block.gpsimd
        def _(pool):
            for u in range(2):
                pool.memset(stacked[1][u][MASK_ROW:ROWS], 1.0).then_inc(cleared, 1)
            for u in range(2):
                pool.wait_ge(cleared, 2 + 2 * u)
                pool.memset(v[:, u, :, :, CH:2 * CH], 0.0).then_inc(cleared, 1)
                pool.wait_ge(cleared, 3 + 2 * u)
                pool.memset(v[:, u, :, :, CH:CH + 1], 1.0).then_inc(cleared, 1)
            with pool.Fori(0, TURNS) as turn:
                for u in range(2):
                    norm_pool(core, norm, turn, u, NORM_STEPS)

        @block.scalar
        def _(act):
            act.dma_start(b_q[:, :], weights["bq"]).then_inc(constants_loaded, 16)
            act.dma_start(b_k[:, :], weights["bk"]).then_inc(constants_loaded, 16)
            act.dma_start(b_v[:, :, :], weights["bv"].rearrange("(a b n) -> a b n", a=1, b=1).broadcast_to([P, 2, SIZE]))\
                .then_inc(constants_loaded, 16)
            act.dma_start(source_mask[:, :, :], mask_cols).then_inc(constants_loaded, 16)
            act.dma_start(gather[:, :, :], onehot).then_inc(constants_loaded, 16)
            act.wait_ge(constants_loaded, CONSTANTS)

            def run(steps, at, b, u):
                for kind, n in steps:
                    if kind == "exp":
                        if n >= 8:
                            c, s = divmod((n - 8) // 4, PT)
                            if s == PT - 1:
                                at.wait_full(act, f"context{c}")
                            else:
                                act.wait_ge(context_done, b * (4 * (PT - 1)) + (c * (PT - 1) + s + 1))
                        at.wait_full(act, f"exp{n}")
                        act.activation(probs[:, n % 8, :], psum[at.bank(f"exp{n}")], ACT.Exp, scale=SCALE)\
                            .then_inc(free[at.bank(f"exp{n}")], 1)
                    if kind in ("shift", "shift'"):
                        owner, to = (b, u) if kind == "shift" else (b + 1, 1 - u)
                        use = f"{kind}{n}"
                        at.wait_full(act, use)
                        act.copy(max_rows[:, n % 2, :], psum[7].bitcast(BF16)[0:PARTS * 4, 0:POS]).then_inc(free[7], 1)
                        at.wait_free(act, use)
                        for k in range(PARTS):
                            act.dma_start(stacked[0][to][MAX_ROW + k:MAX_ROW + k + 1, 4 * n:4 * n + 4, :],
                                          max_rows[4 * k:4 * k + 4, n % 2, :]).then_inc(shift_ready[n % 2], 16)
                    if kind in ("project q", "project k") and n in (1, 3):
                        w, part = "qk".index(kind[-1]), n // 2
                        if part == 0:
                            at.wait_free(act, f"{kind}0")
                        else:
                            act.wait_ge(rest_ready, (b + 1) * 2 + (w + 1))
                        act.copy(parts[:, w, part], (whole, rest)[part][:, :, :]).then_inc(part_ready[part], 1)
                    if kind == "project v":
                        at.wait_free(act, "project v0")
                        act.wait_ge(cleared, 6)
                        for s in range(PT):
                            ins = act.activation(v[:, 1 - u, s, :, 0:CH], v_biased[:, s // 2, s % 2, :].rearrange("p (h d) -> p h d", h=H),
                                                 ACT.Copy, scale=source_mask[:, b + 1, s:s + 1])
                        ins.then_inc(v_ready, 1)
                    if kind == "context" and n % 4 == 3:
                        c = n // 4
                        at.wait_full(act, f"context{c}")
                        act.copy(heads_out[:, c % 2, :], psum[6]).then_inc(free[6], 1)

            every_sequence(act, run)

        @block.vector
        def _(dve):
            dve.wait_ge(masks_loaded, 16)
            dve.tensor_scalar(mask_rest[:, 0, 0], mask_rows[:, :], NEG / SCALE, None, ALU.mult).then_inc(mask_split, 1)
            dve.tensor_scalar(mask_rest[:, 1, 0], mask_rows[:, :], 1.0, None, ALU.subtract).then_inc(mask_split, 1)
            for k in range(PARTS):
                dve.wait_ge(mask_split, 2 + 2 * k)
                dve.tensor_copy(mask_parts[:, :, k, :], mask_rest[:, :, k % 2, :]).then_inc(mask_split, 1)
                if k < PARTS - 1:
                    dve.wait_ge(mask_split, 3 + 2 * k)
                    dve.tensor_tensor(mask_rest[:, :, 1 - k % 2, :], mask_rest[:, :, k % 2, :], mask_parts[:, :, k, :], ALU.subtract)\
                        .then_inc(mask_split, 1)
            dve.wait_ge(constants_loaded, CONSTANTS)

            def run(steps, at, b, u):
                nb = b + 1
                for kind, n in steps:
                    if kind in ("score", "score'"):
                        use, h, c = f"{kind}{n}", n // 2, n // 8
                        at.wait_full(dve, use)
                        dve.tensor_reduce(minus_max[:, c % 2, h % 4, 2 * (n % 2):2 * (n % 2) + 2], at.pair(use), AX.X, ALU.max, negate=True)\
                            .then_inc(free[at.bank(use)], 1)
                    if kind in ("maxima", "maxima'"):
                        owner = b if kind == "maxima" else nb
                        s = (owner * 4 + n) * 4
                        by_tile = minus_max[:, n % 2].rearrange("p h t -> p t h")
                        at.wait_free(dve, f"score{8 * n + 7}" if kind == "maxima" else "score'7")
                        dve.tensor_copy(max_parts[:, :, 0, :], by_tile).then_inc(max_steps, 1)
                        dve.wait_ge(max_steps, s + 1)
                        dve.tensor_tensor(max_rest[:, :, :], by_tile, max_parts[:, :, 0, :], ALU.subtract).then_inc(max_steps, 1)
                        dve.wait_ge(max_steps, s + 2)
                        dve.tensor_copy(max_parts[:, :, 1, :], max_rest[:, :, :]).then_inc(max_steps, 1)
                        dve.wait_ge(max_steps, s + 3)
                        dve.tensor_tensor(max_parts[:, :, 2, :], max_rest[:, :, :], max_parts[:, :, 1, :], ALU.subtract).then_inc(max_steps, 1)
                    if kind in ("project q", "project k"):
                        w = "qk".index(kind[-1])
                        count = nb * 2 + (w + 1)
                        if n == 0:
                            use = f"{kind}0"
                            at.wait_full(dve, use)
                            dve.wait_ge(context_loaded[1 - u], (nb_turns(at, nb)) * 32)
                            for m in range(TT):
                                ins = dve.scalar_tensor_tensor(out=whole[:, m, :], in0=at.pair(use)[:, m, :],
                                                               scalar=(b_q, b_k)[w][:, m:m + 1], in1=target_mask[:, 1 - u, :],
                                                               op0=ALU.add, op1=ALU.mult)
                            ins.then_inc(free[at.bank(use)], 1)
                        if n == 2:
                            dve.wait_ge(part_ready[0], count)
                            dve.tensor_tensor(rest[:, :, :], whole[:, :, :], parts[:, w, 0], ALU.subtract).then_inc(rest_ready, 1)
                        if n == 4:
                            dve.wait_ge(part_ready[1], count)
                            dve.tensor_tensor(parts[:, w, 2], rest[:, :, :], parts[:, w, 1], ALU.subtract).then_inc(part_ready[2], 1)
                            dve.wait_ge(part_ready[2], count)
                    if kind == "project v":
                        use = "project v0"
                        at.wait_full(dve, use)
                        for k in range(2):
                            ins = dve.tensor_tensor(v_biased[:, k], at.pair(use)[:, k, :].rearrange("p (s n) -> p s n", s=2), b_v[:, :, :], ALU.add)
                        ins.then_inc(free[at.bank(use)], 1)
                    if kind == "finish":
                        s = (b * 2 + n) * 2
                        at.wait_full(dve, f"sum{n}")
                        dve.reciprocal(inverse[:, :], psum[7]).then_inc(free[7], 1)
                        use = f"y{n}"
                        at.wait_full(dve, use)
                        at.wait_free(dve, f"sum{n}")
                        dve.tensor_tensor(scaled[:, :], psum[at.bank(use)], inverse[:, :], ALU.mult).then_inc(free[at.bank(use)], 1)
                        at.wait_free(dve, use)
                        dve.tensor_tensor(masked[:, :], scaled[:, :], target_mask[:, u, :], ALU.mult).then_inc(finish_steps, 1)
                        dve.wait_ge(finish_steps, b * 2 + (n + 1))
                        if n == 0:
                            dve.wait_ge(norm.stored[u], stored_before(at, b))
                        dve.tensor_tensor(norm.z[:, u, n, :], masked[:, :], norm.x[:, u, n, :], ALU.add).then_inc(finish_z, 1)
                        dve.wait_ge(finish_z, b * 2 + (n + 1))
                        dve.bn_stats(norm.stats[:, n, :], norm.z[:, u, n, :]).then_inc(norm.moved, 1)
                        if n == 1:
                            m = b * NORM_STEPS
                            dve.wait_ge(norm.moved, m + 2)
                            dve.memset(norm.vareps[:, :], EPS).then_inc(norm.moved, 1)
                            for t in range(TT):
                                ins = dve.bn_aggr(norm.moments[:, t, :], norm.stats[:, t, :])
                            ins.then_inc(norm.moved, 1)
                            dve.wait_ge(norm.moved, m + 4)
                            dve.tensor_scalar(norm.vareps[:, :], norm.moments[:, :, 1], EPS, None, ALU.add).then_inc(norm.moved, 1)
                    if kind == "normalise":
                        for t in range(TT):
                            dve.wait_ge(norm.rstd_ready, b + 1)
                            dve.tensor_scalar(norm.z[:, u, t, :], norm.z[:, u, t, :], norm.moments[:, t, 0:1], norm.rstd[:, t:t + 1],
                                              ALU.subtract, ALU.mult).then_inc(norm.out_ready, 1)

            def nb_turns(at, nb):
                if isinstance(nb, int):
                    return nb // 2 + 1
                return at.turn + (1 if at.u == 0 else 2)

            def stored_before(at, b):
                return (b // 2 if isinstance(b, int) else at.turn) * 16 + 1

            every_sequence(dve, run)

        @block.tensor
        def _(pe):
            pe.wait_ge(constants_loaded, CONSTANTS)

            def parity_count(at, b, ahead):
                if isinstance(b, int):
                    return (b + ahead) // 2 + 1
                return at.turn + (1 if at.u + ahead < 2 else 2)

            def run(steps, at, b, u):
                nb = b + 1
                for kind, n in steps:
                    if kind in ("score", "score'"):
                        use, h = f"{kind}{n}", n // 2
                        ahead = 1 if kind == "score'" else 0
                        to = u ^ ahead
                        at.wait_bank(pe, use)
                        if n == 0:
                            for w in range(2):
                                pe.wait_ge(stacked_ready[w][to], parity_count(at, b, ahead) * 7 * 16)
                        for k in range(2):
                            t = 2 * (n % 2) + k
                            ins = pe.matmul(at.pair(use)[:, k, :], stacked[0][to][0:MAX_ROW, h, t * P:(t + 1) * P],
                                            stacked[1][to][0:MAX_ROW, h, :], start=True, stop=True)
                        ins.then_inc(full[at.bank(use)], 1)
                    if kind in ("shift", "shift'"):
                        owner = b if kind == "shift" else nb
                        use = f"{kind}{n}"
                        at.wait_bank(pe, use)
                        pe.wait_ge(max_steps, (owner * 4 + (n + 1)) * 4)
                        for t in range(PT):
                            ins = pe.transpose(psum[7].bitcast(BF16)[0:PARTS * 4, t * P:(t + 1) * P],
                                               max_parts[:, t].rearrange("p k h -> p (k h)"), core.ident_bf[:, :])
                        ins.then_inc(full[7], 1)
                    if kind == "exp":
                        use, c, s, h = f"exp{n}", n // 16, n % 16 // 4, n // 16 * 4 + n % 4
                        at.wait_bank(pe, use)
                        if n % 16 == 0:
                            pe.wait_ge(shift_ready[c % 2], (b * 2 + (c // 2 + 1)) * PARTS * 16)
                        ins = pe.matmul(psum[at.bank(use)], stacked[1][u][:, h, s * P:(s + 1) * P], stacked[0][u][:, h, :], start=True, stop=True)
                        ins.then_inc(full[at.bank(use)], 1)
                    if kind == "context":
                        c, s = n // 4, n % 4
                        if s == 0:
                            at.wait_bank(pe, f"context{c}")
                        if n == 0:
                            pe.wait_ge(v_ready, b + 1)
                        for i in (2, 3):
                            at.wait_free(pe, f"exp{4 * n + i}")
                        for i in range(4):
                            ins = pe.matmul(psum[6][32 * i:32 * i + 32, :], v[:, u, s, 4 * c + i, :], probs[:, (4 * n + i) % 8, :],
                                            start=s == 0, stop=s == PT - 1)
                        ins.then_inc(full[6] if s == PT - 1 else context_done, 1)
                    if kind in ("project q", "project k") and n == 0:
                        w, use = "qk".index(kind[-1]), f"{kind}0"
                        at.wait_bank(pe, use)
                        if w == 0:
                            pe.wait_ge(norm.loaded[1 - u], parity_count(at, b, 1) * 16)
                        else:
                            pe.wait_ge(context_loaded[1 - u], parity_count(at, b, 1) * 32)
                        src = (norm.x, context)[w]
                        for m in range(TT):
                            for c in range(TT):
                                ins = pe.matmul(at.pair(use)[:, m, :], (w_q, w_k)[w][:, c, m * P:(m + 1) * P], src[:, 1 - u, c, :],
                                                start=c == 0, stop=c == TT - 1)
                        ins.then_inc(full[at.bank(use)], 1)
                    if kind == "project v":
                        use = "project v0"
                        at.wait_bank(pe, use)
                        for s in range(PT):
                            for c in range(TT):
                                ins = pe.matmul(at.pair(use)[:, s // 2, s % 2 * SIZE:(s % 2 + 1) * SIZE], context[:, 1 - u, c, s * P:(s + 1) * P],
                                                w_v[:, c, :], start=c == 0, stop=c == TT - 1)
                        ins.then_inc(full[at.bank(use)], 1)
                    if kind == "finish":
                        at.wait_bank(pe, f"sum{n}")
                        at.wait_free(pe, f"context{2 * n + 1}")
                        for half in range(2):
                            ins = pe.matmul(psum[7], gather[:, 2 + half, :], heads_out[:, half, :], start=half == 0, stop=half == 1)
                        ins.then_inc(full[7], 1)
                        at.wait_bank(pe, f"y{n}")
                        for half in range(2):
                            ins = pe.matmul(psum[at.bank(f"y{n}")], gather[:, half, :], heads_out[:, half, :], start=half == 0, stop=half == 1)
                        ins.then_inc(full[at.bank(f"y{n}")], 1)

            every_sequence(pe, run)



E = 8
RL = 8
F0 = 1376
FT = -(-F0 // P)
NL = (E + 1) * RL
NLP = 96
AHEAD = 3


def ffn0_layout(inputs):
    import numpy as np

    def tall(name):
        a = np.asarray(inputs[f"L0_ffn_A_{name}"])
        return np.concatenate([a.transpose(1, 0, 2).reshape(a.shape[1], E * RL),
                               np.asarray(inputs[f"L0_ffn_sA_{name}"])], axis=1)

    def wide(name):
        b = np.asarray(inputs[f"L0_ffn_B_{name}"])
        whole = np.zeros((NLP, b.shape[2]), b.dtype)
        whole[0:E * RL] = b.reshape(E * RL, b.shape[2])
        whole[E * RL:NL] = np.asarray(inputs[f"L0_ffn_sB_{name}"])
        return whole

    down = np.zeros((F0, NLP), np.asarray(inputs["L0_ffn_A_down"]).dtype)
    down[:, 0:NL] = tall("down")
    return {
        "first": np.concatenate([tall("gate"), tall("up"), np.asarray(inputs["L0_ffn_W_router"])], axis=1),
        "gate": np.asarray(inputs["L0_ffn_W_gate"]), "up": np.asarray(inputs["L0_ffn_W_up"]),
        "down": np.asarray(inputs["L0_ffn_W_down"]), "B_gate": wide("gate"), "B_up": wide("up"),
        "A_down": down, "B_down": wide("down"), "bias": np.asarray(inputs["L0_ffn_expert_bias"]),
    }


def feed_forward_lora(core, name, x_src, x_dst, weights):
    nc = core.nc
    FIRST = 2 * NL + E
    ring = [6, 7, 0, 3, 1, 2, 4, 5, 6, 7, 0]
    turn_uses = []
    for u in range(2):
        turn_uses += [(f"xT0.{u}", 0), (f"xT1.{u}", 3), (f"low.{u}", 4)]
        turn_uses += [(f"h{j}.{u}", ring[j]) for j in range(AHEAD)]
        turn_uses += [(f"lowT.{u}", 5)]
        turn_uses += [(f"h{j}.{u}", ring[j]) for j in range(AHEAD, FT)]
        turn_uses += [(f"hA.{u}", 3), (f"hAT.{u}", 4), (f"y0.{u}", 1), (f"y1.{u}", 2)]
    uses = BankUses(core.uses, turn_uses, TURNS)
    core.uses = uses.after
    full, free, psum = core.bank_full, core.bank_free, core.psum

    with ExitStack() as ctx:
        core.ctx_stage = ctx

        def sb(tag, shape, dtype=F32):
            return ctx.enter_context(nc.sbuf_tensor(f"{name}_{tag}", shape, dtype))

        def sem(tag):
            return core.semaphore(f"{name}_{tag}")

        norm = Norm(core, name)
        w_first = sb("w_first", [P, KC, FIRST])
        w_gate = sb("w_gate", [P, KC, F0])
        w_up = sb("w_up", [P, KC, F0])
        w_down = sb("w_down", [P, FT, D])
        b_gate = sb("b_gate", [NLP, F0])
        b_up = sb("b_up", [NLP, F0])
        b_down = sb("b_down", [NLP, D])
        a_down = sb("a_down", [P, FT, NLP])
        bias = sb("bias", [P, E])
        order = sb("order", [P, E])
        gate_rest = sb("gate_rest", [P, KC, F0])
        up_rest = sb("up_rest", [P, KC, F0])
        PART = 2 * P
        raw_gate = sb("raw_gate", [P, 2, KC, PART])
        raw_up = sb("raw_up", [P, 2, KC, PART])
        xT = sb("xT", [P, KC, T])
        x_high = sb("x_high", [P, KC, T])
        x_rest = sb("x_rest", [P, KC, T])
        scores = sb("scores", [P, TT, E])
        biased = sb("biased", [P, TT, E])
        rank = sb("rank", [P, TT, E])
        top = sb("top", [P, TT])
        chosen = sb("chosen", [P, 2, TT, E])
        share = sb("share", [P, TT, E])
        total = sb("total", [P, TT])
        low = sb("low", [P, TT, 2, NLP])
        lowT = sb("lowT", [NLP, 2, T])
        silu = sb("silu", [P, 3, T])
        hT = sb("hT", [P, FT, T])
        hA = sb("hA", [P, TT, NLP])
        hAT = sb("hAT", [NLP, T])
        first_loaded = sem("first_loaded")
        raw_loaded = [sem(f"raw_loaded{k}") for k in range(2)]
        low_loaded = sem("low_loaded")
        down_loaded = sem("down_loaded")
        weight_steps = sem("weight_steps")
        gate_split = sem("gate_split")
        up_split = sem("up_split")
        x_steps = sem("x_steps")
        padded = sem("padded")
        scored = sem("scored")
        routed = sem("routed")
        silu_ready = sem("silu_ready")
        ROUTE = 19
        PARTS_OF_W = -(-F0 // PART)
        whole = (FT - 1) * P

        def wait_bank(engine, use, turn):
            engine.wait_ge(free[uses.bank(use)], uses.before(use, turn) + 1)

        def wait_full(engine, use, turn):
            engine.wait_ge(full[uses.bank(use)], uses.before(use, turn) + 1)

        def wait_free(engine, use, turn):
            engine.wait_ge(free[uses.bank(use)], uses.before(use, turn) + 2)

        def columns(k):
            return slice(k * PART, min((k + 1) * PART, F0))

        def width(j):
            return P if j < FT - 1 else F0 - whole

        block = ctx.enter_context(nc.Block())

        @block.sync
        def _(sp):
            rows_in_and_out(core, norm, uses, x_src, x_dst)

        @block.gpsimd
        def _(pool):
            pool.memset(low[:, :, :, :], 0.0).then_inc(padded, 1)
            pool.memset(hA[:, :, :], 0.0).then_inc(padded, 1)
            pool.iota(order[:, :], pattern=[[-1, E]], base=E, channel_multiplier=0,
                      allow_small_or_imprecise_dtypes=True).then_inc(padded, 1)

            def load_part(k):
                n = columns(k).stop - columns(k).start
                for key, raw in (("gate", raw_gate), ("up", raw_up)):
                    pool.dma_start(raw[:, k % 2, :, 0:n], weights[key].rearrange("(c p) n -> p c n", p=P)[:, :, columns(k)])\
                        .then_inc(raw_loaded[k % 2], 16)

            load_part(0)
            load_part(1)
            for k in range(PARTS_OF_W):
                cols, n = columns(k), columns(k).stop - columns(k).start
                pool.wait_ge(weight_steps, 2 * k + 2)
                subtract(pool, up_rest[:, :, cols], raw_up[:, k % 2, :, 0:n], w_up[:, :, cols]).then_inc(up_split, 1)
                if k + 2 < PARTS_OF_W:
                    pool.wait_ge(up_split, k + 1)
                    pool.wait_ge(gate_split, k + 1)
                    load_part(k + 2)
            with pool.Fori(0, TURNS) as turn:
                for u in range(2):
                    norm_pool(core, norm, turn, u)

        @block.scalar
        def _(act):
            act.dma_start(w_first[:, :, :], weights["first"].rearrange("(c p) n -> p c n", p=P)).then_inc(first_loaded, 16)
            act.dma_start(bias[:, :], weights["bias"].rearrange("(a e) -> a e", a=1).broadcast_to([P, E])).then_inc(first_loaded, 16)
            for key, w in (("B_gate", b_gate), ("B_up", b_up)):
                act.dma_start(w[:, :], weights[key]).then_inc(low_loaded, 16)
            act.dma_start(a_down[:, 0:FT - 1, :], weights["A_down"][0:whole].rearrange("(c p) n -> p c n", p=P)).then_inc(down_loaded, 16)
            act.dma_start(a_down[0:F0 - whole, FT - 1, :], weights["A_down"][whole:F0]).then_inc(down_loaded, 16)
            act.dma_start(w_down[:, 0:FT - 1, :], weights["down"][0:whole].rearrange("(c p) n -> p c n", p=P)).then_inc(down_loaded, 16)
            act.dma_start(w_down[0:F0 - whole, FT - 1, :], weights["down"][whole:F0]).then_inc(down_loaded, 16)
            act.dma_start(b_down[:, :], weights["B_down"]).then_inc(down_loaded, 16)
            with act.Fori(0, TURNS) as turn:
                for u in range(2):
                    for j in range(2):
                        use = f"xT{j}.{u}"
                        wait_full(act, use, turn)
                        act.copy(xT[:, 2 * j:2 * j + 2, :], psum[uses.bank(use)][:, :].rearrange("p (c t) -> p c t", c=2))\
                            .then_inc(free[uses.bank(use)], 1)
                    wait_full(act, f"low.{u}", turn)
                    act.activation(scores[:, :, :],
                                   psum[uses.bank(f"low.{u}")][:, :].rearrange("p (t n) -> p t n", t=TT)[:, :, 2 * NL:FIRST],
                                   ACT.Sigmoid).then_inc(scored, 1)
                    use = f"lowT.{u}"
                    wait_full(act, use, turn)
                    act.copy(lowT[:, :, :], psum[uses.bank(use)][0:NLP, :].rearrange("p (g t) -> p g t", g=2))\
                        .then_inc(free[uses.bank(use)], 1)
                    for j in range(FT):
                        use, m = f"h{j}.{u}", width(j)
                        wait_full(act, use, turn)
                        if j >= 3:
                            wait_free(act, f"h{j - 3}.{u}", turn)
                        act.activation(silu[0:m, j % 3, :], psum[uses.bank(use)][0:m, 0:T], ACT.Silu).then_inc(silu_ready, 1)
                    use = f"hAT.{u}"
                    wait_full(act, use, turn)
                    act.copy(hAT[:, :], psum[uses.bank(use)][0:NLP, 0:T]).then_inc(free[uses.bank(use)], 1)

        @block.vector
        def _(dve):
            dve.wait_ge(padded, 3)
            dve.wait_ge(first_loaded, 32)
            for k in range(PARTS_OF_W):
                cols, n = columns(k), columns(k).stop - columns(k).start
                dve.wait_ge(raw_loaded[k % 2], 32 * (k // 2 + 1))
                high_part(dve, w_gate[:, :, cols], raw_gate[:, k % 2, :, 0:n]).then_inc(weight_steps, 1)
                high_part(dve, w_up[:, :, cols], raw_up[:, k % 2, :, 0:n]).then_inc(weight_steps, 1)
                dve.wait_ge(weight_steps, 2 * k + 1)
                subtract(dve, gate_rest[:, :, cols], raw_gate[:, k % 2, :, 0:n], w_gate[:, :, cols]).then_inc(gate_split, 1)
            with dve.Fori(0, TURNS) as turn:
                for u in range(2):
                    b = turn * 2 + u

                    def step(ins, n):
                        ins.then_inc(routed, 1)
                        if n < ROUTE:
                            dve.wait_ge(routed, b * ROUTE + n)

                    def per_row(a):
                        return a.unsqueeze(2).broadcast_to([P, TT, E])

                    for j in range(2):
                        wait_free(dve, f"xT{j}.{u}", turn)
                    high_part(dve, x_high[:, :, :], xT[:, :, :]).then_inc(x_steps, 1)
                    dve.wait_ge(x_steps, b * 2 + 1)
                    subtract(dve, x_rest[:, :, :], xT[:, :, :], x_high[:, :, :]).then_inc(x_steps, 1)
                    dve.wait_ge(scored, b + 1)
                    step(dve.tensor_tensor(biased[:, :, :], scores[:, :, :],
                                           bias[:, :].unsqueeze(1).broadcast_to([P, TT, E]), ALU.add), 1)
                    for k in range(2):
                        s = 1 + 6 * k
                        step(dve.tensor_reduce(top[:, :], biased[:, :, :], AX.X, ALU.max), s + 1)
                        step(dve.tensor_tensor(rank[:, :, :], biased[:, :, :], per_row(top[:, :]), ALU.is_equal), s + 2)
                        step(dve.tensor_tensor(rank[:, :, :], rank[:, :, :],
                                               order[:, :].unsqueeze(1).broadcast_to([P, TT, E]), ALU.mult), s + 3)
                        step(dve.tensor_reduce(top[:, :], rank[:, :, :], AX.X, ALU.max), s + 4)
                        step(dve.tensor_tensor(chosen[:, k], rank[:, :, :], per_row(top[:, :]), ALU.is_equal), s + 5)
                        if k == 0:
                            step(dve.scalar_tensor_tensor(out=biased[:, :, :], in0=chosen[:, 0], scalar=-1e30,
                                                          in1=biased[:, :, :], op0=ALU.mult, op1=ALU.add), s + 6)
                        else:
                            step(dve.tensor_tensor(share[:, :, :], chosen[:, 0], chosen[:, 1], ALU.add), s + 6)
                    step(dve.tensor_tensor(share[:, :, :], share[:, :, :], scores[:, :, :], ALU.mult), 14)
                    step(dve.tensor_reduce(total[:, :], share[:, :, :], AX.X, ALU.add), 15)
                    step(dve.tensor_scalar(total[:, :], total[:, :], 1e-8, float(RL), ALU.add, ALU.mult), 16)
                    step(dve.reciprocal(total[:, :], total[:, :]), 17)
                    step(dve.tensor_tensor(share[:, :, :], share[:, :, :], per_row(total[:, :]), ALU.mult), 18)
                    use = f"low.{u}"
                    bank = psum[uses.bank(use)]
                    wait_full(dve, use, turn)
                    for t in range(TT):
                        dve.tensor_tensor(low[:, t, :, 0:E * RL].rearrange("p g (e r) -> p g e r", r=RL),
                                          bank[:, t * T:t * T + 2 * NL].rearrange("p (g n) -> p g n", g=2)[:, :, 0:E * RL]
                                          .rearrange("p g (e r) -> p g e r", r=RL),
                                          share[:, t, :].unsqueeze(1).unsqueeze(3).broadcast_to([P, 2, E, RL]), ALU.mult)
                        ins = dve.tensor_scalar(low[:, t, :, E * RL:NL],
                                                bank[:, t * T:t * T + 2 * NL].rearrange("p (g n) -> p g n", g=2)[:, :, E * RL:NL],
                                                1.0 / RL, None, ALU.mult)
                        if t == 0:
                            step(ins, ROUTE)
                    ins.then_inc(free[uses.bank(use)], 1)
                    for j in range(FT):
                        use, m = f"h{j}.{u}", width(j)
                        dve.wait_ge(silu_ready, b * FT + (j + 1))
                        dve.tensor_tensor(hT[0:m, j, :], psum[uses.bank(use)][0:m, T:2 * T], silu[0:m, j % 3, :], ALU.mult)\
                            .then_inc(free[uses.bank(use)], 1)
                    use = f"hA.{u}"
                    wait_full(dve, use, turn)
                    bank = psum[uses.bank(use)][:, 0:TT * NLP].rearrange("p (t n) -> p t n", t=TT)
                    dve.tensor_tensor(hA[:, :, 0:E * RL].rearrange("p t (e r) -> p t e r", r=RL),
                                      bank[:, :, 0:E * RL].rearrange("p t (e r) -> p t e r", r=RL),
                                      share[:, :, :].unsqueeze(3).broadcast_to([P, TT, E, RL]), ALU.mult)
                    dve.tensor_scalar(hA[:, :, E * RL:NL], bank[:, :, E * RL:NL], 1.0 / RL, None, ALU.mult)\
                        .then_inc(free[uses.bank(use)], 1)
                    norm_dve(core, norm, uses, turn, u)

        @block.tensor
        def _(pe):
            pe.wait_ge(first_loaded, 32)
            with pe.Fori(0, TURNS) as turn:
                for u in range(2):
                    def done(ins, use):
                        ins.then_inc(full[uses.bank(use)], 1)

                    pe.wait_ge(norm.loaded[u], turn * 16 + 16)
                    for j in range(2):
                        use = f"xT{j}.{u}"
                        wait_bank(pe, use, turn)
                        for c in range(2):
                            for t in range(TT):
                                d = 2 * j + c
                                ins = pe.transpose(psum[uses.bank(use)][:, (c * TT + t) * P:(c * TT + t + 1) * P],
                                                   norm.x[:, u, t, d * P:(d + 1) * P], core.ident[:, :])
                        done(ins, use)
                    for j in range(2):
                        wait_free(pe, f"xT{j}.{u}", turn)
                    use = f"low.{u}"
                    wait_bank(pe, use, turn)
                    for t in range(TT):
                        for c in range(KC):
                            ins = pe.matmul(psum[uses.bank(use)][:, t * T:t * T + FIRST], xT[:, c, t * P:(t + 1) * P],
                                            w_first[:, c, :], start=c == 0, stop=c == KC - 1)
                    done(ins, use)

                    def dense(j):
                        use, m = f"h{j}.{u}", width(j)
                        if j % 2 == 0:
                            pe.wait_ge(gate_split, j // 2 + 1)
                            pe.wait_ge(up_split, j // 2 + 1)
                        if j == 0:
                            pe.wait_ge(x_steps, turn * 4 + (2 * u + 2))
                        wait_bank(pe, use, turn)
                        cols = slice(j * P, j * P + m)
                        for g, (high, rest) in enumerate(((w_gate, gate_rest), (w_up, up_rest))):
                            for c in range(KC):
                                split_matmul(pe, psum[uses.bank(use)][0:m, g * T:(g + 1) * T], (high[:, c, cols], rest[:, c, cols]),
                                             (x_high[:, c, :], x_rest[:, c, :]), start=g == 0 and c == 0, stop=False,
                                             skip_group_check=True)

                    def low_rank(j):
                        use, m = f"h{j}.{u}", width(j)
                        if j == 0:
                            pe.wait_ge(low_loaded, 32)
                        for g, w in enumerate((b_gate, b_up)):
                            ins = pe.matmul(psum[uses.bank(use)][0:m, g * T:(g + 1) * T], w[:, j * P:j * P + m], lowT[:, g, :],
                                            start=False, stop=True, skip_group_check=True)
                        done(ins, use)

                    for j in range(AHEAD):
                        dense(j)
                    use = f"lowT.{u}"
                    wait_bank(pe, use, turn)
                    wait_free(pe, f"low.{u}", turn)
                    for g in range(2):
                        for t in range(TT):
                            ins = pe.transpose(psum[uses.bank(use)][0:NLP, g * T + t * P:g * T + (t + 1) * P], low[:, t, g, :], core.ident[:, :])
                    done(ins, use)
                    wait_free(pe, use, turn)
                    for j in range(AHEAD):
                        low_rank(j)
                    for j in range(AHEAD, FT):
                        dense(j)
                        low_rank(j)
                    use = f"hA.{u}"
                    wait_bank(pe, use, turn)
                    pe.wait_ge(down_loaded, 80)
                    wait_free(pe, f"h{FT - 1}.{u}", turn)
                    for t in range(TT):
                        for j in range(FT):
                            m = width(j)
                            ins = pe.matmul(psum[uses.bank(use)][:, t * NLP:(t + 1) * NLP], hT[0:m, j, t * P:(t + 1) * P],
                                            a_down[0:m, j, :], start=j == 0, stop=j == FT - 1)
                    done(ins, use)
                    for t in range(TT):
                        use = f"y{t}.{u}"
                        if t == 0:
                            wait_bank(pe, "hAT." + str(u), turn)
                        wait_bank(pe, use, turn)
                        for j in range(FT):
                            m = width(j)
                            pe.matmul(psum[uses.bank(use)][:, :], hT[0:m, j, t * P:(t + 1) * P], w_down[0:m, j, :],
                                      start=j == 0, stop=False, skip_group_check=True)
                        if t == 0:
                            wait_free(pe, f"hA.{u}", turn)
                            for k in range(TT):
                                ins = pe.transpose(psum[uses.bank(f"hAT.{u}")][0:NLP, k * P:(k + 1) * P], hA[:, k, :], core.ident[:, :])
                            done(ins, f"hAT.{u}")
                            wait_free(pe, f"hAT.{u}", turn)
                        ins = pe.matmul(psum[uses.bank(use)][:, :], hAT[:, t * P:(t + 1) * P], b_down[:, :], start=False, stop=True,
                                        skip_group_check=True)
                        done(ins, use)



HD = 128
G = 4
HG = H // G
S1 = 256
QUEUE = 3


def cross_attention_grouped(core, name, x_src, ctxT_src, x_dst, weights):
    nc = core.nc
    turn_uses = []
    for u in range(2):
        turn_uses += [(f"xT0.{u}", 0), (f"xT1.{u}", 1), (f"q0_0.{u}", 2), (f"q0_1.{u}", 3), (f"k0.{u}", 4), (f"k1.{u}", 5),
                      (f"v0.{u}", 6), (f"v1.{u}", 7), (f"kT0.{u}", 4), (f"kT1.{u}", 5), (f"qT0_0.{u}", 0), (f"qT0_1.{u}", 1)]
        for s in range(H + 2):
            if s < H:
                turn_uses.append((f"S{s}.{u}", 2 + s % 2))
                if s < H - HG:
                    turn_uses.append(((f"q{s // HG + 1}_{s % HG}.{u}", s % HG) if s % HG < 2
                                      else (f"qT{s // HG + 1}_{s % HG - 2}.{u}", s % HG - 2)))
            if 1 <= s <= H:
                turn_uses.append((f"T{s - 1}.{u}", 4 + (s - 1) % 2))
            if s >= 2:
                turn_uses += [(f"R{s - 2}.{u}", 7), (f"O{s - 2}.{u}", 6)]
        turn_uses += [(f"y0.{u}", 2), (f"y1.{u}", 3)]
    uses = BankUses(core.uses, turn_uses, TURNS)
    core.uses = uses.after
    full, free, psum = core.bank_full, core.bank_free, core.psum

    with ExitStack() as ctx:
        core.ctx_stage = ctx

        def sb(tag, shape, dtype=F32):
            return ctx.enter_context(nc.sbuf_tensor(f"{name}_{tag}", shape, dtype))

        def sem(tag):
            return core.semaphore(f"{name}_{tag}")

        norm = Norm(core, name)
        w_q = sb("w_q", [P, KC, H * HD])
        w_k = sb("w_k", [P, KC, G * HD])
        w_v = sb("w_v", [P, KC, G * HD])
        w_o = sb("w_o", [P, H, D])
        gains = sb("gains", [P, 2])
        gain = sb("gain", [P, 1])
        context = sb("context", [P, 2, KC, S1])
        xT = sb("xT", [P, KC, T])
        squares = sb("squares", [P, QUEUE, 512])
        square_sums = sb("square_sums", [P, 5, HG, TT])
        mean_squares = sb("mean_squares", [P, 5, HG, TT])
        rroot = sb("rroot", [P, 5, HG, TT])
        q_rows = sb("q_rows", [P, 2, TT, HG * HD])
        qT = sb("qT", [P, 2, HG, T])
        k_rows = sb("k_rows", [P, TT, G * HD])
        kT = sb("kT", [P, G, S1])
        v = sb("v", [P, TT, G * HD])
        row_max = sb("row_max", [P, H, TT])
        minus_max = sb("minus_max", [P, H, TT])
        probs = sb("probs", [P, QUEUE, TT, S1])
        probsT = sb("probsT", [P, QUEUE, TT, T])
        sums = sb("sums", [P, H, TT])
        inverse = sb("inverse", [P, H, TT])
        inverse_rows = sb("inverse_rows", [P, QUEUE, TT, P])
        spread = sb("spread", [P, 2, T])
        ctxT = sb("ctxT", [P, H, T])
        q_weights = [sem(f"q_weights{k}") for k in range(2)]
        kv_weights = sem("kv_weights")
        o_weights = sem("o_weights")
        gain_ready = sem("gain_ready")
        context_loaded = [sem(f"context_loaded{u}") for u in range(2)]
        squared = sem("squared")
        summed = sem("summed")
        mean_ready = sem("mean_ready")
        rroot_ready = sem("rroot_ready")
        max_found = sem("max_found")
        max_ready = sem("max_ready")
        inverted = sem("inverted")
        inverse_spread = sem("inverse_spread")

        def wait_bank(engine, use, turn):
            engine.wait_ge(free[uses.bank(use)], uses.before(use, turn) + 1)

        def wait_full(engine, use, turn):
            engine.wait_ge(full[uses.bank(use)], uses.before(use, turn) + 1)

        def wait_free(engine, use, turn):
            engine.wait_ge(free[uses.bank(use)], uses.before(use, turn) + 2)

        block = ctx.enter_context(nc.Block())

        @block.sync
        def _(sp):
            def load_context(b, u):
                sp.dma_start(context[:, u], ctxT_src[b].rearrange("(c p) s -> p c s", p=P)).then_inc(context_loaded[u], 16)

            rows_in_and_out(core, norm, uses, x_src, x_dst, load_context,
                            lambda turn, u: wait_full(sp, f"v1.{u}", turn))

        @block.gpsimd
        def _(pool):
            with pool.Fori(0, TURNS) as turn:
                for u in range(2):
                    for n, part in enumerate((0, 4, 1, 2, 3)):
                        pool.wait_ge(mean_ready, (turn * 2 + u) * 5 + (n + 1))
                        pool.tensor_tensor(rroot[:, part], mean_squares[:, part],
                                           core.minus_half[:, 0:HG * TT].rearrange("p (h t) -> p h t", t=TT), ALU.pow)\
                            .then_inc(rroot_ready, 1)
                    norm_pool(core, norm, turn, u)

        @block.scalar
        def _(act):
            wq = weights["q"].rearrange("(c p) n -> p c n", p=P)
            act.dma_start(w_q[:, :, 0:512], wq[:, :, 0:512]).then_inc(q_weights[0], 16)
            act.dma_start(gains[:, 0:1], weights["qn"].rearrange("(p a) -> p a", a=1)).then_inc(kv_weights, 16)
            act.dma_start(gains[:, 1:2], weights["kn"].rearrange("(p a) -> p a", a=1)).then_inc(kv_weights, 16)
            act.dma_start(w_k[:, :, :], weights["k"].rearrange("(c p) n -> p c n", p=P)).then_inc(kv_weights, 16)
            act.dma_start(w_v[:, :, :], weights["v"].rearrange("(c p) n -> p c n", p=P)).then_inc(kv_weights, 16)
            act.dma_start(w_q[:, :, 512:], wq[:, :, 512:]).then_inc(q_weights[1], 16)
            act.dma_start(w_o[:, :, :], weights["o"].rearrange("(c p) n -> p c n", p=P)).then_inc(o_weights, 16)
            act.wait_ge(gain_ready, 2)
            with act.Fori(0, TURNS) as turn:
                for u in range(2):
                    b = turn * 2 + u

                    def square(use, n):
                        wait_full(act, use, turn)
                        if n < QUEUE:
                            act.wait_ge(summed, b * 10 + 1)
                        else:
                            act.wait_ge(summed, b * 10 + (n - QUEUE + 2))
                        return act.activation(squares[:, n % QUEUE, :], psum[uses.bank(use)][:, :], ACT.Square).then_inc(squared, 1)

                    def q_out(g, t, n):
                        use = f"q{g}_{t}.{u}"
                        square(use, n)
                        act.copy(q_rows[:, g % 2, t, :], psum[uses.bank(use)][:, :]).then_inc(free[uses.bank(use)], 1)

                    def qT_out(g, j):
                        use = f"qT{g}_{j}.{u}"
                        wait_full(act, use, turn)
                        act.copy(qT[:, g % 2, 2 * j:2 * j + 2, :], psum[uses.bank(use)][:, :].rearrange("p (h t) -> p h t", h=2))\
                            .then_inc(free[uses.bank(use)], 1)

                    for j in range(2):
                        use = f"xT{j}.{u}"
                        wait_full(act, use, turn)
                        act.copy(xT[:, 2 * j:2 * j + 2, :], psum[uses.bank(use)][:, :].rearrange("p (c t) -> p c t", c=2))\
                            .then_inc(free[uses.bank(use)], 1)
                    q_out(0, 0, 0)
                    q_out(0, 1, 1)
                    square(f"k0.{u}", 2)
                    square(f"k1.{u}", 3)
                    for t in range(TT):
                        use = f"v{t}.{u}"
                        wait_full(act, use, turn)
                        act.copy(v[:, t, :], psum[uses.bank(use)][:, :]).then_inc(free[uses.bank(use)], 1)
                    for j in range(2):
                        use = f"kT{j}.{u}"
                        wait_full(act, use, turn)
                        act.activation(kT[:, 2 * j:2 * j + 2, :], psum[uses.bank(use)][:, :].rearrange("p (h t) -> p h t", h=2),
                                       ACT.Copy, scale=gain[:, 0:1]).then_inc(free[uses.bank(use)], 1)
                    for j in range(2):
                        qT_out(0, j)
                    for s in range(H + 2):
                        if s < H:
                            use = f"S{s}.{u}"
                            act.wait_ge(max_ready, b * H + (s + 1))
                            if s >= QUEUE:
                                wait_full(act, f"T{s - QUEUE}.{u}", turn)
                            for t in range(TT):
                                ins = act.activation(probs[:, s % QUEUE, t, :], psum[uses.bank(use)][:, t * S1:(t + 1) * S1], ACT.Exp,
                                                     bias=minus_max[:, s, t:t + 1], scale=rroot[:, s // HG, s % HG, t:t + 1],
                                                     accum_out=sums[:, s, t:t + 1])
                            ins.then_inc(free[uses.bank(use)], 1)
                            if s < H - HG:
                                g, i = s // HG + 1, s % HG
                                if i < 2:
                                    q_out(g, i, 4 + 2 * (g - 1) + i)
                                else:
                                    qT_out(g, i - 2)
                        if s >= 2:
                            use = f"R{s - 2}.{u}"
                            wait_full(act, use, turn)
                            if s >= 4:
                                wait_free(act, f"O{s - 4}.{u}", turn)
                            act.copy(spread[:, s % 2, :], psum[uses.bank(use)][:, 0:T]).then_inc(free[uses.bank(use)], 1)

        @block.vector
        def _(dve):
            dve.sem_inc(summed, 1)
            dve.wait_ge(kv_weights, 64)
            dve.tensor_tensor(gain[:, :], gains[:, 0:1], gains[:, 1:2], ALU.mult).then_inc(gain_ready, 1)
            dve.wait_ge(gain_ready, 1)
            dve.tensor_scalar(gain[:, :], gain[:, :], float(HD) ** -0.5, None, ALU.mult).then_inc(gain_ready, 1)
            with dve.Fori(0, TURNS) as turn:
                for u in range(2):
                    b = turn * 2 + u

                    def sum_squares(part, t, n):
                        dve.wait_ge(squared, b * 10 + (n + 1))
                        dve.tensor_reduce(square_sums[:, part, :, t], squares[:, n % QUEUE, :].rearrange("p (h d) -> p h d", h=HG),
                                          AX.X, ALU.add).then_inc(summed, 1)

                    def mean_square(part, n):
                        dve.wait_ge(summed, b * 10 + n + 1)
                        dve.tensor_scalar(mean_squares[:, part], square_sums[:, part], 1.0 / HD, 1e-6, ALU.mult, ALU.add)\
                            .then_inc(mean_ready, 1)

                    sum_squares(0, 0, 0)
                    sum_squares(0, 1, 1)
                    mean_square(0, 2)
                    sum_squares(4, 0, 2)
                    sum_squares(4, 1, 3)
                    mean_square(4, 4)
                    for t in range(TT):
                        use = f"k{t}.{u}"
                        dve.wait_ge(rroot_ready, b * 5 + 2)
                        dve.tensor_tensor(k_rows[:, t, :].rearrange("p (h d) -> p h d", h=G),
                                          psum[uses.bank(use)][:, :].rearrange("p (h d) -> p h d", h=G),
                                          rroot[:, 4, :, t].unsqueeze(2).broadcast_to([P, G, HD]), ALU.mult)\
                            .then_inc(free[uses.bank(use)], 1)
                    for s in range(H + 2):
                        if s < H:
                            use = f"S{s}.{u}"
                            wait_full(dve, use, turn)
                            dve.tensor_reduce(row_max[:, s, :], psum[uses.bank(use)][:, :].rearrange("p (t s) -> p t s", t=TT),
                                              AX.X, ALU.max).then_inc(max_found, 1)
                            dve.wait_ge(max_found, b * H + (s + 1))
                            if s % HG == 0:
                                g = s // HG
                                dve.wait_ge(rroot_ready, b * 5 + (1 if g == 0 else g + 2))
                            dve.scalar_tensor_tensor(out=minus_max[:, s, :], in0=row_max[:, s, :], scalar=-1.0,
                                                     in1=rroot[:, s // HG, s % HG, :], op0=ALU.mult, op1=ALU.mult)\
                                .then_inc(max_ready, 1)
                            if s < H - HG:
                                g, i = s // HG + 1, s % HG
                                if i < 2:
                                    sum_squares(g, i, 4 + 2 * (g - 1) + i)
                                if i == 2:
                                    mean_square(g, 4 + 2 * g)
                        if 1 <= s <= H:
                            h = s - 1
                            wait_free(dve, f"S{h}.{u}", turn)
                            dve.reciprocal(inverse[:, h, :], sums[:, h, :]).then_inc(inverted, 1)
                            use = f"T{h}.{u}"
                            wait_full(dve, use, turn)
                            if h >= QUEUE:
                                wait_full(dve, f"O{h - QUEUE}.{u}", turn)
                            dve.tensor_copy(probsT[:, h % QUEUE], psum[uses.bank(use)][:, :].rearrange("p (s t) -> p s t", s=TT))\
                                .then_inc(free[uses.bank(use)], 1)
                            dve.wait_ge(inverted, b * H + (h + 1))
                            dve.tensor_copy(inverse_rows[:, h % QUEUE], inverse[:, h, :].unsqueeze(2).broadcast_to([P, TT, P]))\
                                .then_inc(inverse_spread, 1)
                        if s >= 2:
                            use = f"O{s - 2}.{u}"
                            wait_full(dve, use, turn)
                            wait_free(dve, f"R{s - 2}.{u}", turn)
                            dve.tensor_tensor(ctxT[:, s - 2, :], psum[uses.bank(use)][:, 0:T], spread[:, s % 2, :], ALU.mult)\
                                .then_inc(free[uses.bank(use)], 1)
                    norm_dve(core, norm, uses, turn, u)

        @block.tensor
        def _(pe):
            with pe.Fori(0, TURNS) as turn:
                for u in range(2):
                    b = turn * 2 + u

                    def done(ins, use):
                        ins.then_inc(full[uses.bank(use)], 1)

                    def rows(use, left, w, cols):
                        wait_bank(pe, use, turn)
                        for c in range(KC):
                            ins = pe.matmul(psum[uses.bank(use)][:, :], left(c), w[:, c, cols], start=c == 0, stop=c == KC - 1)
                        done(ins, use)

                    def q_group(g, t):
                        if g == 1 and t == 0:
                            pe.wait_ge(q_weights[1], 16)
                        rows(f"q{g}_{t}.{u}", lambda c: xT[:, c, t * P:(t + 1) * P], w_q, slice(g * 512, (g + 1) * 512))

                    def transpose_q(g, j):
                        use = f"qT{g}_{j}.{u}"
                        wait_bank(pe, use, turn)
                        if j == 0:
                            wait_free(pe, f"q{g}_1.{u}", turn)
                        for i in range(2):
                            for t in range(TT):
                                h = 2 * j + i
                                ins = pe.transpose(psum[uses.bank(use)][:, (i * TT + t) * P:(i * TT + t + 1) * P],
                                                   q_rows[:, g % 2, t, h * HD:(h + 1) * HD], core.ident[:, :])
                        done(ins, use)

                    pe.wait_ge(norm.loaded[u], turn * 16 + 16)
                    for j in range(2):
                        use = f"xT{j}.{u}"
                        wait_bank(pe, use, turn)
                        for c in range(2):
                            for t in range(TT):
                                d = 2 * j + c
                                ins = pe.transpose(psum[uses.bank(use)][:, (c * TT + t) * P:(c * TT + t + 1) * P],
                                                   norm.x[:, u, t, d * P:(d + 1) * P], core.ident[:, :])
                        done(ins, use)
                    for j in range(2):
                        wait_free(pe, f"xT{j}.{u}", turn)
                    pe.wait_ge(q_weights[0], 16)
                    for t in range(TT):
                        q_group(0, t)
                    pe.wait_ge(kv_weights, 64)
                    pe.wait_ge(context_loaded[u], turn * 16 + 16)
                    for key, w in (("k", w_k), ("v", w_v)):
                        for t in range(TT):
                            rows(f"{key}{t}.{u}", lambda c: context[:, u, c, t * P:(t + 1) * P], w, slice(0, G * HD))
                    for j in range(2):
                        use = f"kT{j}.{u}"
                        wait_bank(pe, use, turn)
                        for t in range(TT):
                            if j == 0:
                                wait_free(pe, f"k{t}.{u}", turn)
                        for i in range(2):
                            for t in range(TT):
                                g = 2 * j + i
                                ins = pe.transpose(psum[uses.bank(use)][:, (i * TT + t) * P:(i * TT + t + 1) * P],
                                                   k_rows[:, t, g * HD:(g + 1) * HD], core.ident[:, :])
                        done(ins, use)
                    for j in range(2):
                        transpose_q(0, j)
                    for j in range(2):
                        wait_free(pe, f"kT{j}.{u}", turn)
                        wait_free(pe, f"v{j}.{u}", turn)
                    for s in range(H + 2):
                        if s < H:
                            use, g = f"S{s}.{u}", s // HG
                            wait_bank(pe, use, turn)
                            if s % HG in (0, 2):
                                wait_free(pe, f"qT{g}_{s % HG // 2}.{u}", turn)
                            for t in range(TT):
                                ins = pe.matmul(psum[uses.bank(use)][:, t * S1:(t + 1) * S1], qT[:, g % 2, s % HG, t * P:(t + 1) * P],
                                                kT[:, g, :], start=True, stop=True)
                            done(ins, use)
                            if s < H - HG:
                                if s % HG < 2:
                                    q_group(g + 1, s % HG)
                                else:
                                    transpose_q(g + 1, s % HG - 2)
                        if 1 <= s <= H:
                            h = s - 1
                            use = f"T{h}.{u}"
                            wait_bank(pe, use, turn)
                            wait_free(pe, f"S{h}.{u}", turn)
                            for k in range(TT):
                                for t in range(TT):
                                    ins = pe.transpose(psum[uses.bank(use)][:, k * T + t * P:k * T + (t + 1) * P],
                                                       probs[:, h % QUEUE, t, k * P:(k + 1) * P], core.ident[:, :])
                            done(ins, use)
                        if s >= 2:
                            h = s - 2
                            use = f"R{h}.{u}"
                            wait_bank(pe, use, turn)
                            pe.wait_ge(inverse_spread, b * H + (h + 1))
                            for t in range(TT):
                                ins = pe.transpose(psum[uses.bank(use)][:, t * P:(t + 1) * P], inverse_rows[:, h % QUEUE, t, :], core.ident[:, :])
                            done(ins, use)
                            use = f"O{h}.{u}"
                            wait_bank(pe, use, turn)
                            wait_free(pe, f"T{h}.{u}", turn)
                            for k in range(TT):
                                ins = pe.matmul(psum[uses.bank(use)][:, 0:T], v[:, k, (h // HG) * HD:(h // HG + 1) * HD],
                                                probsT[:, h % QUEUE, k, :], start=k == 0, stop=k == TT - 1)
                            done(ins, use)
                    pe.wait_ge(o_weights, 16)
                    for t in range(TT):
                        use = f"y{t}.{u}"
                        wait_bank(pe, use, turn)
                        for h in range(H):
                            if t == 0 and h == H - 1:
                                wait_free(pe, f"O{h}.{u}", turn)
                            elif t == 0 and h == 0:
                                wait_free(pe, f"O{H - 2}.{u}", turn)
                            ins = pe.matmul(psum[uses.bank(use)][:, :], ctxT[:, h, t * P:(t + 1) * P], w_o[:, h, :],
                                            start=h == 0, stop=h == H - 1)
                        done(ins, use)



ALL_ROWS = B * T
NT = ALL_ROWS // P
NS = NT + E - 1
ROUTER = 96
AT_ONCE = 4
BUFFERS = 3
FACTS = 1 + BUFFERS
COPIES = 48


def mixture_constants():
    import numpy as np
    buffer = [0] + [1 if e % BUFFERS else 1 - BUFFERS for e in range(1, E)]
    loads = [[COPIES * (e % BUFFERS == k) + (e == 0) for e in range(E)] for k in range(BUFFERS)]
    row = np.concatenate([P * np.arange(NT), np.arange(NS), buffer, *loads]).astype(np.float32)
    return np.tile(row[None, :], (P, 1))


def mixture(core, name, x_src, x_dst, slot_x, slot_y, weights):
    nc, psum = core.nc, core.psum
    XT, GATE, UP, DOWN = 0, 2, 4, 6
    LAST = NT + NS - 1

    with ExitStack() as ctx:
        def sb(tag, shape, dtype=F32):
            return ctx.enter_context(nc.sbuf_tensor(f"{name}_{tag}", shape, dtype))

        def sem(tag):
            return core.semaphore(f"{name}_{tag}")

        rows = sb("rows", [P, NT + NS, D])
        w = sb("w", [P, BUFFERS, 3, KC, D])
        SHARED = BUFFERS - 1
        router = sb("router", [P, KC, ROUTER])
        table = sb("table", [P, NT + NS + FACTS * E])
        x_in = sb("x_in", [P, AT_ONCE, D])
        xT = sb("xT", [P, AT_ONCE, KC, P])
        silu = sb("silu", [P, 2, D])
        h = sb("h", [P, 2, D])
        hT = sb("hT", [P, 2, KC, P])
        scaled_x = sb("scaled_x", [P, 2, D])
        before = sb("before", [P, P], BF16)
        ones = sb("ones", [P, P], BF16)
        order = sb("order", [P, E])
        logits = sb("logits", [P, NT, E])
        top = sb("top", [P, NT])
        score = sb("score", [P, NT])
        rank = sb("rank", [P, NT, E])
        chosen = sb("chosen", [P, NT, E])
        chosen_bf = sb("chosen_bf", [P, NT, E], BF16)
        HALF = NT // 2
        running = [sb(f"running{k}", [P, HALF + NT, E]) for k in range(2)]
        starts = [sb(f"starts{k}", [P, E // 2 + E]) for k in range(2)]
        above = sb("above", [P, E, NT])
        position = sb("position", [P, NT])
        index = sb("index", [P, NT], mybir.dt.uint32)
        reached = sb("reached", [P, NS, E])
        parts = sb("parts", [P, FACTS, NS, E])
        facts = sb("facts", [P, FACTS, NS])
        slot_facts = sb("slot_facts", [P, FACTS, NS], mybir.dt.int32)
        expert_end = sb("expert_end", [P, E], mybir.dt.int32)
        stats = sb("stats", [P, NT, 6])
        moments = sb("moments", [P, NT, 2])
        vareps = sb("vareps", [P, NT])
        rstd = sb("rstd", [P, NT])

        x_loaded = [sem(f"x_loaded{k}") for k in range(2)]
        router_loaded = sem("router_and_table_loaded")
        shared_loaded = sem("shared_loaded")
        expert_loaded = [sem(f"expert_loaded{k}") for k in range(BUFFERS)]
        filled = sem("filled")
        zeros_stored = sem("zeros_stored")
        first_in = sem("first_in")
        first_full = sem("first_full")
        first_ready = sem("first_ready")
        logits_full = sem("logits_full")
        logits_ready = sem("logits_ready")
        counts_full = sem("counts_full")
        routed = sem("routed")
        score_ready = sem("score_ready")
        scaled = sem("scaled")
        scattered = [sem(f"scattered{k}") for k in range(2)]
        slots_loaded = sem("slots_loaded")
        in_ready = sem("in_ready")
        xT_full = sem("xT_full")
        xT_ready = sem("xT_ready")
        gate_full = sem("gate_full")
        silu_ready = sem("silu_ready")
        up_full = sem("up_full")
        h_ready = sem("h_ready")
        hT_full = sem("hT_full")
        hT_ready = sem("hT_ready")
        y_full = sem("y_full")
        y_ready = sem("y_ready")
        y_stored = sem("y_stored")
        gathered = [sem(f"gathered{k}") for k in range(4)]
        z_ready = sem("z_ready")
        z_stats = sem("z_stats")
        moved = sem("moved")
        rstd_ready = sem("rstd_ready")
        out_ready = sem("out_ready")
        stored = sem("stored")
        src = x_src.rearrange("b (j p) d -> p (b j) d", p=P)
        dst = x_dst.rearrange("b (j p) d -> p (b j) d", p=P)
        GROUP = 4
        CUTS = [0, 8, 16, 20, NS]
        ROUTED = 25

        block = ctx.enter_context(nc.Block())

        @block.sync
        def _(sp):
            for counted in (first_full, logits_full, logits_ready, y_ready, *expert_loaded):
                sp.sem_inc(counted, 1)
            for k in range(2):
                sp.dma_start(rows[:, k * HALF:(k + 1) * HALF, :], src[:, k * HALF:(k + 1) * HALF, :]).then_inc(x_loaded[k], 16)
            for m, key in enumerate(("sg", "su", "sd")):
                sp.dma_start(w[:, SHARED, m], weights[key].rearrange("(c p) n -> p c n", p=P)).then_inc(shared_loaded, 16)
            sp.wait_ge(filled, 2)
            sp.dma_start(slot_x.rearrange("(g p) d -> p g d", p=P), rows[:, NT:NT + NS, :]).then_inc(zeros_stored, 16)
            done = []
            for e in range(E):
                if e == SHARED:
                    sp.wait_ge(y_full, NT)
                    sp.wait_ge(routed, ROUTED)
                if e == BUFFERS:
                    done = [sp.value_load(expert_end[0:1, k:k + 1], min_val=NT, max_val=NT + NS) for k in range(E - BUFFERS)]
                if e >= BUFFERS:
                    sp.wait_ge(y_full, done[e - BUFFERS])
                for m, key in enumerate(("g", "u", "d")):
                    sp.dma_start(w[:, e % BUFFERS, m], weights[key][e].rearrange("(c p) n -> p c n", p=P))\
                        .then_inc(expert_loaded[e % BUFFERS], 16)
            for k in range(NT // GROUP):
                sp.wait_ge(out_ready, (k + 1) * GROUP)
                sp.dma_start(dst[:, k * GROUP:(k + 1) * GROUP, :], rows[:, k * GROUP:(k + 1) * GROUP, :]).then_inc(stored, 16)
            sp.wait_ge(stored, 16 * (NT // GROUP))

        @block.gpsimd
        def _(pool):
            pool.memset(rows[:, NT:NT + HALF, :], 0.0).then_inc(filled, 1)
            pool.memset(rows[:, NT + HALF:NT + NS, :], 0.0).then_inc(filled, 1)
            pool.memset(before[:, :], 0.0).then_inc(filled, 1)
            pool.memset(ones[:, :], 1.0).then_inc(filled, 1)
            for k in range(2):
                pool.memset(running[k][:, :, :], 0.0).then_inc(filled, 1)
                pool.memset(starts[k][:, :], 0.0).then_inc(filled, 1)
            pool.iota(order[:, :], pattern=[[-1, E]], base=E, channel_multiplier=0,
                      allow_small_or_imprecise_dtypes=True).then_inc(filled, 1)
            pool.wait_ge(filled, 3)
            pool.affine_select(out=before[:, :], in_=before[:, :], compare_op=ALU.is_ge, fill=1.0, base=0,
                               pattern=[[-1, P]], channel_multiplier=1).then_inc(filled, 1)
            pool.wait_ge(score_ready, 1)
            pool.wait_ge(x_loaded[0], 16)
            pool.wait_ge(x_loaded[1], 16)
            for t in range(NT):
                if t >= 2:
                    pool.wait_ge(scattered[t % 2], 16 * (t // 2))
                pool.tensor_tensor(scaled_x[:, t % 2, :], rows[:, t, :], score[:, t:t + 1].broadcast_to([P, D]), ALU.mult)\
                    .then_inc(scaled, 1)
                if t == 0:
                    pool.wait_ge(routed, ROUTED)
                    pool.wait_ge(zeros_stored, 16)
                pool.wait_ge(scaled, t + 1)
                pool.indirect_dma_start(out=slot_x, out_offset=bass.IndirectOffsetOnAxis(ap=index[:, t:t + 1], axis=0),
                                        in_=scaled_x[:, t % 2, :], in_offset=None).then_inc(scattered[t % 2], 16)
            for k in range(2):
                pool.wait_ge(scattered[k], 16 * HALF)
            pool.dma_start(rows[:, NT:NT + NS, :], slot_x.rearrange("(g p) d -> p g d", p=P)).then_inc(slots_loaded, 16)
            for k in range(len(CUTS) - 1):
                pool.wait_ge(y_ready, 1 + NT + CUTS[k + 1])
                pool.dma_start(slot_y.rearrange("(g p) d -> p g d", p=P)[:, CUTS[k]:CUTS[k + 1], :],
                               rows[:, NT + CUTS[k]:NT + CUTS[k + 1], :]).then_inc(y_stored, 16)
            pool.wait_ge(y_stored, 16 * (len(CUTS) - 1))
            for t in range(NT):
                pool.indirect_dma_start(out=rows[:, NT + t, :], out_offset=None, in_=slot_y,
                                        in_offset=bass.IndirectOffsetOnAxis(ap=index[:, t:t + 1], axis=0))\
                    .then_inc(gathered[t // GROUP], 16)
            for k in range(NT // GROUP):
                cols = slice(k * GROUP, (k + 1) * GROUP)
                pool.wait_ge(moved, (k + 1) * (GROUP + 1))
                pool.tensor_tensor(rstd[:, cols], vareps[:, cols], core.minus_half[:, 0:GROUP], ALU.pow).then_inc(rstd_ready, 1)

        @block.scalar
        def _(act):
            act.dma_start(router[:, :, :], weights["r"].rearrange("(c p) n -> p c n", p=P)).then_inc(router_loaded, 16)
            act.dma_start(table[:, :], weights["table"]).then_inc(router_loaded, 16)
            with act.Fori(0, NT // AT_ONCE) as some:
                for u in range(AT_ONCE):
                    act.wait_ge(first_full, some * AT_ONCE + (u + 2))
                    act.wait_ge(logits_full, some * AT_ONCE + 1)
                    act.copy(xT[:, u], psum[XT + u].rearrange("p (c t) -> p c t", c=KC)).then_inc(first_ready, 1)
            act.wait_ge(routed, 1)
            act.activation(score[:, :], top[:, :], ACT.Sigmoid).then_inc(score_ready, 1)

            def take_xT(t, u, first=False):
                act.wait_ge(xT_full, t + 1)
                if not first:
                    act.wait_ge(up_full, t - 1)
                act.copy(xT[:, u], psum[XT + u].rearrange("p (c t) -> p c t", c=KC)).then_inc(xT_ready, 1)

            def step(t, u, first=False, last=False):
                if not last:
                    take_xT(t + 1, 1 - u, first and u == 0)
                act.wait_ge(gate_full, t + 1)
                if not first:
                    act.wait_ge(h_ready, t - 1)
                act.activation(silu[:, u, :], psum[GATE + u], ACT.Silu).then_inc(silu_ready, 1)
                act.wait_ge(hT_full, t + 1)
                if not first:
                    act.wait_ge(y_full, t - 1)
                act.copy(hT[:, u], psum[XT + u].rearrange("p (c t) -> p c t", c=KC)).then_inc(hT_ready, 1)

            act.wait_ge(logits_full, NT + 1)
            take_xT(0, 0, True)
            step(0, 0, True)
            step(1, 1, True)
            with act.Fori(0, (LAST - 2) // 2) as turn:
                step(turn * 2 + 2, 0)
                step(turn * 2 + 3, 1)
            step(LAST, 0, last=True)

        @block.vector
        def _(dve):
            for k in range(2):
                dve.wait_ge(x_loaded[k], 16)
                with dve.Fori(0, HALF // AT_ONCE) as some:
                    for u in range(AT_ONCE):
                        dve.wait_ge(first_full, some * AT_ONCE + (k * HALF + 1))
                        dve.tensor_copy(x_in[:, u, :], rows[:, bass.ds(some * AT_ONCE + (k * HALF + u), 1), :]
                                        .rearrange("p a d -> p (a d)")).then_inc(first_in, 1)
                    for u in range(AT_ONCE):
                        dve.wait_ge(logits_full, some * AT_ONCE + (k * HALF + u + 2))
                        dve.tensor_copy(logits[:, bass.ds(some * AT_ONCE + (k * HALF + u), 1), :].rearrange("p a e -> p (a e)"),
                                        psum[AT_ONCE + u][:, 0:E]).then_inc(logits_ready, 1)

            steps = [0]

            def step(ins):
                ins.then_inc(routed, 1)
                steps[0] += 1
                dve.wait_ge(routed, steps[0])

            def per_tile(a):
                return a.unsqueeze(2).broadcast_to([P, NT, E])

            multiples = table[:, 0:NT]
            numbers = table[:, NT:NT + NS]
            shares = table[:, NT + NS:NT + NS + FACTS * E].rearrange("p (k e) -> p k e", k=FACTS)
            dve.wait_ge(filled, 10)
            dve.wait_ge(router_loaded, 32)
            dve.wait_ge(logits_ready, NT + 1)
            step(dve.tensor_reduce(top[:, :], logits[:, :, :], AX.X, ALU.max))
            step(dve.tensor_tensor(rank[:, :, :], logits[:, :, :], per_tile(top[:, :]), ALU.is_equal))
            step(dve.tensor_tensor(rank[:, :, :], rank[:, :, :], order[:, :].unsqueeze(1).broadcast_to([P, NT, E]), ALU.mult))
            step(dve.tensor_reduce(position[:, :], rank[:, :, :], AX.X, ALU.max))
            step(dve.tensor_tensor(chosen[:, :, :], rank[:, :, :], per_tile(position[:, :]), ALU.is_equal))
            step(dve.tensor_copy(chosen_bf[:, :, :], chosen[:, :, :]))
            dve.wait_ge(counts_full, 2)
            step(dve.tensor_copy(running[0][:, HALF:, :], psum[UP][:, 0:P].rearrange("p (t e) -> p t e", t=NT)))
            for k in range(4):
                a, b = running[k % 2], running[1 - k % 2]
                step(dve.tensor_tensor(b[:, HALF:, :], a[:, HALF:, :], a[:, HALF - 2 ** k:HALF + NT - 2 ** k, :], ALU.add))
            step(dve.tensor_tensor(above[:, :, :], running[0][:, HALF + NT - 1, :].unsqueeze(2).broadcast_to([P, E, NT]),
                                   multiples.unsqueeze(1).broadcast_to([P, E, NT]), ALU.is_gt))
            PAD = E // 2
            step(dve.tensor_reduce(starts[0][:, PAD:], above[:, :, :], AX.X, ALU.add))
            for k in range(3):
                a, b = starts[k % 2], starts[1 - k % 2]
                step(dve.tensor_tensor(b[:, PAD:], a[:, PAD:], a[:, PAD - 2 ** k:PAD + E - 2 ** k], ALU.add))
            first_slot = starts[1][:, PAD - 1:PAD + E - 1]
            step(dve.scalar_tensor_tensor(out=rank[:, :, :], in0=first_slot.unsqueeze(1).broadcast_to([P, NT, E]),
                                          scalar=float(P), in1=running[0][:, HALF - 1:HALF + NT - 1, :], op0=ALU.mult, op1=ALU.add))
            step(dve.tensor_tensor(rank[:, :, :], psum[DOWN][:, 0:P].rearrange("p (t e) -> p t e", t=NT), rank[:, :, :], ALU.add))
            step(dve.tensor_tensor(rank[:, :, :], rank[:, :, :], chosen[:, :, :], ALU.mult))
            step(dve.tensor_reduce(position[:, :], rank[:, :, :], AX.X, ALU.add))
            step(dve.tensor_copy(index[:, :], position[:, :]))
            step(dve.tensor_tensor(reached[:, :, :], first_slot.unsqueeze(1).broadcast_to([P, NS, E]),
                                   numbers.unsqueeze(2).broadcast_to([P, NS, E]), ALU.is_le))
            for k in range(FACTS):
                ins = dve.tensor_tensor(parts[:, k], reached[:, :, :], shares[:, k, :].unsqueeze(1).broadcast_to([P, NS, E]), ALU.mult)
            step(ins)
            step(dve.tensor_reduce(facts[:, :, :], parts[:, :, :, :], AX.X, ALU.add))
            dve.tensor_copy(slot_facts[:, :, :], facts[:, :, :])
            step(dve.tensor_scalar(expert_end[:, :], starts[1][:, PAD:], float(NT), None, ALU.add))
            assert steps[0] == ROUTED, steps[0]

            def take_x(t, u):
                dve.tensor_copy(x_in[:, u, :], rows[:, bass.ds(t, 1), :].rearrange("p a d -> p (a d)")
                                if not isinstance(t, int) else rows[:, t, :]).then_inc(in_ready, 1)

            def give_y(t, u, slot):
                y = rows[:, t, :] if isinstance(t, int) else rows[:, bass.ds(t, 1), :].rearrange("p a d -> p (a d)")
                dve.wait_ge(y_full, t + 1)
                if slot:
                    dve.tensor_copy(y, psum[DOWN + u]).then_inc(y_ready, 1)
                else:
                    dve.wait_ge(scaled, t + 1)
                    dve.tensor_tensor(y, psum[DOWN + u], y, ALU.add).then_inc(y_ready, 1)

            def work(t, u, first=False, last=False, slot=False):
                dve.wait_ge(silu_ready, t + 1)
                dve.wait_ge(up_full, t + 1)
                if not first:
                    dve.wait_ge(hT_full, t - 1)
                dve.tensor_tensor(h[:, u, :], psum[UP + u], silu[:, u, :], ALU.mult).then_inc(h_ready, 1)
                if not (first and u == 0):
                    give_y(t - 1, 1 - u, slot)
                if not last:
                    dve.wait_ge(xT_full, t + 1)
                    take_x(t + 2, u)

            take_x(0, 0)
            take_x(1, 1)
            work(0, 0, first=True)
            work(1, 1, first=True)
            with dve.Fori(0, (NT - 4) // 2) as turn:
                work(turn * 2 + 2, 0)
                work(turn * 2 + 3, 1)
            dve.wait_ge(slots_loaded, 16)
            work(NT - 2, 0)
            work(NT - 1, 1)
            work(NT, 0)
            with dve.Fori(0, (NS - 3) // 2) as turn:
                work(turn * 2 + (NT + 1), 1, slot=True)
                work(turn * 2 + (NT + 2), 0, slot=True)
            work(LAST - 1, 1, last=True, slot=True)
            work(LAST, 0, last=True, slot=True)
            give_y(LAST, 0, True)

            def normalise(k):
                for t in range(k * GROUP, (k + 1) * GROUP):
                    if t == k * GROUP:
                        dve.wait_ge(rstd_ready, k + 1)
                    dve.tensor_scalar(rows[:, t, :], rows[:, t, :], moments[:, t, 0:1], rstd[:, t:t + 1],
                                      ALU.subtract, ALU.mult).then_inc(out_ready, 1)

            for k in range(NT // GROUP):
                for t in range(k * GROUP, (k + 1) * GROUP):
                    dve.wait_ge(gathered[k], 16 * GROUP)
                    if t == 0:
                        dve.wait_ge(y_ready, NT + 1)
                    dve.tensor_tensor(rows[:, t, :], rows[:, t, :], rows[:, NT + t, :], ALU.add).then_inc(z_ready, 1)
                    dve.wait_ge(z_ready, t + 1)
                    dve.bn_stats(stats[:, t, :], rows[:, t, :]).then_inc(z_stats, 1)
                for t in range(k * GROUP, (k + 1) * GROUP):
                    dve.wait_ge(z_stats, t + 1)
                    dve.bn_aggr(moments[:, t, :], stats[:, t, :]).then_inc(moved, 1)
                cols = slice(k * GROUP, (k + 1) * GROUP)
                dve.wait_ge(moved, k * (GROUP + 1) + GROUP)
                dve.tensor_scalar(vareps[:, cols], moments[:, cols, 1], EPS, None, ALU.add).then_inc(moved, 1)
                if k >= 1:
                    normalise(k - 1)
            normalise(NT // GROUP - 1)

        @block.tensor
        def _(pe):
            for k in range(2):
                with pe.Fori(0, HALF // AT_ONCE) as some:
                    for u in range(AT_ONCE):
                        pe.wait_ge(first_in, some * AT_ONCE + (k * HALF + u + 1))
                        for c in range(KC):
                            ins = pe.transpose(psum[XT + u][:, c * P:(c + 1) * P], x_in[:, u, c * P:(c + 1) * P], core.ident[:, :])
                        ins.then_inc(first_full, 1)
                    for u in range(AT_ONCE):
                        if k == 0 and u == 0:
                            pe.wait_ge(router_loaded, 32)
                        pe.wait_ge(first_ready, some * AT_ONCE + (k * HALF + u + 1))
                        pe.wait_ge(logits_ready, some * AT_ONCE + (k * HALF + 1))
                        for c in range(KC):
                            ins = pe.matmul(psum[AT_ONCE + u][:, 0:ROUTER], xT[:, u, c, :], router[:, c, :], start=c == 0, stop=c == KC - 1)
                        ins.then_inc(logits_full, 1)
            pe.wait_ge(routed, 6)
            pe.wait_ge(filled, 10)
            chosen_flat = chosen_bf[:, :, :].rearrange("p t e -> p (t e)")
            pe.matmul(psum[UP][:, 0:P], ones[:, :], chosen_flat, start=True, stop=True).then_inc(counts_full, 1)
            pe.matmul(psum[DOWN][:, 0:P], before[:, :], chosen_flat, start=True, stop=True).then_inc(counts_full, 1)

            def transpose_x(t, u, first=False):
                pe.wait_ge(in_ready, t + 1)
                if not first:
                    pe.wait_ge(hT_ready, t - 1)
                for c in range(KC):
                    ins = pe.transpose(psum[XT + u][:, c * P:(c + 1) * P], x_in[:, u, c * P:(c + 1) * P], core.ident[:, :])
                ins.then_inc(xT_full, 1)

            def weight(slot, m, c):
                if slot is None:
                    return w[:, SHARED, m, c, :]
                return w[:, bass.ds(slot, 1), m, c, :].rearrange("p a n -> p (a n)")

            def buffer_of(g):
                return pe.value_load(slot_facts[0:1, 0, g:g + 1] if isinstance(g, int) else slot_facts[0:1, 0, bass.ds(g, 1)],
                                     min_val=0, max_val=BUFFERS - 1)

            def down(t, u, buffer, first=False):
                pe.wait_ge(hT_ready, t + 1)
                if not first:
                    pe.wait_ge(y_ready, t)
                for c in range(KC):
                    ins = pe.matmul(psum[DOWN + u], hT[:, u, c, :], weight(buffer, 2, c), start=c == 0, stop=c == KC - 1)
                ins.then_inc(y_full, 1)

            def step(t, u, buffer=None, previous=None, needs=None, first=False, last=False):
                if not last:
                    transpose_x(t + 1, 1 - u, first and u == 0)
                pe.wait_ge(xT_ready, t + 1)
                if not first:
                    pe.wait_ge(silu_ready, t - 1)
                if needs:
                    for k in range(BUFFERS):
                        pe.wait_ge(expert_loaded[k], needs[k])
                for c in range(KC):
                    ins = pe.matmul(psum[GATE + u], xT[:, u, c, :], weight(buffer, 0, c), start=c == 0, stop=c == KC - 1)
                ins.then_inc(gate_full, 1)
                if not first:
                    pe.wait_ge(h_ready, t - 1)
                for c in range(KC):
                    ins = pe.matmul(psum[UP + u], xT[:, u, c, :], weight(buffer, 1, c), start=c == 0, stop=c == KC - 1)
                ins.then_inc(up_full, 1)
                if not (first and u == 0):
                    down(t - 1, 1 - u, previous, first=first)
                pe.wait_ge(h_ready, t + 1)
                for c in range(KC):
                    ins = pe.transpose(psum[XT + u][:, c * P:(c + 1) * P], h[:, u, c * P:(c + 1) * P], core.ident[:, :])
                ins.then_inc(hT_full, 1)

            def slot_step(t, u, g, last=False, shared_before=False):
                def fact(k, at):
                    ap = slot_facts[0:1, k, at:at + 1] if isinstance(at, int) else slot_facts[0:1, k, bass.ds(at, 1)]
                    return pe.value_load(ap, min_val=min(k, 1), max_val=COPIES * E if k else BUFFERS - 1)
                needs = [fact(1 + k, g) for k in range(BUFFERS)]
                step(t, u, fact(0, g), None if shared_before else fact(0, g - 1), needs, last=last)

            transpose_x(0, 0, True)
            pe.wait_ge(shared_loaded, 48)
            step(0, 0, first=True)
            step(1, 1, first=True)
            with pe.Fori(0, (NT - 2) // 2) as turn:
                step(turn * 2 + 2, 0)
                step(turn * 2 + 3, 1)
            pe.wait_ge(routed, ROUTED)
            slot_step(NT, 0, 0, shared_before=True)
            with pe.Fori(0, (NS - 3) // 2) as turn:
                slot_step(turn * 2 + (NT + 1), 1, turn * 2 + 1)
                slot_step(turn * 2 + (NT + 2), 0, turn * 2 + 2)
            slot_step(LAST - 1, 1, NS - 2)
            slot_step(LAST, 0, NS - 1, last=True)
            down(LAST, 0, buffer_of(NS - 1))



def decoder_layers(nc, a, x, result):
    between = [nc.dram_tensor(f"x_after_{k}", (B, T, D), F32).ap() for k in range(1, 6)]
    slot_x = nc.dram_tensor("slot_x", (NS * P, D), F32).ap()
    slot_y = nc.dram_tensor("slot_y", (NS * P, D), F32).ap()

    def group(prefix, *keys):
        return {key: a[f"{prefix}_{key}"] for key in keys}

    with ExitStack() as ctx:
        core = Core(nc, ctx)
        constants(core)
        self_attention(core, "a0", x, between[0], group("a0", "q", "k", "v", "o"), False)
        core.release_semaphores()
        cross_attention_masked(core, "x0", between[0], a["ctx"], between[1], a["mask"], a["mask_cols"],
                               a["x0_onehot"], group("x0", "q", "k", "v", "bq", "bk", "bv"))
        feed_forward_lora(core, "f0", between[1], between[2],
                          group("f0", "first", "gate", "up", "down", "B_gate", "B_up", "A_down", "B_down", "bias"))
        self_attention(core, "a1", between[2], between[3],
                       group("a1", "dq", "dkv", "uq", "ukv", "q_g", "q_b", "kv_g", "kv_b", "o"), True)
        cross_attention_grouped(core, "x1", between[3], a["ctxT"], between[4], group("x1", "q", "k", "v", "o", "qn", "kn"))
        mixture(core, "m1", between[4], result, slot_x, slot_y, group("m1", "r", "g", "u", "d", "sg", "su", "sd", "table"))


def layout(inputs):
    import numpy as np
    i = {name: np.asarray(value) for name, value in inputs.items()}
    mask = i["mask_Bx1x2048_fk1"].reshape(B, D)
    padded_router = np.zeros((D, ROUTER), i["L1_ffn_router_w"].dtype)
    padded_router[:, 0:E] = i["L1_ffn_router_w"]
    laid = {
        "x": i["x"], "ctx": i["ctx_2048"], "ctxT": i["ctx_2048"].transpose(0, 2, 1),
        "mask": mask, "mask_cols": mask.reshape(B, KC, P).transpose(2, 0, 1), "x0_onehot": xattn_constants(),
        "x0_q": i["L0_xattn_Wq"].T, "x0_k": i["L0_xattn_Wk"].T, "x0_v": i["L0_xattn_Wv"].T,
        "x0_bq": i["L0_xattn_bq"].reshape(-1, P).T, "x0_bk": i["L0_xattn_bk"].reshape(-1, P).T,
        "x0_bv": i["L0_xattn_bv"],
        "a1_o": i["L1_attn_W_o"].T,
        "m1_r": padded_router, "m1_table": mixture_constants(),
    }
    natural = {
        "a0": ("L0_attn_", dict(q="q_out", k="k_out", v="v_out", o="w_out")),
        "a1": ("L1_attn_", dict(dq="W_dq", dkv="W_dkv", uq="W_uq", ukv="W_ukv", q_g="q_ln_g", q_b="q_ln_b",
                                kv_g="kv_ln_g", kv_b="kv_ln_b")),
        "x1": ("L1_xattn_", dict(q="Wq", k="Wk", v="Wv", o="Wo", qn="q_norm_w", kn="k_norm_w")),
        "m1": ("L1_ffn_", dict(g="gate_w", u="up_w", d="down_w", sg="shared_gate_w", su="shared_up_w",
                               sd="shared_down_w")),
    }
    for short, (prefix, names) in natural.items():
        for key, name in names.items():
            laid[f"{short}_{key}"] = i[prefix + name]
    for key, value in ffn0_layout(i).items():
        laid[f"f0_{key}"] = value
    return {name: np.ascontiguousarray(value) for name, value in laid.items()}


def kernel(**inputs):
    import concourse.bacc as bacc
    from concourse.bass_utils import run_bass_kernel_spmd

    nc = bacc.Bacc("TRN2", target_bir_lowering=False, num_devices=1)
    arrays = layout(inputs)
    aps = {name: nc.dram_tensor(f"in_{name}", value.shape, mybir.dt.from_np(value.dtype), kind="ExternalInput").ap()
           for name, value in arrays.items()}
    result = nc.dram_tensor("result", (B, T, D), F32, kind="ExternalOutput").ap()
    decoder_layers(nc, aps, aps["x"], result)
    ran = run_bass_kernel_spmd(nc, [{f"in_{name}": value for name, value in arrays.items()}], core_ids=[0])
    return ran.results[0]["result"]
```
